# Optimizing a Trainium2 kernel written in Bass

```python
import numpy as np
import jax
import jax.numpy as jnp

def _softmax(x, axis=-1):
    return jax.nn.softmax(x, axis=axis)

def _gelu(x):
    return jax.nn.gelu(x, approximate=True)

def _silu(x):
    return jax.nn.silu(x)

def _sigmoid(x):
    return jax.nn.sigmoid(x)

def _layernorm(x, axis=-1, eps=1e-05):
    m = jnp.mean(x, axis=axis, keepdims=True)
    v = jnp.var(x, axis=axis, keepdims=True)
    return (x - m) / jnp.sqrt(v + eps)

def _scatter_add(tgt, idx, src, axis=0):
    return tgt.at[idx].add(src)

def _segment_sum(src, seg, n):
    return jax.ops.segment_sum(src, seg, n)
kernel_name = 'mk_gnn_preln_d4_gnn_r8_87c4cf'

def setup_inputs(seed: int=0):
    np.random.seed(seed)
    _w = jnp.asarray

    def _rec_inputs():
        import jax
        import jax.numpy as jnp
        _gk = jax.random.key(seed)
        x = -0.000202 + 1 * jax.random.normal(jax.random.fold_in(_gk, 1), (6250, 128), jnp.float32)
        _s = jax.random.randint(jax.random.fold_in(_gk, 2), (100000,), 0, 6250, jnp.int32)
        _d = jax.random.randint(jax.random.fold_in(_gk, 3), (100000,), 0, 6250, jnp.int32)
        _loop = jnp.arange(6250, dtype=jnp.int32)
        src = jnp.concatenate([_s, _d, _loop])
        dst = jnp.concatenate([_d, _s, _loop])
        _o = jnp.argsort(dst, stable=True)
        src = src[_o]
        dst = dst[_o]
        edge_attr_128 = -6.74381e-05 + 0.999835 * jax.random.normal(jax.random.fold_in(_gk, 13), (206250, 128), jnp.float32)
        edge_attr_2 = -0.000414295 + 0.999828 * jax.random.normal(jax.random.fold_in(_gk, 14), (206250, 2), jnp.float32)
        edge_weight = jax.random.uniform(jax.random.fold_in(_gk, 16), (206250,), jnp.float32, 0.0, 1)
        return (x, src, dst, edge_attr_128, edge_attr_2, edge_weight)
    x, src, dst, edge_attr_128, edge_attr_2, edge_weight = _rec_inputs()

    def _L0_gnn_setup():
        import jax, jax.numpy as jnp
        import numpy as np
        N_NODES = 6250
        key = jax.random.key(seed)
        k1, k2, k3, k4 = jax.random.split(key, 4)
        features = jax.random.normal(k1, (N_NODES, 128), dtype=jnp.float32)
        edge_weight = jax.random.uniform(k2, (100000,), dtype=jnp.float32)
        edge_src = jax.random.randint(k3, (100000,), 0, N_NODES, dtype=jnp.int64)
        edge_dst = jax.random.randint(k4, (100000,), 0, N_NODES, dtype=jnp.int64)
        return {'features': features, 'edge_weight': edge_weight, 'edge_src': edge_src, 'edge_dst': edge_dst}
    _L0_gnn_all = _L0_gnn_setup()
    _L0_gnn_in = {k: v for k, v in _L0_gnn_all.items() if k in ()}
    del _L0_gnn_all

    def _L1_gnn_setup():
        import jax, jax.numpy as jnp
        import numpy as np
        N_NODES = 6250
        N_EDGES = 100000
        IN_DIM = 128
        OUT_DIM = 128
        EDGE_DIM = 2
        LN_EPS = 1e-05
        key = jax.random.key(seed)
        ks = jax.random.split(key, 8)
        s = lambda fan_in: 1.0 / np.sqrt(fan_in)
        x = jax.random.normal(ks[0], (N_NODES, IN_DIM), dtype=jnp.float32)
        edge_attr = jax.random.normal(ks[1], (N_EDGES, EDGE_DIM), dtype=jnp.float32)
        mW1 = jax.random.normal(ks[2], (2 * IN_DIM + EDGE_DIM, OUT_DIM), dtype=jnp.float32) * s(2 * IN_DIM + EDGE_DIM)
        mb1 = jnp.zeros((OUT_DIM,), jnp.float32)
        mW2 = jax.random.normal(ks[3], (OUT_DIM, OUT_DIM), dtype=jnp.float32) * s(OUT_DIM)
        mb2 = jnp.zeros((OUT_DIM,), jnp.float32)
        uW1 = jax.random.normal(ks[4], (IN_DIM + OUT_DIM, OUT_DIM), dtype=jnp.float32) * s(IN_DIM + OUT_DIM)
        ub1 = jnp.zeros((OUT_DIM,), jnp.float32)
        uW2 = jax.random.normal(ks[5], (OUT_DIM, OUT_DIM), dtype=jnp.float32) * s(OUT_DIM)
        ub2 = jnp.zeros((OUT_DIM,), jnp.float32)
        gamma = jnp.ones((OUT_DIM,), jnp.float32)
        beta = jnp.zeros((OUT_DIM,), jnp.float32)
        edge_index = jax.random.randint(ks[6], (2, N_EDGES), 0, N_NODES, dtype=jnp.int64 if jax.config.jax_enable_x64 else jnp.int32)
        return {'x': x, 'edge_attr': edge_attr, 'mW1': mW1, 'mb1': mb1, 'mW2': mW2, 'mb2': mb2, 'uW1': uW1, 'ub1': ub1, 'uW2': uW2, 'ub2': ub2, 'gamma': gamma, 'beta': beta, 'edge_index': edge_index}
    _L1_gnn_all = _L1_gnn_setup()
    _L1_gnn_in = {k: v for k, v in _L1_gnn_all.items() if k in ('mW1', 'mb1', 'mW2', 'mb2', 'uW1', 'ub1', 'uW2', 'ub2', 'gamma', 'beta')}
    del _L1_gnn_all

    def _L2_gnn_setup():
        import jax, jax.numpy as jnp
        import numpy as np
        N_NODES = 6250
        N_EDGES = 100000
        HIDDEN = 128
        key = jax.random.key(seed)
        k1, k2, k3, k4, k5, k6 = jax.random.split(key, 6)
        stdv = 1.0 / np.sqrt(HIDDEN)
        h = jax.random.normal(k1, (N_NODES, HIDDEN), dtype=jnp.float32)
        edge_src = jax.random.randint(k2, (N_EDGES,), 0, N_NODES, dtype=jnp.int32)
        edge_dst = jax.random.randint(k3, (N_EDGES,), 0, N_NODES, dtype=jnp.int32)
        edge_val = jax.random.uniform(k4, (N_EDGES,), dtype=jnp.float32)
        weight = jax.random.uniform(k5, (HIDDEN, HIDDEN), dtype=jnp.float32, minval=-stdv, maxval=stdv)
        bias = jax.random.uniform(k6, (HIDDEN,), dtype=jnp.float32, minval=-stdv, maxval=stdv)
        return {'h': h, 'edge_src': edge_src, 'edge_dst': edge_dst, 'edge_val': edge_val, 'weight': weight, 'bias': bias}
    _L2_gnn_all = _L2_gnn_setup()
    _L2_gnn_in = {k: v for k, v in _L2_gnn_all.items() if k in ('weight', 'bias')}
    del _L2_gnn_all

    def _L3_gnn_setup():
        import jax, jax.numpy as jnp
        import numpy as np
        N = 12500
        E = 78125
        D = 128
        L = 3
        NUM_GRAPHS = 512
        LN_EPS = 1e-05

        def _layernorm(x, g, b):
            mu = jnp.mean(x, axis=-1, keepdims=True)
            var = jnp.mean(jnp.square(x - mu), axis=-1, keepdims=True)
            return (x - mu) * jax.lax.rsqrt(var + LN_EPS) * g + b
        key = jax.random.key(seed)
        ks = jax.random.split(key, 14)
        h = jax.random.normal(ks[0], (N, D), dtype=jnp.float32)
        h_edge_attr = jax.random.normal(ks[1], (E, D), dtype=jnp.float32)
        batch = jnp.sort(jax.random.randint(ks[2], (N,), 0, NUM_GRAPHS))
        edge_index = jax.random.randint(ks[3], (2, E), 0, N)
        s = 0.02
        W1 = jax.random.normal(ks[4], (L, D, D), dtype=jnp.float32) * s
        b1 = jnp.zeros((L, D), dtype=jnp.float32)
        g1 = jnp.ones((L, D), dtype=jnp.float32)
        be1 = jnp.zeros((L, D), dtype=jnp.float32)
        W2 = jax.random.normal(ks[5], (L, D, D), dtype=jnp.float32) * s
        b2 = jnp.zeros((L, D), dtype=jnp.float32)
        g2 = jnp.ones((L, D), dtype=jnp.float32)
        be2 = jnp.zeros((L, D), dtype=jnp.float32)
        return {'h': h, 'h_edge_attr': h_edge_attr, 'batch': batch, 'edge_index': edge_index, 'W1': W1, 'b1': b1, 'g1': g1, 'be1': be1, 'W2': W2, 'b2': b2, 'g2': g2, 'be2': be2}
    _L3_gnn_all = _L3_gnn_setup()
    _L3_gnn_in = {k: v for k, v in _L3_gnn_all.items() if k in ('W1', 'b1', 'g1', 'be1', 'W2', 'b2', 'g2', 'be2')}
    del _L3_gnn_all
    return {'x': x, 'src': src, 'dst': dst, 'edge_attr_128': edge_attr_128, 'edge_attr_2': edge_attr_2, 'edge_weight': edge_weight, 'L1_gnn_mW1': _L1_gnn_in['mW1'], 'L1_gnn_mb1': _L1_gnn_in['mb1'], 'L1_gnn_mW2': _L1_gnn_in['mW2'], 'L1_gnn_mb2': _L1_gnn_in['mb2'], 'L1_gnn_uW1': _L1_gnn_in['uW1'], 'L1_gnn_ub1': _L1_gnn_in['ub1'], 'L1_gnn_uW2': _L1_gnn_in['uW2'], 'L1_gnn_ub2': _L1_gnn_in['ub2'], 'L1_gnn_gamma': _L1_gnn_in['gamma'], 'L1_gnn_beta': _L1_gnn_in['beta'], 'L2_gnn_weight': _L2_gnn_in['weight'], 'L2_gnn_bias': _L2_gnn_in['bias'], 'L3_gnn_W1': _L3_gnn_in['W1'], 'L3_gnn_b1': _L3_gnn_in['b1'], 'L3_gnn_g1': _L3_gnn_in['g1'], 'L3_gnn_be1': _L3_gnn_in['be1'], 'L3_gnn_W2': _L3_gnn_in['W2'], 'L3_gnn_b2': _L3_gnn_in['b2'], 'L3_gnn_g2': _L3_gnn_in['g2'], 'L3_gnn_be2': _L3_gnn_in['be2']}

def reference(x, src, dst, edge_attr_128, edge_attr_2, edge_weight, L1_gnn_mW1, L1_gnn_mb1, L1_gnn_mW2, L1_gnn_mb2, L1_gnn_uW1, L1_gnn_ub1, L1_gnn_uW2, L1_gnn_ub2, L1_gnn_gamma, L1_gnn_beta, L2_gnn_weight, L2_gnn_bias, L3_gnn_W1, L3_gnn_b1, L3_gnn_g1, L3_gnn_be1, L3_gnn_W2, L3_gnn_b2, L3_gnn_g2, L3_gnn_be2):
    import jax
    import jax.numpy as jnp

    def _L0_gnn_ref(features, edge_weight, edge_src, edge_dst):
        import jax, jax.numpy as jnp
        import numpy as np
        N_NODES = 6250
        msgs = edge_weight[:, None] * features[edge_src]
        out = jax.ops.segment_sum(msgs, edge_dst, num_segments=N_NODES)
        return out

    def _L1_gnn_ref(x, edge_attr, mW1, mb1, mW2, mb2, uW1, ub1, uW2, ub2, gamma, beta, edge_index):
        import jax, jax.numpy as jnp
        import numpy as np
        N_NODES = 6250
        N_EDGES = 100000
        IN_DIM = 128
        OUT_DIM = 128
        EDGE_DIM = 2
        LN_EPS = 1e-05
        num_nodes = x.shape[0]
        src, dst = (edge_index[0], edge_index[1])
        msg_in = jnp.concatenate([x[src], x[dst], edge_attr], axis=-1)
        msgs = jnp.maximum(msg_in @ mW1 + mb1, 0.0) @ mW2 + mb2
        agg = jax.ops.segment_sum(msgs, dst, num_segments=num_nodes)
        cnt = jax.ops.segment_sum(jnp.ones((dst.shape[0],), x.dtype), dst, num_segments=num_nodes)
        agg = agg / jnp.clip(cnt, 1.0)[:, None]
        upd_in = jnp.concatenate([x, agg], axis=-1)
        upd = jnp.maximum(upd_in @ uW1 + ub1, 0.0) @ uW2 + ub2
        upd = upd + x
        mu = jnp.mean(upd, axis=-1, keepdims=True)
        var = jnp.mean(jnp.square(upd - mu), axis=-1, keepdims=True)
        return (upd - mu) * jax.lax.rsqrt(var + LN_EPS) * gamma + beta

    def _L2_gnn_ref(h, edge_src, edge_dst, edge_val, weight, bias):
        import jax, jax.numpy as jnp
        import numpy as np
        N_NODES = 6250
        N_EDGES = 100000
        HIDDEN = 128
        support = jnp.matmul(h, weight)
        msgs = edge_val[:, None] * support[edge_src]
        out = jax.ops.segment_sum(msgs, edge_dst, num_segments=N_NODES)
        out = out + bias
        out = jax.nn.relu(out)
        return out

    def _L3_gnn_ref(h, h_edge_attr, batch, edge_index, W1, b1, g1, be1, W2, b2, g2, be2):
        import jax, jax.numpy as jnp
        import numpy as np
        N = 12500
        E = 78125
        D = 128
        L = 3
        NUM_GRAPHS = 512
        LN_EPS = 1e-05

        def _layernorm(x, g, b):
            mu = jnp.mean(x, axis=-1, keepdims=True)
            var = jnp.mean(jnp.square(x - mu), axis=-1, keepdims=True)
            return (x - mu) * jax.lax.rsqrt(var + LN_EPS) * g + b
        src = edge_index[0]
        dst = edge_index[1]
        n = h.shape[0]
        for l in range(W1.shape[0]):
            msg = h[src] + h_edge_attr
            agg = jax.ops.segment_sum(msg, dst, num_segments=n)
            out = agg + h
            z = _layernorm(out @ W1[l].T + b1[l], g1[l], be1[l])
            z = jax.nn.gelu(z, approximate=False)
            z = _layernorm(z @ W2[l].T + b2[l], g2[l], be2[l])
            h = jax.nn.gelu(z + h, approximate=False)
        return h
    edge_index = jnp.stack([src, dst])
    batch0 = jnp.zeros((6250,), jnp.int32)
    h = jnp.maximum(_layernorm(x, axis=-1), 0.0)
    x = x + _L0_gnn_ref(h, edge_weight, src, dst)
    h = jnp.maximum(_layernorm(x, axis=-1), 0.0)
    x = x + _L1_gnn_ref(h, edge_attr_2, L1_gnn_mW1, L1_gnn_mb1, L1_gnn_mW2, L1_gnn_mb2, L1_gnn_uW1, L1_gnn_ub1, L1_gnn_uW2, L1_gnn_ub2, L1_gnn_gamma, L1_gnn_beta, edge_index)
    h = jnp.maximum(_layernorm(x, axis=-1), 0.0)
    x = x + _L2_gnn_ref(h, src, dst, edge_weight, L2_gnn_weight, L2_gnn_bias)
    h = jnp.maximum(_layernorm(x, axis=-1), 0.0)
    x = x + _L3_gnn_ref(h, edge_attr_128, batch0, edge_index, L3_gnn_W1, L3_gnn_b1, L3_gnn_g1, L3_gnn_be1, L3_gnn_W2, L3_gnn_b2, L3_gnn_g2, L3_gnn_be2)
    return x

_drawn_inputs = setup_inputs


def setup_inputs(seed=0):
    import zlib

    import numpy as np

    out = dict(_drawn_inputs(seed))
    spreads = {'L1_gnn_mb1': (0.0, 0.8),
     'L1_gnn_mb2': (0.0, 0.8),
     'L1_gnn_ub1': (0.0, 0.646),
     'L1_gnn_ub2': (0.0, 0.373),
     'L1_gnn_gamma': (1.0, 0.2),
     'L1_gnn_beta': (0.0, 0.416),
     'L3_gnn_b1': (0.0, 0.8),
     'L3_gnn_g1': (1.0, 0.2),
     'L3_gnn_be1': (0.0, 0.752),
     'L3_gnn_b2': (0.0, 0.1),
     'L3_gnn_g2': (1.0, 0.539),
     'L3_gnn_be2': (0.0, 0.48)}
    factors = {'edge_attr_2': 8.0, 'L2_gnn_bias': 8.0}
    for name, (base, spread) in spreads.items():
        noise = np.random.default_rng([zlib.crc32(name.encode()), seed]).standard_normal(out[name].shape)
        drawn = base * np.exp(spread * noise) if base else spread * noise
        out[name] = jnp.asarray(drawn.astype(out[name].dtype))
    for name, factor in factors.items():
        out[name] = (out[name] * factor).astype(out[name].dtype)
    return out
```

```python
from contextlib import ExitStack

import concourse.bass as bass
from concourse import mybir

FP32 = mybir.dt.float32
I32 = mybir.dt.int32
ALU = mybir.AluOpType
ACT = mybir.ActivationFunctionType
ENG = mybir.EngineType

NODES = 6250
EDGES = 206250
F = 128
P = 128
BLOCKS = -(-NODES // P)
LAST = NODES - (BLOCKS - 1) * P
TILES = -(-EDGES // P)
TAIL = EDGES - (TILES - 1) * P
STEPS = TILES + BLOCKS - 1
SG = -(-STEPS // P)
TROWS = SG * P
U = 20
QUARTER = U // 4
BODIES = STEPS // U
SLOTS = 10
STAGED = 1 + 4 * BODIES
EPS = 1e-5
FAR = 1 << 20
LAYERS = 3
CHUNK = 4
CHUNKS = BLOCKS // CHUNK
C1 = CHUNKS + 1
assert BODIES * U == STEPS and CHUNKS * CHUNK + 1 == BLOCKS and CHUNKS % 2 == 0 and TROWS >= TILES


def build_gnn(nc, x, src, dst, weight, attr128, attr2T, mW1, mb1, mW2, mb2, uW1, ub1, uW2, ub2, gamma, beta,
              W2g, bias2g, L3W1T, L3b1, L3g1, L3be1, L3W2T, L3b2, L3g2, L3be2, out):
    ctx = ExitStack()
    with ctx:
        def sb(name, shape, dt=FP32):
            return ctx.enter_context(nc.sbuf_tensor(name, shape, dt))

        def sem(name):
            return ctx.enter_context(nc.semaphore(name))

        src_rows = nc.dram_tensor("src_rows", (TROWS, P), I32).ap()
        dst_rows = nc.dram_tensor("dst_rows", (TROWS, P), I32).ap()
        w_rows = nc.dram_tensor("w_rows", (TROWS, P), FP32).ap()
        step_tab = nc.dram_tensor("step_tab", (2, TROWS), I32).ap()
        body_tab = nc.dram_tensor("body_tab", (2, BODIES, 32), I32).ap()
        blk_row, start_row = body_tab[0], body_tab[1]
        tables = [nc.dram_tensor(f"table{k}", (NODES, F), FP32).ap() for k in range(2)]

        X = sb("X", [P, BLOCKS, F])
        H = sb("H", [P, BLOCKS, F])
        HT = sb("HT", [P, BLOCKS * P])
        ACC = sb("ACC", [P, BLOCKS, 2 * F + 1])
        T1 = sb("T1", [P, BLOCKS, F])
        T2 = sb("T2", [P, BLOCKS * F])

        G = T2[:, 0:SLOTS * F].rearrange("p (s f) -> p s f", f=F)
        HE0 = SLOTS * F
        HE = T2[:, HE0:HE0 + SLOTS * (2 * F + 1)].rearrange("p (s f) -> p s f", f=2 * F + 1)
        D0 = HE0 + SLOTS * (2 * F + 1)
        D = T2[:, D0:D0 + 4 * P].rearrange("p (s f) -> p s f", f=P)
        DT = T2[:, D0 + 4 * P:D0 + 6 * P].rearrange("p (s f) -> p s f", f=P)
        A2 = T2[0:2, D0 + 6 * P:D0 + 6 * P + SLOTS * P].rearrange("p (s f) -> p s f", f=P)
        assert D0 + 6 * P + SLOTS * P <= BLOCKS * F

        SRC = sb("SRC", [P, TROWS + U], mybir.dt.uint16)
        REL = sb("REL", [P, TROWS])
        WT = sb("WT", [P, TROWS])
        IDX = sb("IDX", [P, 4, QUARTER], I32)

        ident = sb("ident", [P, P])
        iota = sb("iota", [P, P])
        iotai = T1[:, 1, :].bitcast(I32)
        ones = sb("ones", [P, P])
        epsc = sb("epsc", [P, 1])
        mW1s = sb("mW1s", [P, 2 * F])
        mWcs = sb("mWcs", [2, F])
        mW2s = sb("mW2s", [P, F])
        uW1s = sb("uW1s", [P, 2, F])
        uW2s = sb("uW2s", [P, F])
        Wgs = sb("Wgs", [P, F])
        lw1 = sb("lw1", [P, F])
        lw2 = sb("lw2", [P, F])
        bc = {}
        for n in ("mb1", "mb2", "ub2", "gamma", "beta", "bias2g", "g2", "be2"):
            bc[n] = sb("bc_" + n, [P, F])
        ub1c = sb("ub1c", [P, 1])
        g1c = sb("g1c", [P, 1])
        be1c = sb("be1c", [P, 1])
        b1r = sb("b1r", [1, F])
        b2r = sb("b2r", [1, F])

        thr = sb("thr", [P, BLOCKS - 1])
        thrb = sb("thrb", [P, BLOCKS - 1])
        dlasti = sb("dlasti", [P, SG], I32)
        dlast = sb("dlast", [P, SG])
        svec = sb("svec", [P, SG])
        sveci = sb("sveci", [P, SG], I32)
        bs = sb("bs", [P, SG])
        b128 = sb("b128", [P, SG])
        ts = sb("ts", [P, SG])
        es = sb("es", [P, SG])
        tsi = sb("tsi", [P, SG], I32)
        bsi = sb("bsi", [P, SG], I32)
        esi = sb("esi", [P, SG], I32)
        fill = T1[:, 0, :].bitcast(I32)
        ST = sb("ST", [P, BLOCKS, 6])
        MV = sb("MV", [P, BLOCKS, 2])
        rstd = sb("rstd", [P, BLOCKS])
        nmr = sb("nmr", [P, BLOCKS])
        rcnt = sb("rcnt", [P, BLOCKS])
        cn = sb("cn", [P, BLOCKS])

        RS = HT[:, 0:SG * P].bitcast(I32).rearrange("p (g c) -> p g c", c=P)
        RD = HT[:, SG * P:2 * SG * P].bitcast(I32).rearrange("p (g c) -> p g c", c=P)
        RW = HT[:, 2 * SG * P:3 * SG * P].rearrange("p (g c) -> p g c", c=P)
        RELF = T2[:, 0:SG * P].rearrange("p (g c) -> p g c", c=P)
        cmp = T2[:, 2 * SG * P:2 * SG * P + SG * (BLOCKS - 1)].rearrange("p (g b) -> p g b", b=BLOCKS - 1)
        SRCF = T2[:, SG * P:2 * SG * P].rearrange("p (g c) -> p g c", c=P)


        PS = [ctx.enter_context(nc.psum_tensor(f"ps{k}", [P, 512], FP32)) for k in range(8)]

        waits_passed = sem("waits_passed")
        fill_ready, consts, ident_zero = sem("fill_ready"), sem("consts"), sem("ident_zero")
        x_in, weights_in, layer_in = sem("x_in"), sem("weights_in"), sem("layer_weights_in")
        rows_in, tail_in, dlast_in = sem("edge_rows_in"), sem("tail_rows_in"), sem("dlast_in")
        cmp_ready, tau_ready, steps_ready = sem("cmp_ready"), sem("tau_ready"), sem("steps_ready")
        step_rows_out, regs_in = sem("step_rows_out"), sem("step_regs_in")
        rows_gathered, rel_ready = sem("step_rows_gathered"), sem("rel_rows_ready")
        turned, turn_copied = sem("step_rows_turned"), sem("step_table_copied")
        table_out = sem("gather_table_stored")
        staged, slots_free = sem("indices_staged"), sem("slots_free")
        onehot_ready, sum_ready, acc_ready = sem("onehot_ready"), sem("step_sum_ready"), sem("acc_initialised")
        pass_done = sem("pass_done")
        dt_ps, dt_sb, pre_ps = sem("onehotT_in_psum"), sem("onehotT_in_sbuf"), sem("edge_pre_in_psum")
        hid_ready, relu_done = sem("edge_hidden_ready"), sem("edge_relu_done")
        stats_done, aggr_done, std_ready, norm_ready = sem("stats_done"), sem("aggr_done"), sem("std_ready"), sem("norm_ready")
        h_ready, link_done, part_done = sem("h_ready"), sem("vector_link"), sem("vector_part_done")
        hT_ps, hT_sb = sem("hT_in_psum"), sem("hT_in_sbuf")
        p_ps, p_sb, q_sb = sem("pq_in_psum"), sem("p_in_sbuf"), sem("q_in_sbuf")
        s_ready, sT_ps, sT_sb = sem("mean_hidden_ready"), sem("mean_hiddenT_in_psum"), sem("mean_hiddenT_in_sbuf")
        agg_ps, agg_sb, aT_ps, aT_sb = sem("agg_in_psum"), sem("agg_in_sbuf"), sem("aggT_in_psum"), sem("aggT_in_sbuf")
        u_ps, u_sb, o_ps, o_sb = sem("updT_in_psum"), sem("updT_in_sbuf"), sem("upd_in_psum"), sem("upd_in_sbuf")
        sup_ps, sup_sb = sem("support_in_psum"), sem("support_in_sbuf")
        oT_ps, oT_sb, z_ps, z_sb = sem("outT_in_psum"), sem("outT_in_sbuf"), sem("z_in_psum"), sem("z_in_sbuf")
        zn_ready, zT_ps, zT_sb = sem("z_normed"), sem("zT_in_psum"), sem("zT_in_sbuf")
        y_ps, y_sb, yn_ready, gelu_done = sem("y_in_psum"), sem("y_in_sbuf"), sem("y_normed"), sem("layer_out_ready")
        layer_used, out_ready, out_stored = sem("layer_weights_used"), sem("out_ready"), sem("out_stored")
        gathered = [sem(f"gathered{k}") for k in range(SLOTS)]
        attr_in = [sem(f"attr_in{k}") for k in range(SLOTS)]
        copied = (hT_sb, p_sb, q_sb, sT_sb, agg_sb, aT_sb, u_sb, o_sb, sup_sb, oT_sb, z_sb, zT_sb, y_sb)

        def chunks(eng, body):
            with eng.Fori(0, CHUNKS // 2) as i:
                body(i * 2, CHUNK, 0)
                body(i * 2 + 1, CHUNK, 1)
            body(CHUNKS, 1, 0)

        def chunks_of_pe(body):
            for c in range(C1):
                body(c, CHUNK if c < CHUNKS else 1, c % 2)

        def wait_alone(eng, signal, value):
            eng.wait_ge(signal, value)
            eng.sem_inc(waits_passed, 1)

        def node_store(eng, dram, array, signal):
            eng.dma_start(dram[0:(BLOCKS - 1) * P, :].rearrange("(b p) f -> p b f", p=P),
                          array[:, 0:BLOCKS - 1, :]).then_inc(signal, 16)
            eng.dma_start(dram[(BLOCKS - 1) * P:NODES, :], array[0:LAST, BLOCKS - 1, :]).then_inc(signal, 16)

        def registers(engine, row, i, top):
            _, values = nc.values_load_multi_w_load_instructions(
                row[bass.ds(i, 1), 0:U], engines=[engine], min_val=0, max_val=top,
                skip_runtime_bounds_check_because="computed on the chip, at most the last block or tile")
            return values

        def blk(array, c, nb):
            return array[:, bass.ds(c * CHUNK, nb), :]

        def cols(array, c, nb):
            return array[:, bass.ds(c * CHUNK * P, nb * P)]

        def bank(pair, par, nb):
            return PS[pair + par][:, 0:nb * P]

        def bank3(pair, par, nb):
            return bank(pair, par, nb).rearrange("p (b f) -> p b f", f=F)

        T2n = T2[:, :].rearrange("p (b f) -> p b f", f=F)
        ONE = 2 * F
        block = ctx.enter_context(nc.Block())

        @block.sync
        def _(sp):
            sp.dma_start(X[:, 0:BLOCKS - 1, :], x[0:(BLOCKS - 1) * P, :].rearrange("(b p) f -> p b f", p=P)).then_inc(x_in, 16)
            sp.wait_ge(acc_ready, 1)
            sp.dma_start(X[0:LAST, BLOCKS - 1, :], x[(BLOCKS - 1) * P:NODES, :]).then_inc(x_in, 16)
            n0 = (TILES - 1) * P
            for rows, flat in ((src_rows, src), (dst_rows, dst), (w_rows, weight)):
                sp.dma_start(rows[0:TILES - 1, :].rearrange("t c -> (t c)").rearrange("(a b) -> a b", a=16),
                             flat[0:n0].rearrange("(a b) -> a b", a=16)).then_inc(rows_in, 16)
                sp.dma_start(rows[TILES - 1:TILES, :], flat[EDGES - P:EDGES].rearrange("(a b) -> a b", a=1)).then_inc(tail_in, 16)
            sp.wait_ge(fill_ready, 3)
            sp.dma_start(dst_rows[TILES:TROWS, :], fill[0:TROWS - TILES, :]).then_inc(rows_in, 16)
            sp.dma_start(src_rows[TILES:TROWS, :], iotai[0:TROWS - TILES, :]).then_inc(rows_in, 16)
            sp.dma_start(w_rows[TILES:TROWS, :], ones[0:TROWS - TILES, :]).then_inc(rows_in, 16)
            sp.wait_ge(tail_in, 48)
            sp.dma_start(dst_rows[TILES - 1:TILES, 0:P - TAIL], fill[0:1, 0:P - TAIL]).then_inc(rows_in, 16)
            sp.wait_ge(rows_in, 16 * 7)
            full = (TILES - 1) // P
            sp.dma_start(dlasti[:, 0:full], dst_rows[0:full * P, P - 1:P].rearrange("(g p) c -> p (g c)", p=P),
                         allow_slow_non_contiguous=True).then_inc(dlast_in, 16)
            sp.dma_start(dlasti[0:TILES - 1 - full * P, full:full + 1], dst_rows[full * P:TILES - 1, P - 1:P],
                         allow_slow_non_contiguous=True).then_inc(dlast_in, 16)
            for to, of in ((mW1s[:, 0:F], mW1[0:F, :]), (mW1s[:, F:2 * F], mW1[F:2 * F, :]), (mWcs[:, :], mW1[2 * F:2 * F + 2, :]),
                           (mW2s[:, :], mW2), (uW1s[:, 0, :], uW1[0:F, :]), (uW1s[:, 1, :], uW1[F:2 * F, :]), (uW2s[:, :], uW2),
                           (Wgs[:, :], W2g), (bc["mb1"][:, :], mb1.partition_broadcast(P)), (bc["mb2"][:, :], mb2.partition_broadcast(P)),
                           (bc["ub2"][:, :], ub2.partition_broadcast(P)), (bc["gamma"][:, :], gamma.partition_broadcast(P)),
                           (bc["beta"][:, :], beta.partition_broadcast(P)), (bc["bias2g"][:, :], bias2g.partition_broadcast(P)),
                           (ub1c[:, :], ub1.rearrange("(f a) -> f a", a=1))):
                sp.dma_start(to, of).then_inc(weights_in, 16)
            sp.wait_ge(steps_ready, 1)
            sp.dma_start(step_tab[0, :].rearrange("(g p) -> p g", p=P), bsi[:, :], allow_slow_non_contiguous=True).then_inc(step_rows_out, 16)
            sp.dma_start(step_tab[1, :].rearrange("(g p) -> p g", p=P), esi[:, :], allow_slow_non_contiguous=True).then_inc(step_rows_out, 16)
            sp.wait_ge(step_rows_out, 32)
            for k in range(2):
                sp.dma_start(body_tab[k, :, 0:U], step_tab[k, 0:STEPS].rearrange("(i u) -> i u", u=U)).then_inc(regs_in, 16)
            sp.wait_ge(h_ready, C1)
            node_store(sp, tables[0], H, table_out)
            sp.wait_ge(p_sb, C1 + 1)
            node_store(sp, tables[1], T2n, table_out)
            sp.wait_ge(regs_in, 32)
            sp.wait_ge(acc_ready, 2)
            with sp.Fori(0, BODIES) as i:
                first = registers(ENG.SP, start_row, i, EDGES - P)
                for u in range(U):
                    k = u % SLOTS
                    sp.wait_ge(slots_free, i * U + (STEPS + u + 1))
                    sp.dma_start(HE[:, k, F:2 * F], attr128[bass.ds(first[u], P), :]).then_inc(attr_in[k], 16)
                    sp.dma_start(A2[:, k, :], attr2T[:, bass.ds(first[u], P)]).then_inc(attr_in[k], 16)
            sp.wait_ge(sup_sb, C1 + 1)
            node_store(sp, tables[0], T1, table_out)
            with sp.Fori(0, LAYERS) as l:
                wait_alone(sp, layer_used, l)
                wait_alone(sp, gelu_done, l * C1)
                for to, of in ((lw1[:, :], L3W1T[bass.ds(l * F, F), :]), (lw2[:, :], L3W2T[bass.ds(l * F, F), :]),
                               (b1r[:, :], L3b1[bass.ds(l, 1), :]), (b2r[:, :], L3b2[bass.ds(l, 1), :]),
                               (bc["g2"][:, :], L3g2[bass.ds(l, 1), :].broadcast_to([P, F])),
                               (bc["be2"][:, :], L3be2[bass.ds(l, 1), :].broadcast_to([P, F])),
                               (g1c[:, :], L3g1[bass.ds(l * F, F), :]), (be1c[:, :], L3be1[bass.ds(l * F, F), :])):
                    sp.dma_start(to, of).then_inc(layer_in, 16)
                sp.wait_ge(h_ready, 4 * C1)
                node_store(sp, tables[1], H, table_out)
            sp.wait_ge(out_ready, 1)
            node_store(sp, out, X, out_stored)
            sp.wait_ge(out_stored, 32)

        @block.gpsimd
        def _(pool):
            pool.memset(fill[:, :], FAR).then_inc(fill_ready, 1)
            pool.iota(iotai[:, :], pattern=[[1, P]], base=0, channel_multiplier=0).then_inc(fill_ready, 1)
            pool.memset(ones[:, :], 1.0).then_inc(fill_ready, 1)
            pool.iota(sveci[:, :], pattern=[[P, SG]], base=0, channel_multiplier=1).then_inc(consts, 1)
            pool.memset(ident[:, :], 0.0).then_inc(ident_zero, 1)
            pool.wait_ge(ident_zero, 1)
            pool.affine_select(out=ident[:, :], in_=ident[:, :], compare_op=ALU.not_equal, fill=1.0, base=0,
                               pattern=[[-1, P]], channel_multiplier=1).then_inc(consts, 1)
            pool.memset(epsc[:, :], EPS).then_inc(consts, 1)
            pool.memset(SRC[:, TROWS:TROWS + U], 0).then_inc(consts, 1)
            pool.wait_ge(rows_in, 16 * 7)
            pool.wait_ge(steps_ready, 1)
            for g in range(SG):
                for rows, to in ((src_rows, RS), (dst_rows, RD), (w_rows, RW)):
                    pool.indirect_dma_start(to[:, g, :], None, rows, bass.IndirectOffsetOnAxis(ap=tsi[:, g:g + 1], axis=0)
                                            ).then_inc(rows_gathered, 16)
            pool.sem_inc(slots_free, SLOTS)
            pool.wait_ge(turn_copied, 3 * SG)

            def stage(col, q, n):
                pool.tensor_copy(IDX[:, q, :], SRC[:, bass.ds(col, QUARTER)]).then_inc(staged, 1)

            def gathers(table, stored, at):
                wait_alone(pool, table_out, stored)
                stage(0, 0, 0)
                with pool.Fori(0, BODIES) as i:
                    for q in range(4):
                        stage(i * U + (q + 1) * QUARTER, (q + 1) % 4, 0)
                        pool.wait_ge(staged, at * STAGED + (i * 4 + q + 1))
                        for u in range(q * QUARTER, (q + 1) * QUARTER):
                            wait_alone(pool, slots_free, at * STEPS + (i * U + u + 1))
                            pool.indirect_dma_start(G[:, u % SLOTS, :], None, table,
                                                    bass.IndirectOffsetOnAxis(ap=IDX[:, q, u % QUARTER:u % QUARTER + 1], axis=0)
                                                    ).then_inc(gathered[u % SLOTS], 16)
                wait_alone(pool, staged, (at + 1) * STAGED)

            gathers(tables[0], 32, 0)
            gathers(tables[1], 64, 1)
            gathers(tables[0], 96, 2)
            with pool.Fori(0, LAYERS) as l:
                gathers(tables[1], l * 32 + 128, l + 3)

        @block.scalar
        def _(act):
            for s in copied:
                if s not in (q_sb, agg_sb, o_sb, sup_sb):
                    act.sem_inc(s, 1)

            def stds(n):
                act.wait_ge(aggr_done, n * 6)
                act.activation(rstd[:, :], MV[:, :, 1], ACT.Sqrt, bias=epsc[:, 0:1]).then_inc(std_ready, 1)

            def relu_norm(n):
                act.wait_ge(norm_ready, n)

                def body(c, nb, par):
                    for j in range(nb):
                        b = c * CHUNK + j
                        last = act.activation(H[:, b, :], X[:, b, :], ACT.Relu, bias=nmr[:, bass.ds(b, 1)], scale=rstd[:, bass.ds(b, 1)])
                    last.then_inc(h_ready, 1)
                chunks(act, body)

            def copy_out(ready, done, to, pair, func=ACT.Copy, base=0, as_blocks=False, **kw):
                def body(c, nb, par):
                    act.wait_ge(ready, base + c + 1)
                    if as_blocks:
                        act.activation(blk(to, c, nb), bank3(pair, par, nb), func, **kw).then_inc(done, 1)
                    else:
                        act.activation(cols(to, c, nb), bank(pair, par, nb), func, **kw).then_inc(done, 1)
                chunks(act, body)

            act.wait_ge(consts, 4)
            stds(1)
            relu_norm(1)
            for k in range(3 * SG):
                act.wait_ge(turned, k + 1)
                act.activation((SRC, REL, WT)[k % 3][:, k // 3 * P:(k // 3 + 1) * P], PS[k % 4][:, 0:P], ACT.Copy).then_inc(turn_copied, 1)
            stds(2)
            relu_norm(2)
            copy_out(hT_ps, hT_sb, HT, 0)
            copy_out(p_ps, p_sb, T2n, 2, as_blocks=True)
            act.wait_ge(table_out, 64)
            with act.Fori(0, BODIES) as i:
                for u in range(U + 1):
                    if u < U:
                        act.wait_ge(dt_ps, i * U + u + 1)
                        act.activation(DT[:, u % 2, :], PS[u % 2][:, 0:P], ACT.Copy).then_inc(dt_sb, 1)
                    if u >= 1:
                        act.wait_ge(hid_ready, i * U + u)
                        act.activation(HE[:, (u - 1) % SLOTS, 0:F], HE[:, (u - 1) % SLOTS, 0:F], ACT.Relu).then_inc(relu_done, 1)
            copy_out(sT_ps, sT_sb, T2, 0)
            copy_out(aT_ps, aT_sb, T2, 4)
            copy_out(u_ps, u_sb, T2, 6, func=ACT.Relu, bias=ub1c[:, 0:1])
            stds(3)
            stds(4)
            relu_norm(4)
            copy_out(hT_ps, hT_sb, HT, 0, base=C1)
            stds(5)
            relu_norm(5)
            with act.Fori(0, LAYERS) as l:
                copy_out(oT_ps, oT_sb, HT, 0, base=l * C1)
                copy_out(z_ps, z_sb, T1, 2, base=l * C1, as_blocks=True)
                stds(l * 2 + 6)
                act.wait_ge(layer_in, l * 128 + 128)
                copy_out(zT_ps, zT_sb, HT, 4, func=ACT.Gelu, base=l * C1, bias=be1c[:, 0:1], scale=g1c[:, 0:1])
                copy_out(y_ps, y_sb, T1, 6, base=l * C1, as_blocks=True)
                stds(l * 2 + 7)

                def layer_out(c, nb, par):
                    act.wait_ge(yn_ready, l * C1 + c + 1)
                    act.activation(blk(H, c, nb), blk(T1, c, nb), ACT.Gelu).then_inc(gelu_done, 1)
                chunks(act, layer_out)

        @block.tensor
        def _(pe):
            pe.wait_ge(consts, 4)
            pe.wait_ge(fill_ready, 3)
            for g in range(SG):
                pe.wait_ge(cmp_ready, g + 1)
                mm = pe.matmul(PS[7][:, 0:BLOCKS - 1], ones[:, :], cmp[:, g, :], start=(g == 0), stop=(g == SG - 1))
            mm.then_inc(tau_ready, 1)
            for k in range(3 * SG):
                pe.wait_ge(rel_ready, k // 3 * 2 + min(k % 3 + 1, 2))
                if k >= 4:
                    pe.wait_ge(turn_copied, k - 3)
                pe.transpose(PS[k % 4][:, 0:P], (SRCF, RELF, RW)[k % 3][:, k // 3, :], ident[:, :]).then_inc(turned, 1)

            def step_sums(at):
                with pe.Fori(0, BODIES) as i:
                    for u in range(U):
                        pe.wait_ge(gathered[u % SLOTS], (at * BODIES + i) * 32 + 16 * (u // SLOTS + 1))
                        pe.wait_ge(onehot_ready, at * STEPS + (i * U + u + 1))
                        pe.matmul(PS[4 + u % 4][:, 0:F], D[:, u % 4, :], G[:, u % SLOTS, :], start=True, stop=True).then_inc(sum_ready, 1)

            def turn(ready, offset, ps, sb_, array, pair, base=0):
                def body(c, nb, par):
                    pe.wait_ge(ready, c + offset)
                    pe.wait_ge(sb_, base + c)
                    for j in range(nb):
                        mm = pe.transpose(PS[pair + par][:, j * P:(j + 1) * P], array[:, c * CHUNK + j, :], ident[:, :])
                    mm.then_inc(ps, 1)
                chunks_of_pe(body)

            def times(ready, offset, ps, sb_, arrayT, weights, pair, base=0, bias=None):
                def body(c, nb, par):
                    pe.wait_ge(ready, c + offset)
                    pe.wait_ge(sb_, base + c)
                    for j in range(nb):
                        to = PS[pair + par][:, j * P:(j + 1) * P]
                        if bias is not None:
                            pe.matmul(to, ones[0:1, :], bias, start=True, stop=False)
                        mm = pe.matmul(to, arrayT[:, bass.ds((c * CHUNK + j) * P, P)], weights, start=bias is None, stop=True)
                    mm.then_inc(ps, 1)
                chunks_of_pe(body)

            pe.wait_ge(weights_in, 16 * 15)
            step_sums(0)
            turn(h_ready, C1 + 1, hT_ps, hT_sb, H, 0)

            def pq(c, nb, par):
                pe.wait_ge(hT_sb, c + 2)
                pe.wait_ge(p_sb, c)
                pe.wait_ge(q_sb, c)
                for j in range(nb):
                    lhs = HT[:, bass.ds((c * CHUNK + j) * P, P)]
                    pe.matmul(PS[2 + par][:, j * P:(j + 1) * P], lhs, mW1s[:, 0:F], start=True, stop=True)
                    mm = pe.matmul(PS[4 + par][:, j * P:(j + 1) * P], lhs, mW1s[:, F:2 * F], start=True, stop=True)
                mm.then_inc(p_ps, 1)
            chunks_of_pe(pq)
            pe.wait_ge(regs_in, 32)
            pe.wait_ge(q_sb, C1 + 1)
            with pe.Fori(0, BODIES) as i:
                b = registers(ENG.PE, blk_row, i, BLOCKS - 1)
                for u in range(U + 2):
                    if u < U:
                        pe.wait_ge(onehot_ready, i * U + (STEPS + u + 1))
                        pe.transpose(PS[u % 2][:, 0:P], D[:, u % 4, :], ident[:, :]).then_inc(dt_ps, 1)
                    if 1 <= u <= U:
                        v, k = u - 1, (u - 1) % SLOTS
                        pe.wait_ge(dt_sb, i * U + u)
                        pe.wait_ge(attr_in[k], i * 64 + 32 * (v // SLOTS + 1))
                        pe.matmul(PS[2 + v % 2][:, 0:F], DT[:, v % 2, :], T1[:, b[v], :], start=True, stop=False)
                        pe.matmul(PS[2 + v % 2][:, 0:F], A2[:, k, :], mWcs[:, :], start=False, stop=True).then_inc(pre_ps, 1)
                    if u >= 2:
                        v, k = u - 2, (u - 2) % SLOTS
                        pe.wait_ge(relu_done, i * U + u - 1)
                        pe.matmul(PS[4 + v % 4][:, 0:2 * F + 1], D[:, v % 4, :], HE[:, k, :], start=True, stop=True).then_inc(sum_ready, 1)
            turn(s_ready, 1, sT_ps, sT_sb, ACC[:, :, 0:F], 0)
            times(sT_sb, 2, agg_ps, agg_sb, T2, mW2s[:, :], 2)
            turn(agg_sb, 2, aT_ps, aT_sb, ACC[:, :, 0:F], 4)

            def update(c, nb, par):
                pe.wait_ge(aT_sb, c + 2)
                pe.wait_ge(u_sb, c)
                pe.matmul(bank(6, par, nb), uW1s[:, 0, :], cols(HT, c, nb), start=True, stop=False)
                pe.matmul(bank(6, par, nb), uW1s[:, 1, :], cols(T2, c, nb), start=False, stop=True).then_inc(u_ps, 1)
            chunks_of_pe(update)
            times(u_sb, 2, o_ps, o_sb, T2, uW2s[:, :], 0)
            turn(h_ready, 2 * C1 + 1, hT_ps, hT_sb, H, 0, base=C1)
            times(hT_sb, C1 + 2, sup_ps, sup_sb, HT, Wgs[:, :], 2)
            step_sums(2)
            with pe.Fori(0, LAYERS) as l:
                step_sums(l + 3)
                pe.wait_ge(layer_in, l * 128 + 128)
                turn(pass_done, l * C1 + 1, oT_ps, oT_sb, T1, 0, base=l * C1)
                times(oT_sb, l * C1 + 2, z_ps, z_sb, HT, lw1[:, :], 2, base=l * C1, bias=b1r[:, :])
                turn(zn_ready, l * C1 + 1, zT_ps, zT_sb, T1, 4, base=l * C1)
                times(zT_sb, l * C1 + 2, y_ps, y_sb, HT, lw2[:, :], 6, base=l * C1, bias=b2r[:, :])

        @block.vector
        def _(dve):
            links = [0]

            def link(ins):
                ins.then_inc(link_done, 1)
                links[0] += 1
                dve.wait_ge(link_done, links[0])

            for s in (q_sb, agg_sb, o_sb, sup_sb):
                dve.sem_inc(s, 1)

            def per_block(body):
                with dve.Fori(0, BLOCKS // 7) as i:
                    for j in range(7):
                        body(i * 7 + j)

            def statistics(array, n, wait=None):
                if wait is None:
                    per_block(lambda b: dve.bn_stats(ST[:, b, :], array[:, b, :]).then_inc(stats_done, 1))
                wait_alone(dve, stats_done, n * BLOCKS)
                steps = (lambda: dve.tensor_tensor(MV[:, :, 0], ST[:, :, 1], ST[:, :, 4], ALU.add),
                         lambda: dve.tensor_tensor(MV[:, :, 1], ST[:, :, 1], ST[:, :, 4], ALU.subtract),
                         lambda: dve.tensor_tensor(ST[:, :, 2], ST[:, :, 2], ST[:, :, 5], ALU.add),
                         lambda: dve.scalar_tensor_tensor(MV[:, :, 1], MV[:, :, 1], 0.25, MV[:, :, 1], ALU.mult, ALU.mult),
                         lambda: dve.tensor_scalar(MV[:, :, 0], MV[:, :, 0], 0.5, None, ALU.mult),
                         lambda: dve.scalar_tensor_tensor(MV[:, :, 1], ST[:, :, 2], 1.0 / F, MV[:, :, 1], ALU.mult, ALU.add))
                for k, step in enumerate(steps):
                    step().then_inc(aggr_done, 1)
                    dve.wait_ge(aggr_done, (n - 1) * len(steps) + (k + 1))

            def rstds(n):
                dve.wait_ge(std_ready, n)
                dve.reciprocal(rstd[:, :], rstd[:, :]).then_inc(part_done, 1)
                dve.wait_ge(part_done, n)
                dve.scalar_tensor_tensor(nmr[:, :], MV[:, :, 0], -1.0, rstd[:, :], ALU.mult, ALU.mult).then_inc(norm_ready, 1)

            link(dve.memset(X[:, BLOCKS - 1, :], 0.0))
            dve.sem_inc(acc_ready, 1)
            dve.wait_ge(consts, 4)
            link(dve.tensor_copy(iota[:, :], iotai[:, :]))
            link(dve.tensor_copy(svec[:, :], sveci[:, :]))
            link(dve.memset(dlast[:, :], float(FAR)))
            link(dve.tensor_scalar(thrb[:, :], iota[:, 0:BLOCKS - 1], 1.0, float(P), ALU.add, ALU.mult))
            dve.wait_ge(dlast_in, 32)
            full = (TILES - 1) // P
            dve.tensor_copy(dlast[:, 0:full], dlasti[:, 0:full])
            link(dve.tensor_copy(dlast[0:TILES - 1 - full * P, full:full + 1], dlasti[0:TILES - 1 - full * P, full:full + 1]))
            for g in range(SG):
                dve.tensor_scalar(cmp[:, g, :], thrb[:, :], dlast[:, g:g + 1], None, ALU.is_gt).then_inc(cmp_ready, 1)
            dve.wait_ge(tau_ready, 1)
            link(dve.scalar_tensor_tensor(thr[:, :], iota[:, 0:BLOCKS - 1], 1.0, PS[7][:, 0:BLOCKS - 1], ALU.add, ALU.add))
            for g in range(SG):
                last = dve.tensor_scalar(cmp[:, g, :], thr[:, :], svec[:, g:g + 1], None, ALU.is_le, ALU.add, accum_out=bs[:, g:g + 1])
            link(last)
            link(dve.tensor_tensor(ts[:, :], svec[:, :], bs[:, :], ALU.subtract))
            dve.tensor_scalar(es[:, :], ts[:, :], float(P), float(EDGES - P), ALU.mult, ALU.min)
            dve.tensor_scalar(b128[:, :], bs[:, :], float(P), None, ALU.mult)
            dve.tensor_copy(tsi[:, :], ts[:, :])
            link(dve.tensor_copy(bsi[:, :], bs[:, :]))
            dve.tensor_copy(esi[:, :], es[:, :]).then_inc(steps_ready, 1)
            dve.wait_ge(x_in, 32)
            statistics(X, 1)
            rstds(1)
            dve.wait_ge(rows_gathered, 16 * 3 * SG)
            for g in range(SG):
                dve.tensor_copy(SRCF[:, g, :], RS[:, g, :]).then_inc(rel_ready, 1)
                dve.tensor_scalar(RELF[:, g, :], RD[:, g, :], b128[:, g:g + 1], None, ALU.subtract).then_inc(rel_ready, 1)
            dve.wait_ge(turn_copied, 3 * SG)
            dve.wait_ge(regs_in, 32)

            def onehot(i, u, weighted):
                col = bass.ds(i * U + u, 1)
                return dve.tensor_scalar(D[:, u % 4, :], iota[:, :], REL[:, col], WT[:, col] if weighted else None,
                                         ALU.is_equal, ALU.mult if weighted else ALU.bypass).then_inc(onehot_ready, 1)

            def accumulate(i, u, at, to, width):
                dve.wait_ge(sum_ready, at * STEPS + (i * U + u + 1))
                dve.wait_ge(slots_free, at * STEPS + (i * U + u + SLOTS))
                dve.tensor_tensor(to, to, PS[4 + u % 4][:, 0:width], ALU.add).then_inc(slots_free, 1)

            def pass_sums(at, array, weighted):
                with dve.Fori(0, BODIES) as i:
                    b = registers(ENG.DVE, blk_row, i, BLOCKS - 1)
                    for u in range(U + 2):
                        if u < U:
                            onehot(i, u, weighted)
                        if u >= 2:
                            accumulate(i, u - 2, at, array[:, b[u - 2], :], F)
                wait_alone(dve, slots_free, (at + 1) * STEPS + SLOTS)

            dve.wait_ge(h_ready, C1)
            pass_sums(0, X, True)
            statistics(X, 2)
            rstds(2)

            def q_out(c, nb, par):
                dve.wait_ge(p_ps, c + 1)
                for j in range(nb):
                    last = dve.tensor_tensor(T1[:, c * CHUNK + j, :], PS[4 + par][:, j * P:(j + 1) * P], bc["mb1"][:, :], ALU.add)
                last.then_inc(q_sb, 1)
            chunks(dve, q_out)
            dve.wait_ge(table_out, 64)
            dve.memset(HE[:, :, ONE:ONE + 1], 1.0)
            link(dve.memset(ACC[:, :, :], 0.0))
            dve.sem_inc(acc_ready, 1)
            with dve.Fori(0, BODIES) as i:
                b = registers(ENG.DVE, blk_row, i, BLOCKS - 1)
                for u in range(U + 2):
                    if u < U:
                        onehot(i, u, False)
                    if 1 <= u <= U:
                        v, k = u - 1, (u - 1) % SLOTS
                        dve.wait_ge(pre_ps, i * U + u)
                        dve.wait_ge(gathered[k], i * 32 + 16 * (v // SLOTS + 1) + BODIES * 32)
                        dve.tensor_tensor(HE[:, k, 0:F], PS[2 + v % 2][:, 0:F], G[:, k, :], ALU.add).then_inc(hid_ready, 1)
                    if u >= 2:
                        accumulate(i, u - 2, 1, ACC[:, b[u - 2], :], 2 * F + 1)
            dve.wait_ge(slots_free, 2 * STEPS + SLOTS)
            link(dve.tensor_scalar(rcnt[:, :], ACC[:, :, ONE], 1.0, None, ALU.max))
            link(dve.reciprocal(rcnt[:, :], rcnt[:, :]))
            link(dve.tensor_tensor(cn[:, :], ACC[:, :, ONE], rcnt[:, :], ALU.mult))

            def mean_hidden(c, nb, par):
                for j in range(nb):
                    b = c * CHUNK + j
                    last = dve.tensor_scalar(ACC[:, b, 0:F], ACC[:, b, 0:F], rcnt[:, bass.ds(b, 1)], None, ALU.mult)
                last.then_inc(s_ready, 1)
            chunks(dve, mean_hidden)

            def agg_out(c, nb, par):
                dve.wait_ge(agg_ps, c + 1)
                for j in range(nb):
                    b = c * CHUNK + j
                    last = dve.scalar_tensor_tensor(ACC[:, b, 0:F], bc["mb2"][:, :], cn[:, bass.ds(b, 1)], PS[2 + par][:, j * P:(j + 1) * P], ALU.mult, ALU.add)
                last.then_inc(agg_sb, 1)
            chunks(dve, agg_out)
            wide = lambda n, nb: bc[n][:, :].rearrange("p (a f) -> p a f", a=1).broadcast_to([P, nb, F])

            def residual(c, nb, par):
                dve.tensor_tensor(blk(H, c, nb), blk(H, c, nb), wide("ub2", nb), ALU.add).then_inc(s_ready, 1)
            chunks(dve, residual)
            dve.wait_ge(s_ready, 2 * C1)

            def upd_out(c, nb, par):
                dve.wait_ge(o_ps, c + 1)
                dve.tensor_tensor(blk(T1, c, nb), bank3(0, par, nb), blk(H, c, nb), ALU.add).then_inc(o_sb, 1)
            chunks(dve, upd_out)
            dve.wait_ge(o_sb, C1 + 1)
            statistics(T1, 3)
            rstds(3)

            def normed(n, to, signal, base):
                wait_alone(dve, norm_ready, n)

                def body(c, nb, par):
                    for j in range(nb):
                        b = c * CHUNK + j
                        last = dve.tensor_scalar(to[:, b, :], to[:, b, :], MV[:, b, 0:1], rstd[:, bass.ds(b, 1)], ALU.subtract, ALU.mult)
                    last.then_inc(signal, 1)
                chunks(dve, body)

            def times_plus(array, scale, shift, plus, signal_a, a0, signal_b):
                def one(c, nb, par):
                    dve.tensor_tensor(blk(array, c, nb), blk(array, c, nb), wide(scale, nb), ALU.mult).then_inc(signal_a, 1)

                def two(c, nb, par):
                    dve.wait_ge(signal_a, a0 + c + 1)
                    dve.tensor_tensor(blk(array, c, nb), blk(array, c, nb), wide(shift, nb) if plus is None else blk(plus, c, nb),
                                      ALU.add).then_inc(signal_b, 1)
                chunks(dve, one)
                chunks(dve, two)

            normed(3, T1, s_ready, 0)
            dve.wait_ge(s_ready, 3 * C1)
            times_plus(T1, "gamma", "beta", None, s_ready, 3 * C1, o_sb)

            def add_to_x(c, nb, par):
                dve.wait_ge(o_sb, c + C1 + 2)
                dve.tensor_tensor(blk(X, c, nb), blk(X, c, nb), blk(T1, c, nb), ALU.add).then_inc(s_ready, 1)
            chunks(dve, add_to_x)
            dve.wait_ge(s_ready, 5 * C1)
            statistics(X, 4)
            rstds(4)

            def support_out(c, nb, par):
                dve.wait_ge(sup_ps, c + 1)
                dve.tensor_copy(blk(T1, c, nb), bank3(2, par, nb)).then_inc(sup_sb, 1)
            chunks(dve, support_out)

            def bias_init(c, nb, par):
                dve.tensor_copy(blk(H, c, nb), wide("bias2g", nb)).then_inc(s_ready, 1)
            dve.wait_ge(hT_sb, 2 * C1 + 1)
            chunks(dve, bias_init)
            dve.wait_ge(s_ready, 6 * C1)
            pass_sums(2, H, True)

            def relu_to_x(c, nb, par):
                dve.scalar_tensor_tensor(blk(X, c, nb), blk(H, c, nb), 0.0, blk(X, c, nb), ALU.max, ALU.add).then_inc(s_ready, 1)
            chunks(dve, relu_to_x)
            dve.wait_ge(s_ready, 7 * C1)
            statistics(X, 5)
            rstds(5)
            dve.wait_ge(h_ready, 4 * C1)
            with dve.Fori(0, LAYERS) as l:
                wait_alone(dve, gelu_done, l * C1)

                def out_init(c, nb, par):
                    dve.tensor_tensor(blk(T1, c, nb), blk(H, c, nb), ACC[:, bass.ds(c * CHUNK, nb), F:2 * F], ALU.add).then_inc(agg_sb, 1)
                chunks(dve, out_init)
                wait_alone(dve, agg_sb, (l + 2) * C1 + 1)
                pass_sums(l + 3, T1, False)
                dve.sem_inc(pass_done, C1)
                wait_alone(dve, z_sb, (l + 1) * C1 + 1)
                statistics(T1, l * 2 + 6)
                rstds(l * 2 + 6)
                normed(l * 2 + 6, T1, zn_ready, 0)
                wait_alone(dve, y_sb, (l + 1) * C1 + 1)
                statistics(T1, l * 2 + 7)
                rstds(l * 2 + 7)
                dve.wait_ge(layer_in, l * 128 + 128)
                wait_alone(dve, table_out, l * 32 + 128)

                def shifted_h(c, nb, par):
                    dve.tensor_tensor(blk(H, c, nb), blk(H, c, nb), wide("be2", nb), ALU.add).then_inc(q_sb, 1)
                chunks(dve, shifted_h)
                normed(l * 2 + 7, T1, q_sb, 0)
                wait_alone(dve, q_sb, (l * 3 + 3) * C1 + 1)
                times_plus(T1, "g2", None, H, q_sb, (l * 3 + 3) * C1 + 1, yn_ready)
                dve.sem_inc(layer_used, 1)
            dve.wait_ge(gelu_done, LAYERS * C1)

            def final(c, nb, par):
                dve.tensor_tensor(blk(X, c, nb), blk(X, c, nb), blk(H, c, nb), ALU.add).then_inc(s_ready, 1)
            chunks(dve, final)
            dve.wait_ge(s_ready, 8 * C1)
            dve.sem_inc(out_ready, 1)


_INS = ["x", "src", "dst", "edge_weight", "edge_attr_128", "edge_attr_2", "L1_gnn_mW1", "L1_gnn_mb1", "L1_gnn_mW2", "L1_gnn_mb2",
        "L1_gnn_uW1", "L1_gnn_ub1", "L1_gnn_uW2", "L1_gnn_ub2", "L1_gnn_gamma", "L1_gnn_beta", "L2_gnn_weight", "L2_gnn_bias",
        "L3_gnn_W1", "L3_gnn_b1", "L3_gnn_g1", "L3_gnn_be1", "L3_gnn_W2", "L3_gnn_b2", "L3_gnn_g2", "L3_gnn_be2"]


def kernel(**inputs):
    import numpy as np
    import concourse.bacc as bacc
    from concourse.bass_utils import run_bass_kernel_spmd

    nc = bacc.Bacc("TRN2", target_bir_lowering=False, num_devices=1)
    layout = {"edge_attr_2": lambda a: a.T,
              "L3_gnn_W1": lambda a: a.transpose(0, 2, 1).reshape(LAYERS * F, F),
              "L3_gnn_W2": lambda a: a.transpose(0, 2, 1).reshape(LAYERS * F, F),
              "L3_gnn_g1": lambda a: a.reshape(LAYERS * F, 1),
              "L3_gnn_be1": lambda a: a.reshape(LAYERS * F, 1)}
    arrays, args = {}, []
    for name in _INS:
        a = np.asarray(inputs[name])
        a = np.ascontiguousarray(layout[name](a) if name in layout else a)
        arrays[f"in_{name}"] = a
        args.append(nc.dram_tensor(f"in_{name}", a.shape, mybir.dt.from_np(a.dtype), kind="ExternalInput").ap())
    out = nc.dram_tensor("out", (NODES, F), FP32, kind="ExternalOutput").ap()
    build_gnn(nc, *args, out)
    r = run_bass_kernel_spmd(nc, [arrays], core_ids=[0])
    return r.results[0]["out"]
```

```python
from contextlib import ExitStack

import concourse.bass as bass
from concourse import mybir

FP32 = mybir.dt.float32
I32 = mybir.dt.int32
ALU = mybir.AluOpType
ACT = mybir.ActivationFunctionType
ENG = mybir.EngineType

NODES = 6250
EDGES = 206250
F = 128
P = 128
BLOCKS = -(-NODES // P)
LAST = NODES - (BLOCKS - 1) * P
TILES = -(-EDGES // P)
TAIL = EDGES - (TILES - 1) * P
STEPS = TILES + BLOCKS - 1
SG = -(-STEPS // P)
TROWS = SG * P
U = 20
QUARTER = U // 4
AHEAD = 8
POOL_WAITS = (0, 3, 5, 8, 10, 13, 15, 18)
LAG_T, LAG_PRE, LAG_RELU, LAG_SUM = 1, 2, 3, 4
BODIES = STEPS // U
SLOTS = 10
DSLOTS = 5
STAGED = 1 + 4 * BODIES
EPS = 1e-5
FAR = 1 << 20
LAYERS = 3
CHUNK = 4
CHUNKS = BLOCKS // CHUNK
C1 = CHUNKS + 1
WN = 2
WCOLS = WN * BLOCKS
WPB = P // WN
WINDOWS = BLOCKS * WPB
WG = -(-WINDOWS // P)
QW = 4
RING = 4
GROUPS = WPB // QW
BF16 = mybir.dt.bfloat16
NP = BLOCKS * P
RUN = P + 1
SPECIAL = TROWS
assert BODIES * U == STEPS and CHUNKS * CHUNK + 1 == BLOCKS and CHUNKS % 2 == 0 and TROWS >= TILES


def build_gnn(nc, x, src, dst, weight, attr128, attr2T, mW1, mb1, mW2, mb2, uW1, ub1, uW2, ub2, gamma, beta,
              W2g, bias2g, L3W1T, L3b1, L3g1, L3be1, L3W2T, L3b2, L3g2, L3be2, out):
    ctx = ExitStack()
    with ctx:
        def sb(name, shape, dt=FP32):
            return ctx.enter_context(nc.sbuf_tensor(name, shape, dt))

        def sem(name):
            return ctx.enter_context(nc.semaphore(name))

        src_rows = nc.dram_tensor("src_rows", (TROWS + 1, P), I32).ap()
        dst_rows = nc.dram_tensor("dst_rows", (TROWS + 1, P), I32).ap()
        w_rows = nc.dram_tensor("w_rows", (TROWS + 1, P), FP32).ap()
        dlast_tab = nc.dram_tensor("dlast_tab", (1, TROWS), FP32).ap()
        flag_tab = nc.dram_tensor("flag_tab", (1, 1), I32).ap()
        weight_mat = nc.dram_tensor("weight_mat", (BLOCKS, P, NP), FP32).ap()
        count_mat = nc.dram_tensor("count_mat", (BLOCKS, P, NP), BF16).ap()
        step_tab = nc.dram_tensor("step_tab", (2, AHEAD + TROWS), I32).ap()
        body_tab = nc.dram_tensor("body_tab", (2, BODIES + 1, 32), I32).ap()
        blk_row, start_row = body_tab[0], body_tab[1]
        tables = [nc.dram_tensor(f"table{k}", (NODES, F), FP32).ap() for k in range(2)]

        X = sb("X", [P, BLOCKS, F])
        H = sb("H", [P, BLOCKS, F])
        ACC = sb("ACC", [P, BLOCKS, 2 * F + 1])
        T1 = sb("T1", [P, BLOCKS, F])
        BIG = sb("BIG", [P, 2 * NP])
        HT = BIG[:, 0:NP]
        T2 = BIG[:, NP:2 * NP]

        G = T2[:, 0:SLOTS * F].rearrange("p (s f) -> p s f", f=F)
        HE0 = SLOTS * F
        HE = T2[:, HE0:HE0 + SLOTS * (2 * F + 1)].rearrange("p (s f) -> p s f", f=2 * F + 1)
        D0 = HE0 + SLOTS * (2 * F + 1)
        D = T2[:, D0:D0 + DSLOTS * P].rearrange("p (s f) -> p s f", f=P)
        DT = T2[:, D0 + DSLOTS * P:D0 + (DSLOTS + 2) * P].rearrange("p (s f) -> p s f", f=P)
        A2 = T2[0:2, D0 + (DSLOTS + 2) * P:D0 + (DSLOTS + 2 + SLOTS) * P].rearrange("p (s f) -> p s f", f=P)
        assert D0 + (DSLOTS + 2 + SLOTS) * P <= BLOCKS * F

        SRC = sb("SRC", [P, TROWS + U], mybir.dt.uint16)
        REL_WT = sb("REL_WT", [P, 2 * TROWS])
        REL = REL_WT[:, 0:TROWS]
        WT = REL_WT[:, TROWS:2 * TROWS]
        IDX = sb("IDX", [P, 4, QUARTER], I32)

        T1f = T1[:, :, :].rearrange("p b f -> p (b f)")
        ACCf = ACC[:, :, :].rearrange("p b f -> p (b f)")
        LO = T1f[:, 0:WINDOWS // 2].bitcast(BF16)
        CODE = T1f[:, WINDOWS // 2:WINDOWS].bitcast(BF16)
        WW = BIG[:, 2 * NP - WINDOWS:2 * NP]
        SR = ACCf[:, 0:WG * P].bitcast(I32)
        DR = ACCf[:, WG * P:WG * (P + RUN)].bitcast(I32)
        WR = ACCf[:, WG * (P + RUN):WG * (2 * P + RUN)]
        LOF = BIG[:, 0:WG * P]
        CODEF = BIG[:, WG * P:2 * WG * P]
        DLB = BIG[:, 0:TROWS]
        TJ = BIG[:, TROWS:2 * TROWS]
        TD = BIG[:, 2 * WG * P:3 * WG * P].bitcast(I32)
        TDF = BIG[:, WG * P:2 * WG * P]
        OA = BIG[:, NP:NP + RING * QW * P].rearrange("p (s c) -> p s c", c=P)
        OR = T1f[:, WINDOWS:WINDOWS + RING * QW * 2 * WCOLS].rearrange("p (s c) -> p s c", c=2 * WCOLS)
        assert WINDOWS + RING * QW * 2 * WCOLS <= NP and NP + RING * QW * P <= 2 * NP - WINDOWS
        WB = [ACCf[:, k * NP:(k + 1) * NP] for k in range(2)]
        CB = [HT.bitcast(BF16)[:, k * NP:(k + 1) * NP] for k in range(2)]
        WIN = [BIG[:, k * NP:(k + 1) * NP] for k in range(2)]
        HP = BIG[:, 0:3 * NP // 2].bitcast(BF16).rearrange("p (b k f) -> p b k f", k=3, f=F)
        CIN = [BIG[:, 3 * NP // 2:2 * NP].bitcast(BF16), REL_WT[:, 0:NP // 2].bitcast(BF16)]

        ident = sb("ident", [P, P])
        iota = sb("iota", [P, P])
        iotai = T1[:, 1, :].bitcast(I32)
        ones = sb("ones", [P, P])
        epsc = sb("epsc", [P, 1])
        mW1s = sb("mW1s", [P, 2 * F])
        mWcs = sb("mWcs", [2, F])
        mW2s = sb("mW2s", [P, F])
        uW1s = sb("uW1s", [P, 2, F])
        uW2s = sb("uW2s", [P, F])
        Wgs = sb("Wgs", [P, F])
        lw1 = sb("lw1", [P, F])
        lw2 = sb("lw2", [P, F])
        bc = {}
        for n in ("mb1", "mb2", "ub2", "gamma", "beta", "bias2g", "g2", "be2"):
            bc[n] = sb("bc_" + n, [P, F])
        ub1c = sb("ub1c", [P, 1])
        g1c = sb("g1c", [P, 1])
        be1c = sb("be1c", [P, 1])
        b1r = sb("b1r", [1, F])
        b2r = sb("b2r", [1, F])

        w2i = sb("w2i", [P, WG], I32)
        w2 = sb("w2", [P, WG])
        tw = sb("tw", [P, WG])
        twi = sb("twi", [P, WG], I32)
        wstart = sb("wstart", [P, WG], I32)
        over = sb("over", [P, WG])
        flag = sb("flag", [1, 1], I32)
        WS = sb("WS", [P, 2, WPB])
        thr = sb("thr", [P, BLOCKS - 1])
        thrb = sb("thrb", [P, BLOCKS - 1])
        dlasti = sb("dlasti", [P, SG], I32)
        dlast = sb("dlast", [P, SG])
        svec = sb("svec", [P, SG])
        sveci = sb("sveci", [P, SG], I32)
        bs = sb("bs", [P, SG])
        b128 = sb("b128", [P, SG])
        ts = sb("ts", [P, SG])
        es = sb("es", [P, SG])
        tsi = sb("tsi", [P, SG], I32)
        bsi = sb("bsi", [P, SG], I32)
        esi = sb("esi", [P, SG], I32)
        fill = T1[:, 0, :].bitcast(I32)
        ST = sb("ST", [P, BLOCKS, 6])
        MV = sb("MV", [P, BLOCKS, 2])
        rstd = sb("rstd", [P, BLOCKS])
        nmr = sb("nmr", [P, BLOCKS])
        rcnt = sb("rcnt", [P, BLOCKS])
        cn = sb("cn", [P, BLOCKS])

        RS = HT[:, 0:SG * P].bitcast(I32).rearrange("p (g c) -> p g c", c=P)
        RD = HT[:, SG * P:2 * SG * P].bitcast(I32).rearrange("p (g c) -> p g c", c=P)
        RW = HT[:, 2 * SG * P:3 * SG * P].rearrange("p (g c) -> p g c", c=P)
        RELF = T2[:, 0:SG * P].rearrange("p (g c) -> p g c", c=P)
        cmp = T2[:, 2 * SG * P:2 * SG * P + SG * (BLOCKS - 1)].rearrange("p (g b) -> p g b", b=BLOCKS - 1)
        SRCF = T2[:, SG * P:2 * SG * P].rearrange("p (g c) -> p g c", c=P)


        PS = [ctx.enter_context(nc.psum_tensor(f"ps{k}", [P, 512], FP32)) for k in range(8)]

        waits_passed = sem("waits_passed")
        fill_ready, consts, ident_zero = sem("fill_ready"), sem("consts"), sem("ident_zero")
        x_in, weights_in, layer_in = sem("x_in"), sem("weights_in"), sem("layer_weights_in")
        rows_in, tail_in, dlast_in = sem("edge_rows_in"), sem("tail_rows_in"), sem("dlast_in")
        cmp_ready, tau_ready, steps_ready = sem("cmp_ready"), sem("tau_ready"), sem("steps_ready")
        step_rows_out, regs_in = sem("step_rows_out"), sem("step_regs_in")
        rows_gathered, rel_ready = sem("step_rows_gathered"), sem("rel_rows_ready")
        turned, turn_copied = sem("step_rows_turned"), sem("step_table_copied")
        table_out = sem("gather_table_stored")
        staged, slots_free = sem("indices_staged"), sem("slots_free")
        onehot_ready, sum_ready, acc_ready = sem("onehot_ready"), sem("step_sum_ready"), sem("acc_initialised")
        pass_done = sem("pass_done")
        dt_ps, dt_sb, pre_ps = sem("onehotT_in_psum"), sem("onehotT_in_sbuf"), sem("edge_pre_in_psum")
        hid_ready, relu_done = sem("edge_hidden_ready"), sem("edge_relu_done")
        stats_done, aggr_done, std_ready, norm_ready = sem("stats_done"), sem("aggr_done"), sem("std_ready"), sem("norm_ready")
        h_ready, link_done, part_done = sem("h_ready"), sem("vector_link"), sem("vector_part_done")
        hT_ps, hT_sb = sem("hT_in_psum"), sem("hT_in_sbuf")
        p_ps, p_sb, q_sb = sem("pq_in_psum"), sem("p_in_sbuf"), sem("q_in_sbuf")
        s_ready, sT_ps, sT_sb = sem("mean_hidden_ready"), sem("mean_hiddenT_in_psum"), sem("mean_hiddenT_in_sbuf")
        agg_ps, agg_sb, aT_ps, aT_sb = sem("agg_in_psum"), sem("agg_in_sbuf"), sem("aggT_in_psum"), sem("aggT_in_sbuf")
        u_ps, u_sb, o_ps, o_sb = sem("updT_in_psum"), sem("updT_in_sbuf"), sem("upd_in_psum"), sem("upd_in_sbuf")
        sup_ps, sup_sb = sem("support_in_psum"), sem("support_in_sbuf")
        oT_ps, oT_sb, z_ps, z_sb = sem("outT_in_psum"), sem("outT_in_sbuf"), sem("z_in_psum"), sem("z_in_sbuf")
        zn_ready, zT_ps, zT_sb = sem("z_normed"), sem("zT_in_psum"), sem("zT_in_sbuf")
        y_ps, y_sb, yn_ready, gelu_done = sem("y_in_psum"), sem("y_in_sbuf"), sem("y_normed"), sem("layer_out_ready")
        layer_used, out_ready, out_stored = sem("layer_weights_used"), sem("out_ready"), sem("out_stored")
        dlast_out, dlb_in = sem("dlast_stored"), sem("dlast_rows_in")
        tw_ready, td_in, wstart_ready, wrows_in = sem("window_tile_ready"), sem("window_tile_in"), sem("window_start_ready"), sem("window_rows_in")
        wcode_ready, wturned, wcopied = sem("window_rows_ready"), sem("window_rows_turned"), sem("window_table_copied")
        over_ready, over_ps, flag_ready, flag_out = sem("overfull_ready"), sem("overfull_in_psum"), sem("flag_ready"), sem("flag_stored")
        hot_ready, hotw_ready = sem("window_onehots_ready"), sem("window_weighted_ready")
        group_ps, group_out = sem("group_in_psum"), sem("group_copied")
        mat_out = [sem(f"matrix_block_stored{k}") for k in range(2)]
        wblk_in = [sem(f"weight_block_in{k}") for k in range(2)]
        cblk_in = [sem(f"count_block_in{k}") for k in range(2)]
        wsum_ps, wsum_used, csum_ps, csum_used = sem("dense_sum_ready"), sem("dense_sum_used"), sem("count_sum_ready"), sem("count_sum_used")
        ws_ready = sem("block_weights_staged")
        csum_part = sem("count_sum_part_added")
        part1, part2, part3 = sem("h_part1_ready"), sem("h_rest1_ready"), sem("h_part2_ready")
        parts_ready = sem("h_parts_ready")
        general_sum, general_slots, general_hot, general_staged, general_init = (
            sem("general_sum_ready"), sem("general_slots_free"), sem("general_onehot_ready"), sem("general_indices_staged"), sem("general_pad"))
        general_out = sem("general_table_stored")
        general_gathered = [sem(f"general_gathered{k}") for k in range(SLOTS)]
        gathered = [sem(f"gathered{k}") for k in range(SLOTS)]
        attr_in = [sem(f"attr_in{k}") for k in range(SLOTS)]
        copied = (hT_sb, p_sb, q_sb, sT_sb, agg_sb, aT_sb, u_sb, o_sb, sup_sb, oT_sb, z_sb, zT_sb, y_sb)

        def chunks(eng, body):
            with eng.Fori(0, CHUNKS // 2) as i:
                body(i * 2, CHUNK, 0)
                body(i * 2 + 1, CHUNK, 1)
            body(CHUNKS, 1, 0)

        def chunks_of_pe(body):
            for c in range(C1):
                body(c, CHUNK if c < CHUNKS else 1, c % 2)

        def pipeline(eng, lag, values, position):
            got = values(0, U)
            for u in range(U):
                position(0, u, got, lambda part, u=u: u >= part)
            with eng.Fori(1, BODIES) as i:
                got = values(i, U)
                for u in range(U):
                    position(i, u, got, lambda part: True)
            if lag:
                got = values(BODIES, 0)
                for u in range(lag):
                    position(BODIES, u, got, lambda part, u=u: u < part)

        def wait_alone(eng, signal, value):
            eng.wait_ge(signal, value)
            eng.sem_inc(waits_passed, 1)

        def node_store(eng, dram, array, signal):
            eng.dma_start(dram[0:(BLOCKS - 1) * P, :].rearrange("(b p) f -> p b f", p=P),
                          array[:, 0:BLOCKS - 1, :]).then_inc(signal, 16)
            eng.dma_start(dram[(BLOCKS - 1) * P:NODES, :], array[0:LAST, BLOCKS - 1, :]).then_inc(signal, 16)

        def registers(engine, row, i, top, lag=0, n=U):
            _, values = nc.values_load_multi_w_load_instructions(
                row[bass.ds(i, 1), AHEAD - lag:AHEAD - lag + n], engines=[engine], min_val=0, max_val=top,
                skip_runtime_bounds_check_because="computed on the chip, at most the last block or tile")
            return values

        def blk(array, c, nb):
            return array[:, bass.ds(c * CHUNK, nb), :]

        def cols(array, c, nb):
            return array[:, bass.ds(c * CHUNK * P, nb * P)]

        def bank(pair, par, nb):
            return PS[pair + par][:, 0:nb * P]

        def bank3(pair, par, nb):
            return bank(pair, par, nb).rearrange("p (b f) -> p b f", f=F)

        def block_pairs(eng, body):
            with eng.Fori(0, BLOCKS // 2) as i:
                body(i * 2, 0, i)
                body(i * 2 + 1, 1, i)
            body(BLOCKS - 1, 0, BLOCKS // 2)

        def flag_of(engine, eng):
            eng.wait_ge(flag_out, 16)
            return nc.values_load(flag_tab[0:1, 0:1], engines=[engine], min_val=0, max_val=P * WG)

        def two_ways(eng, overfull, dense, general):
            with eng.If(overfull == 0):
                dense()
            with eng.Else():
                general()

        T2n = T2[:, :].rearrange("p (b f) -> p b f", f=F)
        ONE = 2 * F
        ROWS_PARTS = 13
        WCOPIES = 3 * -(-WG // 4)
        block = ctx.enter_context(nc.Block())

        @block.sync
        def _(sp):
            sp.dma_start(X[:, 0:BLOCKS - 1, :], x[0:(BLOCKS - 1) * P, :].rearrange("(b p) f -> p b f", p=P)).then_inc(x_in, 16)
            sp.wait_ge(acc_ready, 1)
            sp.dma_start(X[0:LAST, BLOCKS - 1, :], x[(BLOCKS - 1) * P:NODES, :]).then_inc(x_in, 16)
            n0 = (TILES - 1) * P
            for rows, flat in ((src_rows, src), (dst_rows, dst), (w_rows, weight)):
                sp.dma_start(rows[0:TILES - 1, :].rearrange("t c -> (t c)").rearrange("(a b) -> a b", a=16),
                             flat[0:n0].rearrange("(a b) -> a b", a=16)).then_inc(rows_in, 16)
                sp.dma_start(rows[TILES - 1:TILES, 0:TAIL], flat[n0:EDGES].rearrange("(a b) -> a b", a=1)).then_inc(rows_in, 16)
                sp.dma_start(rows[SPECIAL:SPECIAL + 1, :], flat[EDGES - P:EDGES].rearrange("(a b) -> a b", a=1)).then_inc(tail_in, 16)
            sp.wait_ge(fill_ready, 3)
            for rows, pad in ((dst_rows, fill), (src_rows, iotai), (w_rows, ones)):
                sp.dma_start(rows[TILES:TROWS, :], pad[0:TROWS - TILES, :]).then_inc(rows_in, 16)
                sp.dma_start(rows[TILES - 1:TILES, TAIL:P], pad[0:1, TAIL:P]).then_inc(rows_in, 16)
            sp.wait_ge(tail_in, 48)
            sp.dma_start(dst_rows[SPECIAL:SPECIAL + 1, 0:P - TAIL], fill[0:1, 0:P - TAIL]).then_inc(rows_in, 16)
            sp.wait_ge(rows_in, 16 * ROWS_PARTS)
            full = (TILES - 1) // P
            sp.dma_start(dlasti[:, 0:full], dst_rows[0:full * P, P - 1:P].rearrange("(g p) c -> p (g c)", p=P),
                         allow_slow_non_contiguous=True).then_inc(dlast_in, 16)
            sp.dma_start(dlasti[0:TILES - 1 - full * P, full:full + 1], dst_rows[full * P:TILES - 1, P - 1:P],
                         allow_slow_non_contiguous=True).then_inc(dlast_in, 16)
            sp.wait_ge(over_ready, 1)
            sp.dma_start(dlast_tab[0, :].rearrange("(g p) -> p g", p=P), dlast[:, :], allow_slow_non_contiguous=True).then_inc(dlast_out, 16)
            for to, of in ((mW1s[:, 0:F], mW1[0:F, :]), (mW1s[:, F:2 * F], mW1[F:2 * F, :]), (mWcs[:, :], mW1[2 * F:2 * F + 2, :]),
                           (mW2s[:, :], mW2), (uW1s[:, 0, :], uW1[0:F, :]), (uW1s[:, 1, :], uW1[F:2 * F, :]), (uW2s[:, :], uW2),
                           (Wgs[:, :], W2g), (bc["mb1"][:, :], mb1.partition_broadcast(P)), (bc["mb2"][:, :], mb2.partition_broadcast(P)),
                           (bc["ub2"][:, :], ub2.partition_broadcast(P)), (bc["gamma"][:, :], gamma.partition_broadcast(P)),
                           (bc["beta"][:, :], beta.partition_broadcast(P)), (bc["bias2g"][:, :], bias2g.partition_broadcast(P)),
                           (ub1c[:, :], ub1.rearrange("(f a) -> f a", a=1))):
                sp.dma_start(to, of).then_inc(weights_in, 16)
            sp.dma_start(step_tab[:, 0:AHEAD], iotai[0:2, 0:AHEAD]).then_inc(step_rows_out, 16)
            sp.wait_ge(steps_ready, 1)
            sp.dma_start(step_tab[0, AHEAD:].rearrange("(g p) -> p g", p=P), bsi[:, :], allow_slow_non_contiguous=True).then_inc(step_rows_out, 16)
            sp.dma_start(step_tab[1, AHEAD:].rearrange("(g p) -> p g", p=P), esi[:, :], allow_slow_non_contiguous=True).then_inc(step_rows_out, 16)
            sp.wait_ge(step_rows_out, 48)
            for k in range(2):
                sp.dma_start(body_tab[k, 0:BODIES, 0:AHEAD], step_tab[k, 0:STEPS].rearrange("(i u) -> i u", u=U)[:, 0:AHEAD]).then_inc(regs_in, 16)
                sp.dma_start(body_tab[k, 0:BODIES, AHEAD:AHEAD + U], step_tab[k, AHEAD:AHEAD + STEPS].rearrange("(i u) -> i u", u=U)).then_inc(regs_in, 16)
                sp.dma_start(body_tab[k, BODIES:BODIES + 1, 0:AHEAD], step_tab[k:k + 1, STEPS:STEPS + AHEAD]).then_inc(regs_in, 16)
            sp.wait_ge(dlast_out, 16)
            sp.wait_ge(turn_copied, 3 * SG)
            sp.dma_start(DLB, dlast_tab.broadcast_to([P, TROWS])).then_inc(dlb_in, 16)
            sp.wait_ge(flag_ready, 1)
            sp.dma_start(flag_tab, flag[:, :]).then_inc(flag_out, 16)
            overfull = flag_of(ENG.SP, sp)

            def store_block(b, par, i):
                sp.wait_ge(group_out, (b + 1) * GROUPS + 4)
                sp.dma_start(weight_mat[b, :, :], WB[par]).then_inc(mat_out[par], 16)
                sp.dma_start(count_mat[b, :, :], CB[par]).then_inc(mat_out[par], 16)
            block_pairs(sp, store_block)
            sp.wait_ge(mat_out[0], 32 * 25)
            sp.wait_ge(mat_out[1], 32 * 24)

            def load_weights(base):
                def body(b, par, i):
                    sp.wait_ge(wsum_ps, base * BLOCKS + b + 1)
                    sp.dma_start(WIN[par], weight_mat[b, :, :]).then_inc(wblk_in[par], 16)
                block_pairs(sp, body)

            def load_counts(l):
                sp.wait_ge(wsum_used, 2 * BLOCKS + 2)

                def body(b, par, i):
                    sp.wait_ge(csum_ps, l * BLOCKS + b + 1)
                    sp.dma_start(CIN[par], count_mat[b, :, :]).then_inc(cblk_in[par], 16)
                block_pairs(sp, body)

            def general_table(array, signal, count):
                wait_alone(sp, signal, count)
                node_store(sp, tables[0], array, general_out)

            sp.wait_ge(h_ready, C1)
            two_ways(sp, overfull, lambda: load_weights(0), lambda: general_table(H, h_ready, C1))
            sp.wait_ge(p_sb, C1 + 1)
            node_store(sp, tables[1], T2n, table_out)
            sp.wait_ge(regs_in, 96)
            sp.wait_ge(acc_ready, 2)
            with sp.Fori(0, BODIES) as i:
                first = registers(ENG.SP, start_row, i, EDGES - P)
                for u in range(U):
                    k = u % SLOTS
                    sp.wait_ge(slots_free, i * U + (u + 1))
                    sp.dma_start(HE[:, k, F:2 * F], attr128[bass.ds(first[u], P), :]).then_inc(attr_in[k], 16)
                    sp.dma_start(A2[:, k, :], attr2T[:, bass.ds(first[u], P)]).then_inc(attr_in[k], 16)
            sp.wait_ge(sup_sb, C1 + 1)
            two_ways(sp, overfull, lambda: load_weights(1), lambda: general_table(T1, sup_sb, C1 + 1))
            with sp.Fori(0, LAYERS) as l:
                wait_alone(sp, layer_used, l)
                wait_alone(sp, gelu_done, l * C1)
                for to, of in ((lw1[:, :], L3W1T[bass.ds(l * F, F), :]), (lw2[:, :], L3W2T[bass.ds(l * F, F), :]),
                               (b1r[:, :], L3b1[bass.ds(l, 1), :]), (b2r[:, :], L3b2[bass.ds(l, 1), :]),
                               (bc["g2"][:, :], L3g2[bass.ds(l, 1), :].broadcast_to([P, F])),
                               (bc["be2"][:, :], L3be2[bass.ds(l, 1), :].broadcast_to([P, F])),
                               (g1c[:, :], L3g1[bass.ds(l * F, F), :]), (be1c[:, :], L3be1[bass.ds(l * F, F), :])):
                    sp.dma_start(to, of).then_inc(layer_in, 16)
                sp.wait_ge(slots_free, STEPS + SLOTS)
                sp.wait_ge(h_ready, 4 * C1)
                two_ways(sp, overfull, lambda: load_counts(l), lambda: general_table(H, gelu_done, l * C1))
            sp.wait_ge(out_ready, 1)
            node_store(sp, out, X, out_stored)
            sp.wait_ge(out_stored, 32)

        @block.gpsimd
        def _(pool):
            pool.memset(fill[:, :], FAR).then_inc(fill_ready, 1)
            pool.iota(iotai[:, :], pattern=[[1, P]], base=0, channel_multiplier=0).then_inc(fill_ready, 1)
            pool.memset(ones[:, :], 1.0).then_inc(fill_ready, 1)
            pool.iota(sveci[:, :], pattern=[[P, SG]], base=0, channel_multiplier=1).then_inc(consts, 1)
            pool.memset(ident[:, :], 0.0).then_inc(ident_zero, 1)
            pool.wait_ge(ident_zero, 1)
            pool.affine_select(out=ident[:, :], in_=ident[:, :], compare_op=ALU.not_equal, fill=1.0, base=0,
                               pattern=[[-1, P]], channel_multiplier=1).then_inc(consts, 1)
            pool.memset(epsc[:, :], EPS).then_inc(consts, 1)
            pool.memset(SRC[:, TROWS:TROWS + U], 0).then_inc(consts, 1)
            pool.iota(w2i[:, :], pattern=[[WN * P, WG]], base=0, channel_multiplier=WN).then_inc(consts, 1)
            pool.wait_ge(rows_in, 16 * ROWS_PARTS)
            pool.wait_ge(steps_ready, 1)
            for g in range(SG):
                for rows, to in ((src_rows, RS), (dst_rows, RD), (w_rows, RW)):
                    pool.indirect_dma_start(to[:, g, :], None, rows, bass.IndirectOffsetOnAxis(ap=tsi[:, g:g + 1], axis=0)
                                            ).then_inc(rows_gathered, 16)
            pool.wait_ge(tw_ready, 1)
            for g in range(WG):
                pool.indirect_dma_start(TD[:, g * P:(g + 1) * P], None, dst_rows, bass.IndirectOffsetOnAxis(ap=twi[:, g:g + 1], axis=0)).then_inc(td_in, 16)
            pool.wait_ge(wstart_ready, 1)
            for g in range(WG):
                for rows, to, n in ((src_rows, SR, P), (dst_rows, DR, RUN), (w_rows, WR, P)):
                    pool.indirect_dma_start(to[:, g * n:(g + 1) * n], None, rows.rearrange("t (c a) -> (t c) a", a=1),
                                            bass.IndirectOffsetOnAxis(ap=wstart[:, g:g + 1], axis=0)).then_inc(wrows_in, 16)
            pool.sem_inc(slots_free, SLOTS)
            pool.sem_inc(general_slots, SLOTS)
            pool.wait_ge(wcopied, WCOPIES)

            def weighted(b, par, i):
                pool.tensor_copy(WS[:, par, :], WW[:, bass.ds(b * WPB, WPB)]).then_inc(ws_ready, 1)
                wait_alone(pool, ws_ready, b + 1)
                for q in range(GROUPS):
                    wait_alone(pool, hot_ready, b * GROUPS + q + 1)
                    for j in range(QW):
                        k = q % RING * QW + j
                        last = pool.tensor_scalar(OR[:, k, WCOLS:2 * WCOLS], OR[:, k, 0:WCOLS], WS[:, par, q * QW + j:q * QW + j + 1], 1.0, ALU.mult, ALU.mult)
                    last.then_inc(hotw_ready, 1)
            block_pairs(pool, weighted)

            def stage(col, q, staged):
                pool.tensor_copy(IDX[:, q, :], SRC[:, bass.ds(col, QUARTER)]).then_inc(staged, 1)

            def gathers(table, at, staged, slots, done):
                stage(0, 0, staged)
                with pool.Fori(0, BODIES) as i:
                    for q in range(4):
                        stage(i * U + (q + 1) * QUARTER, (q + 1) % 4, staged)
                        pool.wait_ge(staged, at * STAGED + (i * 4 + q + 1))
                        for u in range(q * QUARTER, (q + 1) * QUARTER):
                            if u in POOL_WAITS:
                                n = next((w for w in POOL_WAITS if w > u), U) - u
                                wait_alone(pool, slots, at * STEPS + (i * U + u + n))
                            pool.indirect_dma_start(G[:, u % SLOTS, :], None, table,
                                                    bass.IndirectOffsetOnAxis(ap=IDX[:, q, u % QUARTER:u % QUARTER + 1], axis=0)
                                                    ).then_inc(done[u % SLOTS], 16)
                wait_alone(pool, staged, (at + 1) * STAGED)

            def general(at):
                wait_alone(pool, general_out, (at + 1) * 32)
                gathers(tables[0], at, general_staged, general_slots, general_gathered)

            nothing = lambda: pool.sem_inc(waits_passed, 1)
            overfull = flag_of(ENG.Pool, pool)
            two_ways(pool, overfull, nothing, lambda: general(0))
            pool.wait_ge(table_out, 32)
            gathers(tables[1], 0, staged, slots_free, gathered)
            two_ways(pool, overfull, nothing, lambda: general(1))
            with pool.Fori(0, LAYERS) as l:
                two_ways(pool, overfull, nothing, lambda: general(l + 2))

        @block.scalar
        def _(act):
            for s in copied:
                if s not in (q_sb, agg_sb, o_sb, sup_sb):
                    act.sem_inc(s, 1)

            def stds(n):
                act.wait_ge(aggr_done, n * 6)
                act.activation(rstd[:, :], MV[:, :, 1], ACT.Sqrt, bias=epsc[:, 0:1]).then_inc(std_ready, 1)

            def relu_norm(n):
                act.wait_ge(norm_ready, n)

                def body(c, nb, par):
                    for j in range(nb):
                        b = c * CHUNK + j
                        last = act.activation(H[:, b, :], X[:, b, :], ACT.Relu, bias=nmr[:, bass.ds(b, 1)], scale=rstd[:, bass.ds(b, 1)])
                    last.then_inc(h_ready, 1)
                chunks(act, body)

            def copy_out(ready, done, to, pair, func=ACT.Copy, base=0, as_blocks=False, **kw):
                def body(c, nb, par):
                    act.wait_ge(ready, base + c + 1)
                    if as_blocks:
                        act.activation(blk(to, c, nb), bank3(pair, par, nb), func, **kw).then_inc(done, 1)
                    else:
                        act.activation(cols(to, c, nb), bank(pair, par, nb), func, **kw).then_inc(done, 1)
                chunks(act, body)

            act.wait_ge(consts, 5)
            stds(1)
            relu_norm(1)
            for k in range(3 * SG):
                act.wait_ge(turned, k + 1)
                act.activation((SRC, REL, WT)[k % 3][:, k // 3 * P:(k // 3 + 1) * P], PS[k % 4][:, 0:P], ACT.Copy).then_inc(turn_copied, 1)
            for k in range(WCOPIES):
                which, n = k % 3, min(4 * P, WINDOWS - k // 3 * 4 * P)
                act.wait_ge(wturned, k + 1)
                act.activation((LO, CODE, WW)[which][:, k // 3 * 4 * P:k // 3 * 4 * P + n], PS[k % 4][:, 0:n], ACT.Copy).then_inc(wcopied, 1)
            act.sem_inc(group_out, 4)
            act.sem_inc(wsum_used, 2)
            act.sem_inc(csum_used, 2)

            def group_copies(b, par, i):
                act.wait_ge(mat_out[par], i * 32)
                for q in range(GROUPS):
                    act.wait_ge(group_ps, b * GROUPS + q + 1 + RING)
                    for pair, to in ((q % 4, CB[par]), (4 + q % 4, WB[par])):
                        last = act.activation(
                            to.rearrange("p (h d) -> p h d", d=P)[:, :, q * QW * WN:(q + 1) * QW * WN].rearrange("p h (w j) -> p h w j", j=WN),
                            PS[pair][:, 0:QW * WCOLS].rearrange("p (w h j) -> p h w j", w=QW, j=WN), ACT.Copy)
                    last.then_inc(group_out, 1)
            act.wait_ge(flag_out, 16)
            block_pairs(act, group_copies)
            stds(2)
            relu_norm(2)
            copy_out(hT_ps, hT_sb, HT, 0)
            copy_out(p_ps, p_sb, T2n, 2, as_blocks=True)
            act.wait_ge(table_out, 32)
            overfull = flag_of(ENG.Activation, act)

            def act_step(i, u, _, on):
                if on(LAG_T):
                    v = (u - LAG_T) % U
                    act.wait_ge(dt_ps, i * U + (u - LAG_T + 1))
                    act.activation(DT[:, v % 2, :], PS[v % 2][:, 0:P], ACT.Copy).then_inc(dt_sb, 1)
                if on(LAG_RELU):
                    k = (u - LAG_RELU) % SLOTS
                    act.wait_ge(hid_ready, i * U + (u - LAG_RELU + 1))
                    act.activation(HE[:, k, 0:F], HE[:, k, 0:F], ACT.Relu).then_inc(relu_done, 1)
            pipeline(act, LAG_RELU, lambda i, n: None, act_step)
            copy_out(sT_ps, sT_sb, T2, 0)
            copy_out(aT_ps, aT_sb, T2, 4)
            copy_out(u_ps, u_sb, T2, 6, func=ACT.Relu, bias=ub1c[:, 0:1])
            stds(3)
            stds(4)
            relu_norm(4)
            copy_out(hT_ps, hT_sb, HT, 0, base=C1)
            stds(5)
            relu_norm(5)
            def parts(l):
                def first(c, nb, par):
                    act.activation(HP[:, bass.ds(c * CHUNK, nb), 0, :], blk(H, c, nb), ACT.Copy).then_inc(part1, 1)

                def second(c, nb, par):
                    act.wait_ge(part2, l * C1 + c + 1)
                    act.activation(HP[:, bass.ds(c * CHUNK, nb), 1, :], ACC[:, bass.ds(c * CHUNK, nb), 0:F], ACT.Copy).then_inc(part3, 1)
                act.wait_ge(h_ready, 4 * C1)
                wait_alone(act, gelu_done, l * C1)
                chunks(act, first)
                chunks(act, second)

            with act.Fori(0, LAYERS) as l:
                two_ways(act, overfull, lambda: parts(l), lambda: act.sem_inc(waits_passed, 1))
                copy_out(oT_ps, oT_sb, HT, 0, base=l * C1)
                copy_out(z_ps, z_sb, T1, 2, base=l * C1, as_blocks=True)
                stds(l * 2 + 6)
                act.wait_ge(layer_in, l * 128 + 128)
                copy_out(zT_ps, zT_sb, HT, 4, func=ACT.Gelu, base=l * C1, bias=be1c[:, 0:1], scale=g1c[:, 0:1])
                copy_out(y_ps, y_sb, T1, 6, base=l * C1, as_blocks=True)
                stds(l * 2 + 7)

                def layer_out(c, nb, par):
                    act.wait_ge(yn_ready, l * C1 + c + 1)
                    act.activation(blk(H, c, nb), blk(T1, c, nb), ACT.Gelu).then_inc(gelu_done, 1)
                chunks(act, layer_out)

        @block.tensor
        def _(pe):
            pe.wait_ge(consts, 5)
            pe.wait_ge(fill_ready, 3)
            for g in range(SG):
                pe.wait_ge(cmp_ready, g + 1)
                mm = pe.matmul(PS[7][:, 0:BLOCKS - 1], ones[:, :], cmp[:, g, :], start=(g == 0), stop=(g == SG - 1))
            mm.then_inc(tau_ready, 1)
            for k in range(3 * SG):
                pe.wait_ge(rel_ready, k // 3 * 2 + min(k % 3 + 1, 2))
                if k >= 4:
                    pe.wait_ge(turn_copied, k - 3)
                pe.transpose(PS[k % 4][:, 0:P], (SRCF, RELF, RW)[k % 3][:, k // 3, :], ident[:, :]).then_inc(turned, 1)

            for k in range(WCOPIES):
                pe.wait_ge(wcode_ready, k % 3 + 1)
                pe.wait_ge(turn_copied, 3 * SG)
                if k >= 4:
                    pe.wait_ge(wcopied, k - 3)
                for g in range(k // 3 * 4, min(k // 3 * 4 + 4, WG)):
                    mm = pe.transpose(PS[k % 4][:, g % 4 * P:(g % 4 + 1) * P], (LOF, CODEF, WR)[k % 3][:, g * P:(g + 1) * P], ident[:, :])
                mm.then_inc(wturned, 1)
            pe.wait_ge(over_ready, 2)
            pe.matmul(PS[7][0:1, 0:WG], ones[:, 0:1], over[:, :], start=True, stop=True).then_inc(over_ps, 1)

            pe.wait_ge(flag_out, 16)
            pe.wait_ge(wcopied, WCOPIES)
            pe.sem_inc(group_ps, RING)

            def windows(b, par, i):
                for q in range(GROUPS):
                    pe.wait_ge(hot_ready, b * GROUPS + q + 1)
                    pe.wait_ge(hotw_ready, b * GROUPS + q + 1)
                    pe.wait_ge(group_out, b * GROUPS + q + 1)
                    for j in range(QW):
                        k = q % RING * QW + j
                        pe.matmul(PS[q % 4][:, j * WCOLS:(j + 1) * WCOLS], OA[:, k, :], OR[:, k, 0:WCOLS], start=True, stop=True)
                        mm = pe.matmul(PS[4 + q % 4][:, j * WCOLS:(j + 1) * WCOLS], OA[:, k, :], OR[:, k, WCOLS:2 * WCOLS], start=True, stop=True)
                    mm.then_inc(group_ps, 1)
            block_pairs(pe, windows)
            pe.wait_ge(group_out, BLOCKS * GROUPS + 4)
            overfull = flag_of(ENG.PE, pe)

            def weight_products(base, array):
                def body(b, par, i):
                    pe.wait_ge(wblk_in[par], (i + 1) * 16 + base * 16 * (BLOCKS // 2 + 1 - par))
                    pe.wait_ge(wsum_used, base * BLOCKS + b + 1)
                    for h in range(BLOCKS):
                        mm = pe.matmul(PS[par][:, 0:F], WIN[par][:, h * P:(h + 1) * P], array[:, h, :], start=(h == 0), stop=(h == BLOCKS - 1))
                    mm.then_inc(wsum_ps, 1)
                block_pairs(pe, body)

            def count_products(l):
                def body(b, par, i):
                    pe.wait_ge(cblk_in[par], (i + 1) * 16 + l * (16 * (BLOCKS // 2 + 1 - par)))
                    pe.wait_ge(csum_used, l * BLOCKS + b + 1)
                    for h in range(BLOCKS):
                        mm = pe.matmul(PS[par][:, 0:3 * F], CIN[par][:, h * P:(h + 1) * P], HP[:, h, :, :].rearrange("p k f -> p (k f)"),
                                       start=(h == 0), stop=(h == BLOCKS - 1))
                    mm.then_inc(csum_ps, 1)
                wait_alone(pe, parts_ready, (l + 1) * C1)
                block_pairs(pe, body)

            def step_sums(at):
                with pe.Fori(0, BODIES) as i:
                    for u in range(U):
                        pe.wait_ge(general_gathered[u % SLOTS], (at * BODIES + i) * 32 + 16 * (u // SLOTS + 1))
                        pe.wait_ge(general_hot, at * STEPS + (i * U + u + 1))
                        pe.matmul(PS[4 + u % 4][:, 0:F], D[:, u % 4, :], G[:, u % SLOTS, :], start=True, stop=True).then_inc(general_sum, 1)

            def turn(ready, offset, ps, sb_, array, pair, base=0):
                def body(c, nb, par):
                    pe.wait_ge(ready, c + offset)
                    pe.wait_ge(sb_, base + c)
                    for j in range(nb):
                        mm = pe.transpose(PS[pair + par][:, j * P:(j + 1) * P], array[:, c * CHUNK + j, :], ident[:, :])
                    mm.then_inc(ps, 1)
                chunks_of_pe(body)

            def times(ready, offset, ps, sb_, arrayT, weights, pair, base=0, bias=None):
                def body(c, nb, par):
                    pe.wait_ge(ready, c + offset)
                    pe.wait_ge(sb_, base + c)
                    for j in range(nb):
                        to = PS[pair + par][:, j * P:(j + 1) * P]
                        if bias is not None:
                            pe.matmul(to, ones[0:1, :], bias, start=True, stop=False)
                        mm = pe.matmul(to, arrayT[:, bass.ds((c * CHUNK + j) * P, P)], weights, start=bias is None, stop=True)
                    mm.then_inc(ps, 1)
                chunks_of_pe(body)

            pe.wait_ge(weights_in, 16 * 15)
            pe.sem_inc(wsum_ps, 2)
            pe.sem_inc(csum_ps, 2)
            pe.wait_ge(h_ready, C1)
            two_ways(pe, overfull, lambda: weight_products(0, H), lambda: step_sums(0))
            turn(h_ready, C1 + 1, hT_ps, hT_sb, H, 0)

            def pq(c, nb, par):
                pe.wait_ge(hT_sb, c + 2)
                pe.wait_ge(p_sb, c)
                pe.wait_ge(q_sb, c)
                for j in range(nb):
                    lhs = HT[:, bass.ds((c * CHUNK + j) * P, P)]
                    pe.matmul(PS[2 + par][:, j * P:(j + 1) * P], lhs, mW1s[:, 0:F], start=True, stop=True)
                    mm = pe.matmul(PS[4 + par][:, j * P:(j + 1) * P], lhs, mW1s[:, F:2 * F], start=True, stop=True)
                mm.then_inc(p_ps, 1)
            chunks_of_pe(pq)
            pe.wait_ge(regs_in, 96)
            pe.wait_ge(q_sb, C1 + 1)

            def pe_step(i, u, b, on):
                if on(LAG_T):
                    v = (u - LAG_T) % U
                    pe.wait_ge(onehot_ready, i * U + (u - LAG_T + 1))
                    pe.transpose(PS[v % 2][:, 0:P], D[:, v % DSLOTS, :], ident[:, :]).then_inc(dt_ps, 1)
                if on(LAG_PRE):
                    v = (u - LAG_PRE) % U
                    pe.wait_ge(dt_sb, i * U + (u - LAG_PRE + 1))
                    if on(LAG_PRE + 2):
                        pe.wait_ge(hid_ready, i * U + (u - LAG_PRE - 1))
                    pe.wait_ge(attr_in[v % SLOTS], i * 64 + 32 * ((u - LAG_PRE) // SLOTS + 1))
                    pe.matmul(PS[2 + v % 2][:, 0:F], DT[:, v % 2, :], T1[:, b[u], :], start=True, stop=False)
                    pe.matmul(PS[2 + v % 2][:, 0:F], A2[:, v % SLOTS, :], mWcs[:, :], start=False, stop=True).then_inc(pre_ps, 1)
                if on(LAG_SUM):
                    v = (u - LAG_SUM) % U
                    pe.wait_ge(relu_done, i * U + (u - LAG_SUM + 1))
                    pe.matmul(PS[4 + v % 4][:, 0:2 * F + 1], D[:, v % DSLOTS, :], HE[:, v % SLOTS, :], start=True, stop=True).then_inc(sum_ready, 1)
            pipeline(pe, LAG_SUM, lambda i, n: registers(ENG.PE, blk_row, i, BLOCKS - 1, LAG_PRE, n or LAG_PRE), pe_step)
            turn(s_ready, 1, sT_ps, sT_sb, ACC[:, :, 0:F], 0)
            times(sT_sb, 2, agg_ps, agg_sb, T2, mW2s[:, :], 2)
            turn(agg_sb, 2, aT_ps, aT_sb, ACC[:, :, 0:F], 4)

            def update(c, nb, par):
                pe.wait_ge(aT_sb, c + 2)
                pe.wait_ge(u_sb, c)
                pe.matmul(bank(6, par, nb), uW1s[:, 0, :], cols(HT, c, nb), start=True, stop=False)
                pe.matmul(bank(6, par, nb), uW1s[:, 1, :], cols(T2, c, nb), start=False, stop=True).then_inc(u_ps, 1)
            chunks_of_pe(update)
            times(u_sb, 2, o_ps, o_sb, T2, uW2s[:, :], 0)
            turn(h_ready, 2 * C1 + 1, hT_ps, hT_sb, H, 0, base=C1)
            times(hT_sb, C1 + 2, sup_ps, sup_sb, HT, Wgs[:, :], 2)
            pe.wait_ge(sup_sb, C1 + 1)
            two_ways(pe, overfull, lambda: weight_products(1, T1), lambda: step_sums(1))
            with pe.Fori(0, LAYERS) as l:
                two_ways(pe, overfull, lambda: count_products(l), lambda: step_sums(l + 2))
                pe.wait_ge(layer_in, l * 128 + 128)
                turn(pass_done, l * C1 + 1, oT_ps, oT_sb, T1, 0, base=l * C1)
                times(oT_sb, l * C1 + 2, z_ps, z_sb, HT, lw1[:, :], 2, base=l * C1, bias=b1r[:, :])
                turn(zn_ready, l * C1 + 1, zT_ps, zT_sb, T1, 4, base=l * C1)
                times(zT_sb, l * C1 + 2, y_ps, y_sb, HT, lw2[:, :], 6, base=l * C1, bias=b2r[:, :])

        @block.vector
        def _(dve):
            links = [0]

            def link(ins):
                ins.then_inc(link_done, 1)
                links[0] += 1
                dve.wait_ge(link_done, links[0])

            for s in (q_sb, agg_sb, o_sb, sup_sb):
                dve.sem_inc(s, 1)

            def per_block(body):
                with dve.Fori(0, BLOCKS // 7) as i:
                    for j in range(7):
                        body(i * 7 + j)

            def statistics(array, n, wait=None):
                if wait is None:
                    per_block(lambda b: dve.bn_stats(ST[:, b, :], array[:, b, :]).then_inc(stats_done, 1))
                wait_alone(dve, stats_done, n * BLOCKS)
                steps = (lambda: dve.tensor_tensor(MV[:, :, 0], ST[:, :, 1], ST[:, :, 4], ALU.add),
                         lambda: dve.tensor_tensor(MV[:, :, 1], ST[:, :, 1], ST[:, :, 4], ALU.subtract),
                         lambda: dve.tensor_tensor(ST[:, :, 2], ST[:, :, 2], ST[:, :, 5], ALU.add),
                         lambda: dve.scalar_tensor_tensor(MV[:, :, 1], MV[:, :, 1], 0.25, MV[:, :, 1], ALU.mult, ALU.mult),
                         lambda: dve.tensor_scalar(MV[:, :, 0], MV[:, :, 0], 0.5, None, ALU.mult),
                         lambda: dve.scalar_tensor_tensor(MV[:, :, 1], ST[:, :, 2], 1.0 / F, MV[:, :, 1], ALU.mult, ALU.add))
                for k, step in enumerate(steps):
                    step().then_inc(aggr_done, 1)
                    dve.wait_ge(aggr_done, (n - 1) * len(steps) + (k + 1))

            def rstds(n):
                dve.wait_ge(std_ready, n)
                dve.reciprocal(rstd[:, :], rstd[:, :]).then_inc(part_done, 1)
                dve.wait_ge(part_done, n)
                dve.scalar_tensor_tensor(nmr[:, :], MV[:, :, 0], -1.0, rstd[:, :], ALU.mult, ALU.mult).then_inc(norm_ready, 1)

            link(dve.memset(X[:, BLOCKS - 1, :], 0.0))
            dve.sem_inc(acc_ready, 1)
            dve.wait_ge(consts, 5)
            link(dve.tensor_copy(iota[:, :], iotai[:, :]))
            link(dve.tensor_copy(svec[:, :], sveci[:, :]))
            link(dve.tensor_copy(w2[:, :], w2i[:, :]))
            link(dve.memset(dlast[:, :], float(FAR)))
            link(dve.tensor_scalar(thrb[:, :], iota[:, 0:BLOCKS - 1], 1.0, float(P), ALU.add, ALU.mult))
            dve.wait_ge(dlast_in, 32)
            full = (TILES - 1) // P
            dve.tensor_copy(dlast[:, 0:full], dlasti[:, 0:full])
            link(dve.tensor_copy(dlast[0:TILES - 1 - full * P, full:full + 1], dlasti[0:TILES - 1 - full * P, full:full + 1]))
            dve.sem_inc(over_ready, 1)
            for g in range(SG):
                dve.tensor_scalar(cmp[:, g, :], thrb[:, :], dlast[:, g:g + 1], None, ALU.is_gt).then_inc(cmp_ready, 1)
            dve.wait_ge(tau_ready, 1)
            link(dve.scalar_tensor_tensor(thr[:, :], iota[:, 0:BLOCKS - 1], 1.0, PS[7][:, 0:BLOCKS - 1], ALU.add, ALU.add))
            for g in range(SG):
                last = dve.tensor_scalar(cmp[:, g, :], thr[:, :], svec[:, g:g + 1], None, ALU.is_le, ALU.add, accum_out=bs[:, g:g + 1])
            link(last)
            link(dve.tensor_tensor(ts[:, :], svec[:, :], bs[:, :], ALU.subtract))
            dve.tensor_scalar(es[:, :], ts[:, :], float(P), float(EDGES - P), ALU.mult, ALU.min)
            link(dve.tensor_scalar(b128[:, :], ts[:, :], float(TILES - 1), float(SPECIAL - TILES + 1), ALU.is_equal, ALU.mult))
            link(dve.tensor_tensor(b128[:, :], b128[:, :], ts[:, :], ALU.add))
            link(dve.tensor_copy(tsi[:, :], b128[:, :]))
            dve.tensor_scalar(b128[:, :], bs[:, :], float(P), None, ALU.mult)
            link(dve.tensor_copy(bsi[:, :], bs[:, :]))
            dve.tensor_copy(esi[:, :], es[:, :]).then_inc(steps_ready, 1)
            dve.wait_ge(x_in, 32)
            statistics(X, 1)
            rstds(1)
            dve.wait_ge(rows_gathered, 16 * 3 * SG)
            for g in range(SG):
                dve.tensor_copy(SRCF[:, g, :], RS[:, g, :]).then_inc(rel_ready, 1)
                dve.tensor_scalar(RELF[:, g, :], RD[:, g, :], b128[:, g:g + 1], None, ALU.subtract).then_inc(rel_ready, 1)
            dve.wait_ge(turn_copied, 3 * SG)
            dve.wait_ge(regs_in, 96)

            dve.wait_ge(dlb_in, 16)
            for g in range(WG):
                link(dve.tensor_scalar(TJ, DLB, w2[:, g:g + 1], None, ALU.is_lt, ALU.add, accum_out=tw[:, g:g + 1]))
            dve.tensor_copy(twi[:, :], tw[:, :]).then_inc(tw_ready, 1)
            dve.wait_ge(td_in, 16 * WG)
            link(dve.tensor_copy(TDF, TD))
            for g in range(WG):
                last = dve.tensor_scalar(TDF[:, g * P:(g + 1) * P], TDF[:, g * P:(g + 1) * P], w2[:, g:g + 1], None, ALU.is_lt, ALU.add, accum_out=over[:, g:g + 1])
            link(last)
            link(dve.scalar_tensor_tensor(tw[:, :], tw[:, :], float(P), over[:, :], ALU.mult, ALU.add))
            dve.tensor_copy(wstart[:, :], tw[:, :]).then_inc(wstart_ready, 1)
            dve.wait_ge(wrows_in, 16 * 3 * WG)
            link(dve.tensor_scalar(CODEF.bitcast(I32), SR, P - 1, None, ALU.bitwise_and))
            link(dve.tensor_copy(LOF, CODEF.bitcast(I32)))
            link(dve.tensor_scalar(SR, SR, 7, 1, ALU.logical_shift_right, ALU.logical_shift_left))
            DR3 = DR.rearrange("p (g c) -> p g c", c=RUN)
            for g in range(WG):
                dve.tensor_scalar(over[:, g:g + 1], DR3[:, g, P:RUN], w2[:, g:g + 1], float(WN), ALU.subtract, ALU.is_lt)
                last = dve.tensor_scalar(CODEF[:, g * P:(g + 1) * P], DR3[:, g, 0:P], w2[:, g:g + 1], None, ALU.subtract)
            link(last)
            dve.sem_inc(over_ready, 1)
            FARR = DR[:, 0:WG * P].bitcast(FP32)
            link(dve.tensor_scalar(FARR, CODEF, float(WN), 4096.0, ALU.is_ge, ALU.mult))
            link(dve.tensor_tensor(CODEF, CODEF, FARR, ALU.add))
            link(dve.tensor_copy(FARR, SR))
            link(dve.tensor_tensor(CODEF, CODEF, FARR, ALU.add))
            dve.sem_inc(wcode_ready, 3)
            dve.wait_ge(over_ps, 1)
            link(dve.tensor_reduce(tw[0:1, 0:1], PS[7][0:1, 0:WG], op=ALU.add, axis=mybir.AxisListType.X))
            dve.tensor_copy(flag[:, :], tw[0:1, 0:1]).then_inc(flag_ready, 1)
            dve.wait_ge(wcopied, WCOPIES)

            def onehots(b, par, i):
                for q in range(GROUPS):
                    dve.wait_ge(group_ps, b * GROUPS + q + 1)
                    for j in range(QW):
                        k, w = q % RING * QW + j, bass.ds(b * WPB + q * QW + j, 1)
                        dve.tensor_scalar(OA[:, k, :], iota[:, :], LO[:, w], None, ALU.is_equal)
                        last = dve.tensor_scalar(OR[:, k, 0:WCOLS], iota[:, 0:WCOLS], CODE[:, w], None, ALU.is_equal)
                    last.then_inc(hot_ready, 1)
            block_pairs(dve, onehots)
            dve.wait_ge(group_ps, BLOCKS * GROUPS + RING)
            overfull = flag_of(ENG.DVE, dve)

            def weight_sums(base, array):
                def body(b, par, i):
                    dve.wait_ge(wsum_ps, base * BLOCKS + b + 3)
                    dve.tensor_tensor(array[:, b, :], array[:, b, :], PS[par][:, 0:F], ALU.add).then_inc(wsum_used, 1)
                block_pairs(dve, body)
                dve.wait_ge(wsum_used, (base + 1) * BLOCKS + 2)

            def count_sums(l):
                def rest1(c, nb, par):
                    dve.wait_ge(part1, l * C1 + c + 1)
                    dve.tensor_tensor(ACC[:, bass.ds(c * CHUNK, nb), 0:F], blk(H, c, nb), HP[:, bass.ds(c * CHUNK, nb), 0, :], ALU.subtract).then_inc(part2, 1)

                def rest2(c, nb, par):
                    dve.wait_ge(part3, l * C1 + c + 1)
                    dve.tensor_tensor(HP[:, bass.ds(c * CHUNK, nb), 2, :], ACC[:, bass.ds(c * CHUNK, nb), 0:F], HP[:, bass.ds(c * CHUNK, nb), 1, :],
                                      ALU.subtract).then_inc(parts_ready, 1)
                chunks(dve, rest1)
                chunks(dve, rest2)

                def body(b, par, i):
                    dve.wait_ge(csum_ps, l * BLOCKS + b + 3)
                    for k in (2, 1, 0):
                        dve.tensor_tensor(T1[:, b, :], T1[:, b, :], PS[par][:, k * F:(k + 1) * F], ALU.add).then_inc(csum_used if k == 0 else csum_part, 1)
                        if k:
                            dve.wait_ge(csum_part, (l * BLOCKS + b) * 2 + 3 - k)
                block_pairs(dve, body)
                wait_alone(dve, csum_used, (l + 1) * BLOCKS + 2)

            def onehot(i, u, weighted, slots=4, signal=general_hot):
                col = bass.ds(i * U + u, 1)
                return dve.tensor_scalar(D[:, u % slots, :], iota[:, :], REL[:, col], WT[:, col] if weighted else None,
                                         ALU.is_equal, ALU.mult if weighted else ALU.bypass).then_inc(signal, 1)

            def accumulate(i, u, at, to, width, sums, slots):
                dve.wait_ge(sums, at * STEPS + (i * U + u + 1))
                dve.wait_ge(slots, at * STEPS + (i * U + u + SLOTS))
                dve.tensor_tensor(to, to, PS[4 + u % 4][:, 0:width], ALU.add).then_inc(slots, 1)

            def pass_sums(at, array, weighted):
                with dve.Fori(0, BODIES) as i:
                    b = registers(ENG.DVE, blk_row, i, BLOCKS - 1)
                    for u in range(U + 2):
                        if u < U:
                            onehot(i, u, weighted)
                        if u >= 2:
                            accumulate(i, u - 2, at, array[:, b[u - 2], :], F, general_sum, general_slots)
                wait_alone(dve, general_slots, (at + 1) * STEPS + SLOTS)

            dve.wait_ge(h_ready, C1)
            two_ways(dve, overfull, lambda: weight_sums(0, X), lambda: pass_sums(0, X, True))
            statistics(X, 2)
            rstds(2)

            def q_out(c, nb, par):
                dve.wait_ge(p_ps, c + 1)
                for j in range(nb):
                    last = dve.tensor_tensor(T1[:, c * CHUNK + j, :], PS[4 + par][:, j * P:(j + 1) * P], bc["mb1"][:, :], ALU.add)
                last.then_inc(q_sb, 1)
            chunks(dve, q_out)
            dve.wait_ge(table_out, 32)
            dve.memset(HE[:, :, ONE:ONE + 1], 1.0)
            link(dve.memset(ACC[:, :, :], 0.0))
            dve.sem_inc(acc_ready, 1)

            def dve_step(i, u, b, on):
                if on(0):
                    onehot(i, u, False, DSLOTS, onehot_ready)
                if on(LAG_PRE):
                    v = (u - LAG_PRE) % U
                    dve.wait_ge(pre_ps, i * U + (u - LAG_PRE + 1))
                    dve.wait_ge(gathered[v % SLOTS], i * 32 + 16 * ((u - LAG_PRE) // SLOTS + 1))
                    dve.tensor_tensor(HE[:, v % SLOTS, 0:F], PS[2 + v % 2][:, 0:F], G[:, v % SLOTS, :], ALU.add).then_inc(hid_ready, 1)
                if on(LAG_SUM):
                    accumulate(i, u - LAG_SUM, 0, ACC[:, b[u], :], 2 * F + 1, sum_ready, slots_free)
            pipeline(dve, LAG_SUM, lambda i, n: registers(ENG.DVE, blk_row, i, BLOCKS - 1, LAG_SUM, n or LAG_SUM), dve_step)
            dve.wait_ge(slots_free, STEPS + SLOTS)
            link(dve.tensor_scalar(rcnt[:, :], ACC[:, :, ONE], 1.0, None, ALU.max))
            link(dve.reciprocal(rcnt[:, :], rcnt[:, :]))
            link(dve.tensor_tensor(cn[:, :], ACC[:, :, ONE], rcnt[:, :], ALU.mult))

            def mean_hidden(c, nb, par):
                for j in range(nb):
                    b = c * CHUNK + j
                    last = dve.tensor_scalar(ACC[:, b, 0:F], ACC[:, b, 0:F], rcnt[:, bass.ds(b, 1)], None, ALU.mult)
                last.then_inc(s_ready, 1)
            chunks(dve, mean_hidden)

            def agg_out(c, nb, par):
                dve.wait_ge(agg_ps, c + 1)
                for j in range(nb):
                    b = c * CHUNK + j
                    last = dve.scalar_tensor_tensor(ACC[:, b, 0:F], bc["mb2"][:, :], cn[:, bass.ds(b, 1)], PS[2 + par][:, j * P:(j + 1) * P], ALU.mult, ALU.add)
                last.then_inc(agg_sb, 1)
            chunks(dve, agg_out)
            wide = lambda n, nb: bc[n][:, :].rearrange("p (a f) -> p a f", a=1).broadcast_to([P, nb, F])

            def residual(c, nb, par):
                dve.tensor_tensor(blk(H, c, nb), blk(H, c, nb), wide("ub2", nb), ALU.add).then_inc(s_ready, 1)
            chunks(dve, residual)
            dve.wait_ge(s_ready, 2 * C1)

            def upd_out(c, nb, par):
                dve.wait_ge(o_ps, c + 1)
                dve.tensor_tensor(blk(T1, c, nb), bank3(0, par, nb), blk(H, c, nb), ALU.add).then_inc(o_sb, 1)
            chunks(dve, upd_out)
            dve.wait_ge(o_sb, C1 + 1)
            statistics(T1, 3)
            rstds(3)

            def normed(n, to, signal, base):
                wait_alone(dve, norm_ready, n)

                def body(c, nb, par):
                    for j in range(nb):
                        b = c * CHUNK + j
                        last = dve.tensor_scalar(to[:, b, :], to[:, b, :], MV[:, b, 0:1], rstd[:, bass.ds(b, 1)], ALU.subtract, ALU.mult)
                    last.then_inc(signal, 1)
                chunks(dve, body)

            def times_plus(array, scale, shift, plus, signal_a, a0, signal_b):
                def one(c, nb, par):
                    dve.tensor_tensor(blk(array, c, nb), blk(array, c, nb), wide(scale, nb), ALU.mult).then_inc(signal_a, 1)

                def two(c, nb, par):
                    dve.wait_ge(signal_a, a0 + c + 1)
                    dve.tensor_tensor(blk(array, c, nb), blk(array, c, nb), wide(shift, nb) if plus is None else blk(plus, c, nb),
                                      ALU.add).then_inc(signal_b, 1)
                chunks(dve, one)
                chunks(dve, two)

            normed(3, T1, s_ready, 0)
            dve.wait_ge(s_ready, 3 * C1)
            times_plus(T1, "gamma", "beta", None, s_ready, 3 * C1, o_sb)

            def add_to_x(c, nb, par):
                dve.wait_ge(o_sb, c + C1 + 2)
                dve.tensor_tensor(blk(X, c, nb), blk(X, c, nb), blk(T1, c, nb), ALU.add).then_inc(s_ready, 1)
            chunks(dve, add_to_x)
            dve.wait_ge(s_ready, 5 * C1)
            statistics(X, 4)
            rstds(4)

            def support_out(c, nb, par):
                dve.wait_ge(sup_ps, c + 1)
                dve.tensor_copy(blk(T1, c, nb), bank3(2, par, nb)).then_inc(sup_sb, 1)
            chunks(dve, support_out)

            def bias_init(c, nb, par):
                dve.tensor_copy(blk(H, c, nb), wide("bias2g", nb)).then_inc(s_ready, 1)
            dve.wait_ge(hT_sb, 2 * C1 + 1)
            chunks(dve, bias_init)
            dve.wait_ge(s_ready, 6 * C1)
            two_ways(dve, overfull, lambda: weight_sums(1, H), lambda: pass_sums(1, H, True))

            def relu_to_x(c, nb, par):
                dve.scalar_tensor_tensor(blk(X, c, nb), blk(H, c, nb), 0.0, blk(X, c, nb), ALU.max, ALU.add).then_inc(s_ready, 1)
            chunks(dve, relu_to_x)
            dve.wait_ge(s_ready, 7 * C1)
            statistics(X, 5)
            rstds(5)
            dve.wait_ge(h_ready, 4 * C1)
            with dve.Fori(0, LAYERS) as l:
                wait_alone(dve, gelu_done, l * C1)

                def out_init(c, nb, par):
                    dve.tensor_tensor(blk(T1, c, nb), blk(H, c, nb), ACC[:, bass.ds(c * CHUNK, nb), F:2 * F], ALU.add).then_inc(agg_sb, 1)
                chunks(dve, out_init)
                wait_alone(dve, agg_sb, (l + 2) * C1 + 1)
                two_ways(dve, overfull, lambda: count_sums(l), lambda: pass_sums(l + 2, T1, False))
                dve.sem_inc(pass_done, C1)
                wait_alone(dve, z_sb, (l + 1) * C1 + 1)
                statistics(T1, l * 2 + 6)
                rstds(l * 2 + 6)
                normed(l * 2 + 6, T1, zn_ready, 0)
                wait_alone(dve, y_sb, (l + 1) * C1 + 1)
                statistics(T1, l * 2 + 7)
                rstds(l * 2 + 7)
                wait_alone(dve, layer_in, l * 128 + 128)

                def shifted_h(c, nb, par):
                    dve.tensor_tensor(blk(H, c, nb), blk(H, c, nb), wide("be2", nb), ALU.add).then_inc(q_sb, 1)
                chunks(dve, shifted_h)
                normed(l * 2 + 7, T1, q_sb, 0)
                wait_alone(dve, q_sb, (l * 3 + 3) * C1 + 1)
                times_plus(T1, "g2", None, H, q_sb, (l * 3 + 3) * C1 + 1, yn_ready)
                dve.sem_inc(layer_used, 1)
            dve.wait_ge(gelu_done, LAYERS * C1)

            def final(c, nb, par):
                dve.tensor_tensor(blk(X, c, nb), blk(X, c, nb), blk(H, c, nb), ALU.add).then_inc(s_ready, 1)
            chunks(dve, final)
            dve.wait_ge(s_ready, 8 * C1)
            dve.sem_inc(out_ready, 1)


_INS = ["x", "src", "dst", "edge_weight", "edge_attr_128", "edge_attr_2", "L1_gnn_mW1", "L1_gnn_mb1", "L1_gnn_mW2", "L1_gnn_mb2",
        "L1_gnn_uW1", "L1_gnn_ub1", "L1_gnn_uW2", "L1_gnn_ub2", "L1_gnn_gamma", "L1_gnn_beta", "L2_gnn_weight", "L2_gnn_bias",
        "L3_gnn_W1", "L3_gnn_b1", "L3_gnn_g1", "L3_gnn_be1", "L3_gnn_W2", "L3_gnn_b2", "L3_gnn_g2", "L3_gnn_be2"]


def kernel(**inputs):
    import numpy as np
    import concourse.bacc as bacc
    from concourse.bass_utils import run_bass_kernel_spmd

    nc = bacc.Bacc("TRN2", target_bir_lowering=False, num_devices=1)
    layout = {"edge_attr_2": lambda a: a.T,
              "L3_gnn_W1": lambda a: a.transpose(0, 2, 1).reshape(LAYERS * F, F),
              "L3_gnn_W2": lambda a: a.transpose(0, 2, 1).reshape(LAYERS * F, F),
              "L3_gnn_g1": lambda a: a.reshape(LAYERS * F, 1),
              "L3_gnn_be1": lambda a: a.reshape(LAYERS * F, 1)}
    arrays, args = {}, []
    for name in _INS:
        a = np.asarray(inputs[name])
        a = np.ascontiguousarray(layout[name](a) if name in layout else a)
        arrays[f"in_{name}"] = a
        args.append(nc.dram_tensor(f"in_{name}", a.shape, mybir.dt.from_np(a.dtype), kind="ExternalInput").ap())
    out = nc.dram_tensor("out", (NODES, F), FP32, kind="ExternalOutput").ap()
    build_gnn(nc, *args, out)
    r = run_bass_kernel_spmd(nc, [arrays], core_ids=[0])
    return r.results[0]["out"]
```

```python
from contextlib import ExitStack

import concourse.bass as bass
from concourse import mybir

FP32 = mybir.dt.float32
I32 = mybir.dt.int32
ALU = mybir.AluOpType
ACT = mybir.ActivationFunctionType
ENG = mybir.EngineType

NODES = 6250
EDGES = 206250
F = 128
P = 128
BLOCKS = -(-NODES // P)
LAST = NODES - (BLOCKS - 1) * P
TILES = -(-EDGES // P)
TAIL = EDGES - (TILES - 1) * P
STEPS = TILES + BLOCKS - 1
SG = -(-STEPS // P)
TROWS = SG * P
U = 20
QUARTER = U // 4
AHEAD = 8
POOL_WAITS = (0, 3, 5, 8, 10, 13, 15, 18)
LAG_T, LAG_PRE, LAG_RELU, LAG_SUM = 2, 3, 4, 5
BODIES = STEPS // U
SLOTS = 10
DSLOTS = 10
DROOM = 6
STAGED = 1 + 4 * BODIES
EPS = 1e-5
FAR = 1 << 20
LAYERS = 3
CHUNK = 4
CHUNKS = BLOCKS // CHUNK
C1 = CHUNKS + 1
WN = 2
WCOLS = WN * BLOCKS
WPB = P // WN
WINDOWS = BLOCKS * WPB
WG = -(-WINDOWS // P)
QW = 4
RING = 4
GROUPS = WPB // QW
BF16 = mybir.dt.bfloat16
NP = BLOCKS * P
RUN = P + 1
SPECIAL = TROWS
assert BODIES * U == STEPS and CHUNKS * CHUNK + 1 == BLOCKS and CHUNKS % 2 == 0 and TROWS >= TILES


def build_gnn(nc, x, src, dst, weight, attr128, attr2T, mW1, mb1, mW2, mb2, uW1, ub1, uW2, ub2, gamma, beta,
              W2g, bias2g, L3W1T, L3b1, L3g1, L3be1, L3W2T, L3b2, L3g2, L3be2, out):
    ctx = ExitStack()
    with ctx:
        def sb(name, shape, dt=FP32):
            return ctx.enter_context(nc.sbuf_tensor(name, shape, dt))

        def sem(name):
            return ctx.enter_context(nc.semaphore(name))

        src_rows = nc.dram_tensor("src_rows", (TROWS + 1, P), I32).ap()
        dst_rows = nc.dram_tensor("dst_rows", (TROWS + 1, P), I32).ap()
        w_rows = nc.dram_tensor("w_rows", (TROWS + 1, P), FP32).ap()
        dlast_tab = nc.dram_tensor("dlast_tab", (1, TROWS), FP32).ap()
        flag_tab = nc.dram_tensor("flag_tab", (1, 1), I32).ap()
        weight_mat = nc.dram_tensor("weight_mat", (BLOCKS, P, NP), FP32).ap()
        count_mat = nc.dram_tensor("count_mat", (BLOCKS, P, NP), BF16).ap()
        step_tab = nc.dram_tensor("step_tab", (2, AHEAD + TROWS), I32).ap()
        body_tab = nc.dram_tensor("body_tab", (2, BODIES + 1, 32), I32).ap()
        blk_row, start_row = body_tab[0], body_tab[1]
        tables = [nc.dram_tensor(f"table{k}", (NODES, F), FP32).ap() for k in range(2)]

        X = sb("X", [P, BLOCKS, F])
        H = sb("H", [P, BLOCKS, F])
        ACC = sb("ACC", [P, BLOCKS, 2 * F + 1])
        T1 = sb("T1", [P, BLOCKS, F])
        BIG = sb("BIG", [P, 2 * NP])
        HT = BIG[:, 0:NP]
        T2 = BIG[:, NP:2 * NP]

        G = T2[:, 0:SLOTS * F].rearrange("p (s f) -> p s f", f=F)
        HE0 = SLOTS * F
        HE = T2[:, HE0:HE0 + SLOTS * (2 * F + 1)].rearrange("p (s f) -> p s f", f=2 * F + 1)
        D0 = HE0 + SLOTS * (2 * F + 1)
        DT = T2[:, D0 + DROOM * P:D0 + (DROOM + 2) * P].rearrange("p (s f) -> p s f", f=P)
        A2 = T2[0:2, D0 + (DROOM + 2) * P:D0 + (DROOM + 2 + SLOTS) * P].rearrange("p (s f) -> p s f", f=P)

        SRC = sb("SRC", [P, TROWS + U], mybir.dt.uint16)
        REL_WT = sb("REL_WT", [P, 2 * TROWS])
        REL = REL_WT[:, 0:TROWS]
        WT = REL_WT[:, TROWS:2 * TROWS]
        IDX = sb("IDX", [P, 4, QUARTER], I32)

        T1f = T1[:, :, :].rearrange("p b f -> p (b f)")
        ACCf = ACC[:, :, :].rearrange("p b f -> p (b f)")
        LO = T1f[:, 0:WINDOWS // 2].bitcast(BF16)
        CODE = T1f[:, WINDOWS // 2:WINDOWS].bitcast(BF16)
        WW = BIG[:, 2 * NP - WINDOWS:2 * NP]
        SR = ACCf[:, 0:WG * P].bitcast(I32)
        DR = ACCf[:, WG * P:WG * (P + RUN)].bitcast(I32)
        WR = ACCf[:, WG * (P + RUN):WG * (2 * P + RUN)]
        LOF = BIG[:, 0:WG * P]
        CODEF = BIG[:, WG * P:2 * WG * P]
        DLB = BIG[:, 0:TROWS]
        TJ = BIG[:, TROWS:2 * TROWS]
        TD = BIG[:, 2 * WG * P:3 * WG * P].bitcast(I32)
        TDF = BIG[:, WG * P:2 * WG * P]
        OA = BIG[:, NP:NP + RING * QW * P].rearrange("p (s c) -> p s c", c=P)
        OR = T1f[:, WINDOWS:WINDOWS + RING * QW * 2 * WCOLS].rearrange("p (s c) -> p s c", c=2 * WCOLS)
        assert WINDOWS + RING * QW * 2 * WCOLS <= NP and NP + RING * QW * P <= 2 * NP - WINDOWS
        WB = [ACCf[:, k * NP:(k + 1) * NP] for k in range(2)]
        CB = [HT.bitcast(BF16)[:, k * NP:(k + 1) * NP] for k in range(2)]
        WIN = [BIG[:, k * NP:(k + 1) * NP] for k in range(2)]
        HP = BIG[:, 0:3 * NP // 2].bitcast(BF16).rearrange("p (b k f) -> p b k f", k=3, f=F)
        CIN = [BIG[:, 3 * NP // 2:2 * NP].bitcast(BF16), REL_WT[:, 0:NP // 2].bitcast(BF16)]

        NB_O, NB_OT, NB_Z, NB_ZT, NB_Y, NB_S = ([ACC[:, 2 * k + par, 0:F] for par in range(2)] for k in range(6))

        ident = sb("ident", [P, P])
        iota = sb("iota", [P, P])
        iotai = T1[:, 1, :].bitcast(I32)
        ones = sb("ones", [P, P])
        epsc = sb("epsc", [P, 1])
        mW1s = sb("mW1s", [P, 2 * F])
        mWcs = sb("mWcs", [2, F])
        mW2s = sb("mW2s", [P, F])
        uW1s = sb("uW1s", [P, 2, F])
        uW2s = sb("uW2s", [P, F])
        Wgs = sb("Wgs", [P, F])
        lw1 = sb("lw1", [P, F])
        lw2 = sb("lw2", [P, F])
        bc = {}
        for n in ("mb1", "mb2", "ub2", "gamma", "beta", "bias2g", "g2", "be2"):
            bc[n] = sb("bc_" + n, [P, F])
        D = [T2[:, D0 + k * P:D0 + (k + 1) * P] for k in range(DROOM)] + [lw1[:, :], lw2[:, :], bc["g2"][:, :], bc["be2"][:, :]]
        assert len(D) == DSLOTS and D0 + (DROOM + 2 + SLOTS) * P <= NP
        ub1c = sb("ub1c", [P, 1])
        g1c = sb("g1c", [P, 1])
        be1c = sb("be1c", [P, 1])
        b1r = sb("b1r", [1, F])
        b2r = sb("b2r", [1, F])

        w2i = sb("w2i", [P, WG], I32)
        w2 = sb("w2", [P, WG])
        tw = sb("tw", [P, WG])
        twi = sb("twi", [P, WG], I32)
        wstart = sb("wstart", [P, WG], I32)
        over = sb("over", [P, WG])
        flag = sb("flag", [1, 1], I32)
        WS = sb("WS", [P, 2, WPB])
        thr = sb("thr", [P, BLOCKS - 1])
        thrb = sb("thrb", [P, BLOCKS - 1])
        dlasti = sb("dlasti", [P, SG], I32)
        dlast = sb("dlast", [P, SG])
        svec = sb("svec", [P, SG])
        sveci = sb("sveci", [P, SG], I32)
        bs = sb("bs", [P, SG])
        b128 = sb("b128", [P, SG])
        ts = sb("ts", [P, SG])
        es = sb("es", [P, SG])
        tsi = sb("tsi", [P, SG], I32)
        bsi = sb("bsi", [P, SG], I32)
        esi = sb("esi", [P, SG], I32)
        fill = T1[:, 0, :].bitcast(I32)
        ST = sb("ST", [P, BLOCKS, 6])
        MV = sb("MV", [P, BLOCKS, 2])
        rstd = sb("rstd", [P, BLOCKS])
        nmr = sb("nmr", [P, BLOCKS])
        rcnt = sb("rcnt", [P, BLOCKS])
        cn = sb("cn", [P, BLOCKS])

        RS = HT[:, 0:SG * P].bitcast(I32).rearrange("p (g c) -> p g c", c=P)
        RD = HT[:, SG * P:2 * SG * P].bitcast(I32).rearrange("p (g c) -> p g c", c=P)
        RW = HT[:, 2 * SG * P:3 * SG * P].rearrange("p (g c) -> p g c", c=P)
        RELF = T2[:, 0:SG * P].rearrange("p (g c) -> p g c", c=P)
        cmp = T2[:, 2 * SG * P:2 * SG * P + SG * (BLOCKS - 1)].rearrange("p (g b) -> p g b", b=BLOCKS - 1)
        SRCF = T2[:, SG * P:2 * SG * P].rearrange("p (g c) -> p g c", c=P)


        PS = [ctx.enter_context(nc.psum_tensor(f"ps{k}", [P, 512], FP32)) for k in range(8)]

        waits_passed = sem("waits_passed")
        fill_ready, consts, ident_zero = sem("fill_ready"), sem("consts"), sem("ident_zero")
        x_in, weights_in, layer_in = sem("x_in"), sem("weights_in"), sem("layer_weights_in")
        rows_in, tail_in, dlast_in = sem("edge_rows_in"), sem("tail_rows_in"), sem("dlast_in")
        cmp_ready, tau_ready, steps_ready = sem("cmp_ready"), sem("tau_ready"), sem("steps_ready")
        step_rows_out, regs_in = sem("step_rows_out"), sem("step_regs_in")
        rows_gathered, rel_ready = sem("step_rows_gathered"), sem("rel_rows_ready")
        turned, turn_copied = sem("step_rows_turned"), sem("step_table_copied")
        table_out = sem("gather_table_stored")
        staged, slots_free = sem("indices_staged"), sem("slots_free")
        onehot_ready, sum_ready, acc_ready = sem("onehot_ready"), sem("step_sum_ready"), sem("acc_initialised")
        dt_ps, dt_sb, pre_ps = sem("onehotT_in_psum"), sem("onehotT_in_sbuf"), sem("edge_pre_in_psum")
        hid_ready, relu_done = sem("edge_hidden_ready"), sem("edge_relu_done")
        stats_done, aggr_done, std_ready, norm_ready = sem("stats_done"), sem("aggr_done"), sem("std_ready"), sem("norm_ready")
        h_ready, link_done, part_done = sem("h_ready"), sem("vector_link"), sem("vector_part_done")
        hT_ps, hT_sb = sem("hT_in_psum"), sem("hT_in_sbuf")
        p_ps, p_sb, q_sb = sem("pq_in_psum"), sem("p_in_sbuf"), sem("q_in_sbuf")
        s_ready, sT_ps, sT_sb = sem("mean_hidden_ready"), sem("mean_hiddenT_in_psum"), sem("mean_hiddenT_in_sbuf")
        agg_ps, agg_sb, aT_ps, aT_sb = sem("agg_in_psum"), sem("agg_in_sbuf"), sem("aggT_in_psum"), sem("aggT_in_sbuf")
        u_ps, u_sb, o_ps, o_sb = sem("updT_in_psum"), sem("updT_in_sbuf"), sem("upd_in_psum"), sem("upd_in_sbuf")
        sup_ps, sup_sb = sem("support_in_psum"), sem("support_in_sbuf")
        oT_ps, oT_sb, z_ps = sem("outT_in_psum"), sem("outT_in_sbuf"), sem("z_in_psum")
        z_stats, z_aggr, z_std, z_rstd = sem("z_stats_ready"), sem("z_mean_var_ready"), sem("z_std_ready"), sem("z_rstd_ready")
        y_stats, y_aggr, y_std, y_rstd = sem("y_stats_ready"), sem("y_mean_var_ready"), sem("y_std_ready"), sem("y_rstd_ready")
        zn_ready, zT_ps, zT_sb = sem("z_normed"), sem("zT_in_psum"), sem("zT_in_sbuf")
        y_ps, y_normed, y_scaled, yn_ready = sem("y_in_psum"), sem("y_normed"), sem("y_scaled"), sem("y_plus_h_ready")
        h_shifted, gelu_done = sem("h_shifted"), sem("layer_out_ready")
        layer_used, out_ready, out_stored = sem("layer_weights_used"), sem("out_ready"), sem("out_stored")
        dlast_out, dlb_in = sem("dlast_stored"), sem("dlast_rows_in")
        tw_ready, td_in, wstart_ready, wrows_in = sem("window_tile_ready"), sem("window_tile_in"), sem("window_start_ready"), sem("window_rows_in")
        wcode_ready, wturned, wcopied = sem("window_rows_ready"), sem("window_rows_turned"), sem("window_table_copied")
        dlast_ready = sem("tile_ends_ready")
        over_ready, over_ps, flag_ready, flag_out = sem("overfull_ready"), sem("overfull_in_psum"), sem("flag_ready"), sem("flag_stored")
        hot_ready, hotw_ready = sem("window_onehots_ready"), sem("window_weighted_ready")
        group_ps, group_out = sem("group_in_psum"), sem("group_copied")
        mat_out = [sem(f"matrix_block_stored{k}") for k in range(2)]
        wblk_in = [sem(f"weight_block_in{k}") for k in range(2)]
        cblk_in = [sem(f"count_block_in{k}") for k in range(2)]
        wsum_ps, wsum_used, csum_ps, osum_ready = sem("dense_sum_ready"), sem("dense_sum_used"), sem("count_sum_ready"), sem("out_sum_ready")
        ws_ready = sem("block_weights_staged")
        csum_part = sem("count_sum_part_added")
        part1, part2, part3 = sem("h_part1_ready"), sem("h_rest1_ready"), sem("h_part2_ready")
        parts_ready = sem("h_parts_ready")
        general_sum, general_slots, general_hot, general_staged, general_init = (
            sem("general_sum_ready"), sem("general_slots_free"), sem("general_onehot_ready"), sem("general_indices_staged"), sem("general_pad"))
        general_out = sem("general_table_stored")
        general_gathered = [sem(f"general_gathered{k}") for k in range(SLOTS)]
        gathered = [sem(f"gathered{k}") for k in range(SLOTS)]
        attr_in = [sem(f"attr_in{k}") for k in range(SLOTS)]
        copied = (hT_sb, p_sb, q_sb, sT_sb, agg_sb, aT_sb, u_sb, o_sb, sup_sb)

        def chunks(eng, body):
            with eng.Fori(0, CHUNKS // 2) as i:
                body(i * 2, CHUNK, 0)
                body(i * 2 + 1, CHUNK, 1)
            body(CHUNKS, 1, 0)

        def chunks_of_pe(body):
            for c in range(C1):
                body(c, CHUNK if c < CHUNKS else 1, c % 2)

        def pipeline(eng, lag, values, position):
            got = values(0, U)
            for u in range(U):
                position(0, u, got, lambda part, u=u: u >= part)
            with eng.Fori(1, BODIES) as i:
                got = values(i, U)
                for u in range(U):
                    position(i, u, got, lambda part: True)
            if lag:
                got = values(BODIES, 0)
                for u in range(lag):
                    position(BODIES, u, got, lambda part, u=u: u < part)

        def wait_alone(eng, signal, value):
            eng.wait_ge(signal, value)
            eng.sem_inc(waits_passed, 1)

        def node_store(eng, dram, array, signal):
            eng.dma_start(dram[0:(BLOCKS - 1) * P, :].rearrange("(b p) f -> p b f", p=P),
                          array[:, 0:BLOCKS - 1, :]).then_inc(signal, 16)
            eng.dma_start(dram[(BLOCKS - 1) * P:NODES, :], array[0:LAST, BLOCKS - 1, :]).then_inc(signal, 16)

        def registers(engine, row, i, top, lag=0, n=U):
            _, values = nc.values_load_multi_w_load_instructions(
                row[bass.ds(i, 1), AHEAD - lag:AHEAD - lag + n], engines=[engine], min_val=0, max_val=top,
                skip_runtime_bounds_check_because="computed on the chip, at most the last block or tile")
            return values

        def blk(array, c, nb):
            return array[:, bass.ds(c * CHUNK, nb), :]

        def cols(array, c, nb):
            return array[:, bass.ds(c * CHUNK * P, nb * P)]

        def bank(pair, par, nb):
            return PS[pair + par][:, 0:nb * P]

        def bank3(pair, par, nb):
            return bank(pair, par, nb).rearrange("p (b f) -> p b f", f=F)

        def block_pairs(eng, body):
            with eng.Fori(0, BLOCKS // 2) as i:
                body(i * 2, 0, i)
                body(i * 2 + 1, 1, i)
            body(BLOCKS - 1, 0, BLOCKS // 2)

        def staggered(eng, stages):
            head = -(-max(lag for lag, _ in stages) // 2) + 1

            def apart(b):
                for lag, body in stages:
                    if 0 <= b - lag < BLOCKS:
                        body(b - lag, (b - lag) % 2, (b - lag) // 2)
            for b in range(2 * head):
                apart(b)
            with eng.Fori(head, BLOCKS // 2) as i:
                for u in range(2):
                    for lag, body in stages:
                        body(i * 2 + (u - lag), (u - lag) % 2, i + (u - lag) // 2)
            for b in range(BLOCKS - 1, BLOCKS + max(lag for lag, _ in stages)):
                apart(b)

        def again(v):
            return not isinstance(v, int) or v >= 2

        def flag_of(engine, eng):
            eng.wait_ge(flag_out, 16)
            return nc.values_load(flag_tab[0:1, 0:1], engines=[engine], min_val=0, max_val=P * WG)

        def two_ways(eng, overfull, dense, general):
            with eng.If(overfull == 0):
                dense()
            with eng.Else():
                general()

        T2n = T2[:, :].rearrange("p (b f) -> p b f", f=F)
        ONE = 2 * F
        ROWS_PARTS = 13
        WCOPIES = 3 * -(-WG // 4)
        block = ctx.enter_context(nc.Block())

        @block.sync
        def _(sp):
            sp.dma_start(X[:, 0:BLOCKS - 1, :], x[0:(BLOCKS - 1) * P, :].rearrange("(b p) f -> p b f", p=P)).then_inc(x_in, 16)
            sp.wait_ge(acc_ready, 1)
            sp.dma_start(X[0:LAST, BLOCKS - 1, :], x[(BLOCKS - 1) * P:NODES, :]).then_inc(x_in, 16)
            n0 = (TILES - 1) * P
            for rows, flat in ((src_rows, src), (dst_rows, dst), (w_rows, weight)):
                sp.dma_start(rows[0:TILES - 1, :].rearrange("t c -> (t c)").rearrange("(a b) -> a b", a=16),
                             flat[0:n0].rearrange("(a b) -> a b", a=16)).then_inc(rows_in, 16)
                sp.dma_start(rows[TILES - 1:TILES, 0:TAIL], flat[n0:EDGES].rearrange("(a b) -> a b", a=1)).then_inc(rows_in, 16)
                sp.dma_start(rows[SPECIAL:SPECIAL + 1, :], flat[EDGES - P:EDGES].rearrange("(a b) -> a b", a=1)).then_inc(tail_in, 16)
            sp.wait_ge(fill_ready, 3)
            for rows, pad in ((dst_rows, fill), (src_rows, iotai), (w_rows, ones)):
                sp.dma_start(rows[TILES:TROWS, :], pad[0:TROWS - TILES, :]).then_inc(rows_in, 16)
                sp.dma_start(rows[TILES - 1:TILES, TAIL:P], pad[0:1, TAIL:P]).then_inc(rows_in, 16)
            sp.wait_ge(tail_in, 48)
            sp.dma_start(dst_rows[SPECIAL:SPECIAL + 1, 0:P - TAIL], fill[0:1, 0:P - TAIL]).then_inc(rows_in, 16)
            sp.wait_ge(rows_in, 16 * ROWS_PARTS)
            full = (TILES - 1) // P
            sp.dma_start(dlasti[:, 0:full], dst_rows[0:full * P, P - 1:P].rearrange("(g p) c -> p (g c)", p=P),
                         allow_slow_non_contiguous=True).then_inc(dlast_in, 16)
            sp.dma_start(dlasti[0:TILES - 1 - full * P, full:full + 1], dst_rows[full * P:TILES - 1, P - 1:P],
                         allow_slow_non_contiguous=True).then_inc(dlast_in, 16)
            sp.wait_ge(dlast_ready, 1)
            sp.dma_start(dlast_tab[0, :].rearrange("(g p) -> p g", p=P), dlast[:, :], allow_slow_non_contiguous=True).then_inc(dlast_out, 16)
            for to, of in ((mW1s[:, 0:F], mW1[0:F, :]), (mW1s[:, F:2 * F], mW1[F:2 * F, :]), (mWcs[:, :], mW1[2 * F:2 * F + 2, :]),
                           (mW2s[:, :], mW2), (uW1s[:, 0, :], uW1[0:F, :]), (uW1s[:, 1, :], uW1[F:2 * F, :]), (uW2s[:, :], uW2),
                           (Wgs[:, :], W2g), (bc["mb1"][:, :], mb1.partition_broadcast(P)), (bc["mb2"][:, :], mb2.partition_broadcast(P)),
                           (bc["ub2"][:, :], ub2.partition_broadcast(P)), (bc["gamma"][:, :], gamma.partition_broadcast(P)),
                           (bc["beta"][:, :], beta.partition_broadcast(P)), (bc["bias2g"][:, :], bias2g.partition_broadcast(P)),
                           (ub1c[:, :], ub1.rearrange("(f a) -> f a", a=1))):
                sp.dma_start(to, of).then_inc(weights_in, 16)
            sp.dma_start(step_tab[:, 0:AHEAD], iotai[0:2, 0:AHEAD]).then_inc(step_rows_out, 16)
            sp.wait_ge(steps_ready, 1)
            sp.dma_start(step_tab[0, AHEAD:].rearrange("(g p) -> p g", p=P), bsi[:, :], allow_slow_non_contiguous=True).then_inc(step_rows_out, 16)
            sp.dma_start(step_tab[1, AHEAD:].rearrange("(g p) -> p g", p=P), esi[:, :], allow_slow_non_contiguous=True).then_inc(step_rows_out, 16)
            sp.wait_ge(step_rows_out, 48)
            for k in range(2):
                sp.dma_start(body_tab[k, 0:BODIES, 0:AHEAD], step_tab[k, 0:STEPS].rearrange("(i u) -> i u", u=U)[:, 0:AHEAD]).then_inc(regs_in, 16)
                sp.dma_start(body_tab[k, 0:BODIES, AHEAD:AHEAD + U], step_tab[k, AHEAD:AHEAD + STEPS].rearrange("(i u) -> i u", u=U)).then_inc(regs_in, 16)
                sp.dma_start(body_tab[k, BODIES:BODIES + 1, 0:AHEAD], step_tab[k:k + 1, STEPS:STEPS + AHEAD]).then_inc(regs_in, 16)
            sp.wait_ge(dlast_out, 16)
            sp.wait_ge(turn_copied, 3 * SG)
            sp.dma_start(DLB, dlast_tab.broadcast_to([P, TROWS])).then_inc(dlb_in, 16)
            sp.wait_ge(flag_ready, 1)
            sp.dma_start(flag_tab, flag[:, :]).then_inc(flag_out, 16)
            overfull = flag_of(ENG.SP, sp)

            def store_block(b, par, i):
                sp.wait_ge(group_out, (b + 1) * GROUPS + 4)
                sp.dma_start(weight_mat[b, :, :], WB[par]).then_inc(mat_out[par], 16)
                sp.dma_start(count_mat[b, :, :], CB[par]).then_inc(mat_out[par], 16)
            block_pairs(sp, store_block)
            sp.wait_ge(mat_out[0], 32 * 25)
            sp.wait_ge(mat_out[1], 32 * 24)

            def load_weights(base):
                def body(b, par, i):
                    sp.wait_ge(wsum_ps, base * BLOCKS + b + 1)
                    sp.dma_start(WIN[par], weight_mat[b, :, :]).then_inc(wblk_in[par], 16)
                block_pairs(sp, body)

            def load_counts(l):
                sp.wait_ge(wsum_used, 2 * BLOCKS + 2)

                def body(b, par, _):
                    if again(b):
                        sp.wait_ge(csum_ps, l * BLOCKS + (b - 1))
                    sp.dma_start(CIN[par], count_mat[b, :, :]).then_inc(cblk_in[par], 16)
                body(0, 0, 0)
                body(1, 1, 0)
                with sp.Fori(1, BLOCKS // 2) as i:
                    body(i * 2, 0, i)
                    body(i * 2 + 1, 1, i)
                body(BLOCKS - 1, 0, BLOCKS // 2)

            def general_table(array, signal, count):
                wait_alone(sp, signal, count)
                node_store(sp, tables[0], array, general_out)

            sp.wait_ge(h_ready, C1)
            two_ways(sp, overfull, lambda: load_weights(0), lambda: general_table(H, h_ready, C1))
            sp.wait_ge(p_sb, C1 + 1)
            node_store(sp, tables[1], T2n, table_out)
            sp.wait_ge(regs_in, 96)
            sp.wait_ge(acc_ready, 2)
            with sp.Fori(0, BODIES) as i:
                first = registers(ENG.SP, start_row, i, EDGES - P)
                for u in range(U):
                    k = u % SLOTS
                    if u % 4 == 0:
                        sp.wait_ge(slots_free, i * U + (u + 4))
                    sp.dma_start(HE[:, k, F:2 * F], attr128[bass.ds(first[u], P), :]).then_inc(attr_in[k], 16)
                    sp.dma_start(A2[:, k, :], attr2T[:, bass.ds(first[u], P)]).then_inc(attr_in[k], 16)
            sp.wait_ge(sup_sb, C1 + 1)
            two_ways(sp, overfull, lambda: load_weights(1), lambda: general_table(T1, sup_sb, C1 + 1))
            with sp.Fori(0, LAYERS) as l:
                wait_alone(sp, layer_used, l)
                wait_alone(sp, gelu_done, l * BLOCKS)
                for to, of in ((lw1[:, :], L3W1T[bass.ds(l * F, F), :]), (lw2[:, :], L3W2T[bass.ds(l * F, F), :]),
                               (b1r[:, :], L3b1[bass.ds(l, 1), :]), (b2r[:, :], L3b2[bass.ds(l, 1), :]),
                               (bc["g2"][:, :], L3g2[bass.ds(l, 1), :].broadcast_to([P, F])),
                               (bc["be2"][:, :], L3be2[bass.ds(l, 1), :].broadcast_to([P, F])),
                               (g1c[:, :], L3g1[bass.ds(l * F, F), :]), (be1c[:, :], L3be1[bass.ds(l * F, F), :])):
                    sp.dma_start(to, of).then_inc(layer_in, 16)
                sp.wait_ge(slots_free, STEPS + SLOTS)
                sp.wait_ge(h_ready, 4 * C1)
                two_ways(sp, overfull, lambda: load_counts(l), lambda: general_table(H, gelu_done, l * BLOCKS))
            sp.wait_ge(out_ready, 1)
            node_store(sp, out, X, out_stored)
            sp.wait_ge(out_stored, 32)

        @block.gpsimd
        def _(pool):
            pool.memset(fill[:, :], FAR).then_inc(fill_ready, 1)
            pool.iota(iotai[:, :], pattern=[[1, P]], base=0, channel_multiplier=0).then_inc(fill_ready, 1)
            pool.memset(ones[:, :], 1.0).then_inc(fill_ready, 1)
            pool.iota(sveci[:, :], pattern=[[P, SG]], base=0, channel_multiplier=1).then_inc(consts, 1)
            pool.memset(ident[:, :], 0.0).then_inc(ident_zero, 1)
            pool.wait_ge(ident_zero, 1)
            pool.affine_select(out=ident[:, :], in_=ident[:, :], compare_op=ALU.not_equal, fill=1.0, base=0,
                               pattern=[[-1, P]], channel_multiplier=1).then_inc(consts, 1)
            pool.memset(epsc[:, :], EPS).then_inc(consts, 1)
            pool.memset(SRC[:, TROWS:TROWS + U], 0).then_inc(consts, 1)
            pool.iota(w2i[:, :], pattern=[[WN * P, WG]], base=0, channel_multiplier=WN).then_inc(consts, 1)
            pool.wait_ge(rows_in, 16 * ROWS_PARTS)
            pool.wait_ge(steps_ready, 1)
            for g in range(SG):
                for rows, to in ((src_rows, RS), (dst_rows, RD), (w_rows, RW)):
                    pool.indirect_dma_start(to[:, g, :], None, rows, bass.IndirectOffsetOnAxis(ap=tsi[:, g:g + 1], axis=0)
                                            ).then_inc(rows_gathered, 16)
            pool.wait_ge(tw_ready, 1)
            for g in range(WG):
                pool.indirect_dma_start(TD[:, g * P:(g + 1) * P], None, dst_rows, bass.IndirectOffsetOnAxis(ap=twi[:, g:g + 1], axis=0)).then_inc(td_in, 16)
            pool.wait_ge(wstart_ready, 1)
            for g in range(WG):
                for rows, to, n in ((src_rows, SR, P), (dst_rows, DR, RUN), (w_rows, WR, P)):
                    pool.indirect_dma_start(to[:, g * n:(g + 1) * n], None, rows.rearrange("t (c a) -> (t c) a", a=1),
                                            bass.IndirectOffsetOnAxis(ap=wstart[:, g:g + 1], axis=0)).then_inc(wrows_in, 16)
            pool.sem_inc(slots_free, SLOTS)
            pool.sem_inc(hid_ready, SLOTS)
            pool.sem_inc(general_slots, SLOTS)
            pool.wait_ge(wcopied, WCOPIES)

            def weighted(b, par, i):
                pool.tensor_copy(WS[:, par, :], WW[:, bass.ds(b * WPB, WPB)]).then_inc(ws_ready, 1)
                wait_alone(pool, ws_ready, b + 1)
                for q in range(GROUPS):
                    wait_alone(pool, hot_ready, b * GROUPS + q + 1)
                    for j in range(QW):
                        k = q % RING * QW + j
                        last = pool.tensor_scalar(OR[:, k, WCOLS:2 * WCOLS], OR[:, k, 0:WCOLS], WS[:, par, q * QW + j:q * QW + j + 1], 1.0, ALU.mult, ALU.mult)
                    last.then_inc(hotw_ready, 1)
            block_pairs(pool, weighted)

            def stage(col, q, staged):
                pool.tensor_copy(IDX[:, q, :], SRC[:, bass.ds(col, QUARTER)]).then_inc(staged, 1)

            def gathers(table, at, staged, slots, done):
                stage(0, 0, staged)
                with pool.Fori(0, BODIES) as i:
                    for q in range(4):
                        stage(i * U + (q + 1) * QUARTER, (q + 1) % 4, staged)
                        pool.wait_ge(staged, at * STAGED + (i * 4 + q + 1))
                        for u in range(q * QUARTER, (q + 1) * QUARTER):
                            if u in POOL_WAITS:
                                n = next((w for w in POOL_WAITS if w > u), U) - u
                                wait_alone(pool, slots, at * STEPS + (i * U + u + n))
                            pool.indirect_dma_start(G[:, u % SLOTS, :], None, table,
                                                    bass.IndirectOffsetOnAxis(ap=IDX[:, q, u % QUARTER:u % QUARTER + 1], axis=0)
                                                    ).then_inc(done[u % SLOTS], 16)
                wait_alone(pool, staged, (at + 1) * STAGED)

            def general(at):
                wait_alone(pool, general_out, (at + 1) * 32)
                gathers(tables[0], at, general_staged, general_slots, general_gathered)

            nothing = lambda: pool.sem_inc(waits_passed, 1)
            overfull = flag_of(ENG.Pool, pool)
            two_ways(pool, overfull, nothing, lambda: general(0))
            pool.wait_ge(table_out, 32)
            gathers(tables[1], 0, staged, hid_ready, gathered)
            two_ways(pool, overfull, nothing, lambda: general(1))
            with pool.Fori(0, LAYERS) as l:
                two_ways(pool, overfull, nothing, lambda: general(l + 2))

        @block.scalar
        def _(act):
            for s in copied:
                if s not in (q_sb, agg_sb, o_sb, sup_sb):
                    act.sem_inc(s, 1)

            def stds(n):
                act.wait_ge(aggr_done, n * 6)
                act.activation(rstd[:, :], MV[:, :, 1], ACT.Sqrt, bias=epsc[:, 0:1]).then_inc(std_ready, 1)

            def relu_norm(n):
                act.wait_ge(norm_ready, n)

                def body(c, nb, par):
                    for j in range(nb):
                        b = c * CHUNK + j
                        last = act.activation(H[:, b, :], X[:, b, :], ACT.Relu, bias=nmr[:, bass.ds(b, 1)], scale=rstd[:, bass.ds(b, 1)])
                    last.then_inc(h_ready, 1)
                chunks(act, body)

            def copy_out(ready, done, to, pair, func=ACT.Copy, base=0, as_blocks=False, **kw):
                def body(c, nb, par):
                    act.wait_ge(ready, base + c + 1)
                    if as_blocks:
                        act.activation(blk(to, c, nb), bank3(pair, par, nb), func, **kw).then_inc(done, 1)
                    else:
                        act.activation(cols(to, c, nb), bank(pair, par, nb), func, **kw).then_inc(done, 1)
                chunks(act, body)

            act.wait_ge(consts, 5)
            stds(1)
            relu_norm(1)
            for k in range(3 * SG):
                act.wait_ge(turned, k + 1)
                act.activation((SRC, REL, WT)[k % 3][:, k // 3 * P:(k // 3 + 1) * P], PS[k % 4][:, 0:P], ACT.Copy).then_inc(turn_copied, 1)
            for k in range(WCOPIES):
                which, n = k % 3, min(4 * P, WINDOWS - k // 3 * 4 * P)
                act.wait_ge(wturned, k + 1)
                act.activation((LO, CODE, WW)[which][:, k // 3 * 4 * P:k // 3 * 4 * P + n], PS[k % 4][:, 0:n], ACT.Copy).then_inc(wcopied, 1)
            act.sem_inc(group_out, 4)
            act.sem_inc(wsum_used, 2)

            def group_copies(b, par, i):
                act.wait_ge(mat_out[par], i * 32)
                for q in range(GROUPS):
                    act.wait_ge(group_ps, b * GROUPS + q + 1 + RING)
                    for pair, to in ((q % 4, CB[par]), (4 + q % 4, WB[par])):
                        last = act.activation(
                            to.rearrange("p (h d) -> p h d", d=P)[:, :, q * QW * WN:(q + 1) * QW * WN].rearrange("p h (w j) -> p h w j", j=WN),
                            PS[pair][:, 0:QW * WCOLS].rearrange("p (w h j) -> p h w j", w=QW, j=WN), ACT.Copy)
                    last.then_inc(group_out, 1)
            act.wait_ge(flag_out, 16)
            block_pairs(act, group_copies)
            stds(2)
            relu_norm(2)
            copy_out(hT_ps, hT_sb, HT, 0)
            copy_out(p_ps, p_sb, T2n, 2, as_blocks=True)
            act.wait_ge(table_out, 32)
            overfull = flag_of(ENG.Activation, act)

            def act_step(i, u, _, on):
                if on(LAG_T):
                    v = (u - LAG_T) % U
                    act.wait_ge(dt_ps, i * U + (u - LAG_T + 1))
                    act.activation(DT[:, v % 2, :], PS[v % 2][:, 0:P], ACT.Copy).then_inc(dt_sb, 1)
                if on(LAG_RELU):
                    k = (u - LAG_RELU) % SLOTS
                    act.wait_ge(hid_ready, i * U + (u - LAG_RELU + 1 + SLOTS))
                    act.activation(HE[:, k, 0:F], HE[:, k, 0:F], ACT.Relu).then_inc(relu_done, 1)
            pipeline(act, LAG_RELU, lambda i, n: None, act_step)
            copy_out(sT_ps, sT_sb, T2, 0)
            copy_out(aT_ps, aT_sb, T2, 4)
            copy_out(u_ps, u_sb, T2, 6, func=ACT.Relu, bias=ub1c[:, 0:1])
            stds(3)
            stds(4)
            relu_norm(4)
            copy_out(hT_ps, hT_sb, HT, 0, base=C1)
            stds(5)
            relu_norm(5)
            def parts(l):
                def first(c, nb, par):
                    act.activation(HP[:, bass.ds(c * CHUNK, nb), 0, :], blk(H, c, nb), ACT.Copy).then_inc(part1, 1)

                def second(c, nb, par):
                    act.wait_ge(part2, l * C1 + c + 1)
                    act.activation(HP[:, bass.ds(c * CHUNK, nb), 1, :], ACC[:, bass.ds(c * CHUNK, nb), 0:F], ACT.Copy).then_inc(part3, 1)
                act.wait_ge(h_ready, 4 * C1)
                wait_alone(act, gelu_done, l * BLOCKS)
                chunks(act, first)
                chunks(act, second)

            with act.Fori(0, LAYERS) as l:
                done = lambda v: l * BLOCKS + (v + 1)

                def turned_sum(v, par, _):
                    act.wait_ge(oT_ps, done(v))
                    if again(v):
                        act.wait_ge(z_ps, done(v - 2))
                    act.activation(NB_OT[par], PS[2][:, 0:P], ACT.Copy).then_inc(oT_sb, 1)

                def gelu_z(v, par, _):
                    act.wait_ge(zT_ps, done(v))
                    if again(v):
                        act.wait_ge(y_ps, done(v - 2))
                    act.activation(NB_ZT[par], PS[3][:, 0:P], ACT.Gelu, bias=be1c[:, 0:1], scale=g1c[:, 0:1]).then_inc(zT_sb, 1)

                def std_z(v, par, _):
                    act.wait_ge(z_aggr, done(v))
                    act.activation(rstd[:, par:par + 1], MV[:, par, 1:2], ACT.Sqrt, bias=epsc[:, 0:1]).then_inc(z_std, 1)

                def std_y(v, par, _):
                    act.wait_ge(y_aggr, done(v))
                    act.activation(rstd[:, 2 + par:3 + par], MV[:, 2 + par, 1:2], ACT.Sqrt, bias=epsc[:, 0:1]).then_inc(y_std, 1)

                def layer_out(v, par, _):
                    act.wait_ge(yn_ready, done(v))
                    act.activation(H[:, v, :], NB_Y[par], ACT.Gelu).then_inc(gelu_done, 1)
                two_ways(act, overfull, lambda: parts(l), lambda: act.sem_inc(waits_passed, 1))
                wait_alone(act, layer_in, l * 128 + 128)
                staggered(act, ((1, turned_sum), (3, gelu_z), (2, std_z), (4, std_y), (4, layer_out)))

        @block.tensor
        def _(pe):
            pe.wait_ge(consts, 5)
            pe.wait_ge(fill_ready, 3)
            for g in range(SG):
                pe.wait_ge(cmp_ready, g + 1)
                mm = pe.matmul(PS[7][:, 0:BLOCKS - 1], ones[:, :], cmp[:, g, :], start=(g == 0), stop=(g == SG - 1))
            mm.then_inc(tau_ready, 1)
            for k in range(3 * SG):
                pe.wait_ge(rel_ready, k // 3 * 2 + min(k % 3 + 1, 2))
                if k >= 4:
                    pe.wait_ge(turn_copied, k - 3)
                pe.transpose(PS[k % 4][:, 0:P], (SRCF, RELF, RW)[k % 3][:, k // 3, :], ident[:, :]).then_inc(turned, 1)

            for k in range(WCOPIES):
                pe.wait_ge(wcode_ready, k % 3 + 1)
                pe.wait_ge(turn_copied, 3 * SG)
                if k >= 4:
                    pe.wait_ge(wcopied, k - 3)
                for g in range(k // 3 * 4, min(k // 3 * 4 + 4, WG)):
                    mm = pe.transpose(PS[k % 4][:, g % 4 * P:(g % 4 + 1) * P], (LOF, CODEF, WR)[k % 3][:, g * P:(g + 1) * P], ident[:, :])
                mm.then_inc(wturned, 1)
            pe.wait_ge(over_ready, 1)
            pe.matmul(PS[7][0:1, 0:WG], ones[:, 0:1], over[:, :], start=True, stop=True).then_inc(over_ps, 1)

            pe.wait_ge(flag_out, 16)
            pe.wait_ge(wcopied, WCOPIES)
            pe.sem_inc(group_ps, RING)

            def windows(b, par, i):
                for q in range(GROUPS):
                    pe.wait_ge(hot_ready, b * GROUPS + q + 1)
                    pe.wait_ge(hotw_ready, b * GROUPS + q + 1)
                    pe.wait_ge(group_out, b * GROUPS + q + 1)
                    for j in range(QW):
                        k = q % RING * QW + j
                        pe.matmul(PS[q % 4][:, j * WCOLS:(j + 1) * WCOLS], OA[:, k, :], OR[:, k, 0:WCOLS], start=True, stop=True)
                        mm = pe.matmul(PS[4 + q % 4][:, j * WCOLS:(j + 1) * WCOLS], OA[:, k, :], OR[:, k, WCOLS:2 * WCOLS], start=True, stop=True)
                    mm.then_inc(group_ps, 1)
            block_pairs(pe, windows)
            pe.wait_ge(group_out, BLOCKS * GROUPS + 4)
            overfull = flag_of(ENG.PE, pe)

            def weight_products(base, array):
                def body(b, par, i):
                    pe.wait_ge(wblk_in[par], (i + 1) * 16 + base * 16 * (BLOCKS // 2 + 1 - par))
                    pe.wait_ge(wsum_used, base * BLOCKS + b + 1)
                    for h in range(BLOCKS):
                        mm = pe.matmul(PS[par][:, 0:F], WIN[par][:, h * P:(h + 1) * P], array[:, h, :], start=(h == 0), stop=(h == BLOCKS - 1))
                    mm.then_inc(wsum_ps, 1)
                block_pairs(pe, body)

            def step_sums(at):
                with pe.Fori(0, BODIES) as i:
                    for u in range(U):
                        pe.wait_ge(general_gathered[u % SLOTS], (at * BODIES + i) * 32 + 16 * (u // SLOTS + 1))
                        pe.wait_ge(general_hot, at * STEPS + (i * U + u + 1))
                        pe.matmul(PS[4 + u % 4][:, 0:F], D[u % 4], G[:, u % SLOTS, :], start=True, stop=True).then_inc(general_sum, 1)

            def turn(ready, offset, ps, sb_, array, pair, base=0):
                def body(c, nb, par):
                    pe.wait_ge(ready, c + offset)
                    pe.wait_ge(sb_, base + c)
                    for j in range(nb):
                        mm = pe.transpose(PS[pair + par][:, j * P:(j + 1) * P], array[:, c * CHUNK + j, :], ident[:, :])
                    mm.then_inc(ps, 1)
                chunks_of_pe(body)

            def times(ready, offset, ps, sb_, arrayT, weights, pair, base=0, bias=None):
                def body(c, nb, par):
                    pe.wait_ge(ready, c + offset)
                    pe.wait_ge(sb_, base + c)
                    for j in range(nb):
                        to = PS[pair + par][:, j * P:(j + 1) * P]
                        if bias is not None:
                            pe.matmul(to, ones[0:1, :], bias, start=True, stop=False)
                        mm = pe.matmul(to, arrayT[:, bass.ds((c * CHUNK + j) * P, P)], weights, start=bias is None, stop=True)
                    mm.then_inc(ps, 1)
                chunks_of_pe(body)

            pe.wait_ge(weights_in, 16 * 15)
            pe.sem_inc(wsum_ps, 2)
            pe.wait_ge(h_ready, C1)
            two_ways(pe, overfull, lambda: weight_products(0, H), lambda: step_sums(0))
            turn(h_ready, C1 + 1, hT_ps, hT_sb, H, 0)

            def pq(c, nb, par):
                pe.wait_ge(hT_sb, c + 2)
                pe.wait_ge(p_sb, c)
                pe.wait_ge(q_sb, c)
                for j in range(nb):
                    lhs = HT[:, bass.ds((c * CHUNK + j) * P, P)]
                    pe.matmul(PS[2 + par][:, j * P:(j + 1) * P], lhs, mW1s[:, 0:F], start=True, stop=True)
                    mm = pe.matmul(PS[4 + par][:, j * P:(j + 1) * P], lhs, mW1s[:, F:2 * F], start=True, stop=True)
                mm.then_inc(p_ps, 1)
            chunks_of_pe(pq)
            pe.wait_ge(regs_in, 96)
            pe.wait_ge(q_sb, C1 + 1)

            def pe_step(i, u, b, on):
                if on(LAG_T):
                    v = (u - LAG_T) % U
                    pe.wait_ge(onehot_ready, i * U + (u - LAG_T + 1))
                    pe.transpose(PS[v % 2][:, 0:P], D[v % DSLOTS], ident[:, :]).then_inc(dt_ps, 1)
                if on(LAG_PRE):
                    v = (u - LAG_PRE) % U
                    pe.wait_ge(dt_sb, i * U + (u - LAG_PRE + 1))
                    if on(LAG_PRE + 2):
                        pe.wait_ge(hid_ready, i * U + (u - LAG_PRE - 1 + SLOTS))
                    pe.wait_ge(attr_in[v % SLOTS], i * 64 + 32 * ((u - LAG_PRE) // SLOTS + 1))
                    pe.matmul(PS[2 + v % 2][:, 0:F], DT[:, v % 2, :], T1[:, b[u], :], start=True, stop=False)
                    pe.matmul(PS[2 + v % 2][:, 0:F], A2[:, v % SLOTS, :], mWcs[:, :], start=False, stop=True).then_inc(pre_ps, 1)
                if on(LAG_SUM):
                    v = (u - LAG_SUM) % U
                    pe.wait_ge(relu_done, i * U + (u - LAG_SUM + 1))
                    pe.matmul(PS[4 + v % 4][:, 0:2 * F + 1], D[v % DSLOTS], HE[:, v % SLOTS, :], start=True, stop=True).then_inc(sum_ready, 1)
            pipeline(pe, LAG_SUM, lambda i, n: registers(ENG.PE, blk_row, i, BLOCKS - 1, LAG_PRE, n or LAG_PRE), pe_step)
            turn(s_ready, 1, sT_ps, sT_sb, ACC[:, :, 0:F], 0)
            times(sT_sb, 2, agg_ps, agg_sb, T2, mW2s[:, :], 2)
            turn(agg_sb, 2, aT_ps, aT_sb, ACC[:, :, 0:F], 4)

            def update(c, nb, par):
                pe.wait_ge(aT_sb, c + 2)
                pe.wait_ge(u_sb, c)
                pe.matmul(bank(6, par, nb), uW1s[:, 0, :], cols(HT, c, nb), start=True, stop=False)
                pe.matmul(bank(6, par, nb), uW1s[:, 1, :], cols(T2, c, nb), start=False, stop=True).then_inc(u_ps, 1)
            chunks_of_pe(update)
            times(u_sb, 2, o_ps, o_sb, T2, uW2s[:, :], 0)
            turn(h_ready, 2 * C1 + 1, hT_ps, hT_sb, H, 0, base=C1)
            times(hT_sb, C1 + 2, sup_ps, sup_sb, HT, Wgs[:, :], 2)
            pe.wait_ge(sup_sb, C1 + 1)
            two_ways(pe, overfull, lambda: weight_products(1, T1), lambda: step_sums(1))
            with pe.Fori(0, LAYERS) as l:
                done = lambda v: l * BLOCKS + (v + 1)

                def products(b, par, i):
                    pe.wait_ge(cblk_in[par], (i + 1) * 16 + l * (16 * (BLOCKS // 2 + 1 - par)))
                    if again(b):
                        pe.wait_ge(osum_ready, done(b - 2))
                    for h in range(BLOCKS):
                        mm = pe.matmul(PS[par][:, 0:3 * F], CIN[par][:, h * P:(h + 1) * P], HP[:, h, :, :].rearrange("p k f -> p (k f)"),
                                       start=(h == 0), stop=(h == BLOCKS - 1))
                    mm.then_inc(csum_ps, 1)

                def turn_sum(v, par, _):
                    pe.wait_ge(osum_ready, done(v))
                    if not isinstance(v, int) or v:
                        pe.wait_ge(oT_sb, done(v - 1))
                    pe.transpose(PS[2][:, 0:P], NB_O[par], ident[:, :]).then_inc(oT_ps, 1)

                def times_w1(v, par, _):
                    pe.wait_ge(oT_sb, done(v))
                    if again(v):
                        pe.wait_ge(zn_ready, done(v - 2))
                    pe.matmul(PS[4 + par][:, 0:F], ones[0:1, :], b1r[:, :], start=True, stop=False)
                    pe.matmul(PS[4 + par][:, 0:F], NB_OT[par], lw1[:, :], start=False, stop=True).then_inc(z_ps, 1)

                def turn_z(v, par, _):
                    pe.wait_ge(zn_ready, done(v))
                    if not isinstance(v, int) or v:
                        pe.wait_ge(zT_sb, done(v - 1))
                    pe.transpose(PS[3][:, 0:P], NB_Z[par], ident[:, :]).then_inc(zT_ps, 1)

                def times_w2(v, par, _):
                    pe.wait_ge(zT_sb, done(v))
                    if again(v):
                        pe.wait_ge(y_normed, done(v - 2))
                    pe.matmul(PS[6 + par][:, 0:F], ones[0:1, :], b2r[:, :], start=True, stop=False)
                    pe.matmul(PS[6 + par][:, 0:F], NB_ZT[par], lw2[:, :], start=False, stop=True).then_inc(y_ps, 1)
                nodes = ((1, turn_sum), (2, times_w1), (3, turn_z), (4, times_w2))

                def dense():
                    wait_alone(pe, parts_ready, (l + 1) * C1)
                    staggered(pe, ((0, products),) + nodes)

                def general():
                    step_sums(l + 2)
                    staggered(pe, nodes)
                wait_alone(pe, layer_in, l * 128 + 128)
                two_ways(pe, overfull, dense, general)

        @block.vector
        def _(dve):
            links = [0]

            def link(ins):
                ins.then_inc(link_done, 1)
                links[0] += 1
                dve.wait_ge(link_done, links[0])

            for s in (q_sb, agg_sb, o_sb, sup_sb):
                dve.sem_inc(s, 1)

            def per_block(body):
                with dve.Fori(0, BLOCKS // 7) as i:
                    for j in range(7):
                        body(i * 7 + j)

            def statistics(array, n, wait=None):
                if wait is None:
                    per_block(lambda b: dve.bn_stats(ST[:, b, :], array[:, b, :]).then_inc(stats_done, 1))
                wait_alone(dve, stats_done, n * BLOCKS)
                steps = (lambda: dve.tensor_tensor(MV[:, :, 0], ST[:, :, 1], ST[:, :, 4], ALU.add),
                         lambda: dve.tensor_tensor(MV[:, :, 1], ST[:, :, 1], ST[:, :, 4], ALU.subtract),
                         lambda: dve.tensor_tensor(ST[:, :, 2], ST[:, :, 2], ST[:, :, 5], ALU.add),
                         lambda: dve.scalar_tensor_tensor(MV[:, :, 1], MV[:, :, 1], 0.25, MV[:, :, 1], ALU.mult, ALU.mult),
                         lambda: dve.tensor_scalar(MV[:, :, 0], MV[:, :, 0], 0.5, None, ALU.mult),
                         lambda: dve.scalar_tensor_tensor(MV[:, :, 1], ST[:, :, 2], 1.0 / F, MV[:, :, 1], ALU.mult, ALU.add))
                for k, step in enumerate(steps):
                    step().then_inc(aggr_done, 1)
                    dve.wait_ge(aggr_done, (n - 1) * len(steps) + (k + 1))

            def rstds(n):
                dve.wait_ge(std_ready, n)
                dve.reciprocal(rstd[:, :], rstd[:, :]).then_inc(part_done, 1)
                dve.wait_ge(part_done, n)
                dve.scalar_tensor_tensor(nmr[:, :], MV[:, :, 0], -1.0, rstd[:, :], ALU.mult, ALU.mult).then_inc(norm_ready, 1)

            link(dve.memset(X[:, BLOCKS - 1, :], 0.0))
            dve.sem_inc(acc_ready, 1)
            dve.wait_ge(consts, 5)
            link(dve.tensor_copy(iota[:, :], iotai[:, :]))
            link(dve.tensor_copy(svec[:, :], sveci[:, :]))
            link(dve.tensor_copy(w2[:, :], w2i[:, :]))
            link(dve.memset(dlast[:, :], float(FAR)))
            link(dve.tensor_scalar(thrb[:, :], iota[:, 0:BLOCKS - 1], 1.0, float(P), ALU.add, ALU.mult))
            dve.wait_ge(dlast_in, 32)
            full = (TILES - 1) // P
            dve.tensor_copy(dlast[:, 0:full], dlasti[:, 0:full])
            link(dve.tensor_copy(dlast[0:TILES - 1 - full * P, full:full + 1], dlasti[0:TILES - 1 - full * P, full:full + 1]))
            dve.sem_inc(dlast_ready, 1)
            for g in range(SG):
                dve.tensor_scalar(cmp[:, g, :], thrb[:, :], dlast[:, g:g + 1], None, ALU.is_gt).then_inc(cmp_ready, 1)
            dve.wait_ge(tau_ready, 1)
            link(dve.scalar_tensor_tensor(thr[:, :], iota[:, 0:BLOCKS - 1], 1.0, PS[7][:, 0:BLOCKS - 1], ALU.add, ALU.add))
            for g in range(SG):
                last = dve.tensor_scalar(cmp[:, g, :], thr[:, :], svec[:, g:g + 1], None, ALU.is_le, ALU.add, accum_out=bs[:, g:g + 1])
            link(last)
            link(dve.tensor_tensor(ts[:, :], svec[:, :], bs[:, :], ALU.subtract))
            dve.tensor_scalar(es[:, :], ts[:, :], float(P), float(EDGES - P), ALU.mult, ALU.min)
            link(dve.tensor_scalar(b128[:, :], ts[:, :], float(TILES - 1), float(SPECIAL - TILES + 1), ALU.is_equal, ALU.mult))
            link(dve.tensor_tensor(b128[:, :], b128[:, :], ts[:, :], ALU.add))
            link(dve.tensor_copy(tsi[:, :], b128[:, :]))
            dve.tensor_scalar(b128[:, :], bs[:, :], float(P), None, ALU.mult)
            link(dve.tensor_copy(bsi[:, :], bs[:, :]))
            dve.tensor_copy(esi[:, :], es[:, :]).then_inc(steps_ready, 1)
            dve.wait_ge(x_in, 32)
            statistics(X, 1)
            rstds(1)
            dve.wait_ge(rows_gathered, 16 * 3 * SG)
            for g in range(SG):
                dve.tensor_copy(SRCF[:, g, :], RS[:, g, :]).then_inc(rel_ready, 1)
                dve.tensor_scalar(RELF[:, g, :], RD[:, g, :], b128[:, g:g + 1], None, ALU.subtract).then_inc(rel_ready, 1)
            dve.wait_ge(turn_copied, 3 * SG)
            dve.wait_ge(regs_in, 96)

            dve.wait_ge(dlb_in, 16)
            for g in range(WG):
                link(dve.tensor_scalar(TJ, DLB, w2[:, g:g + 1], None, ALU.is_lt, ALU.add, accum_out=tw[:, g:g + 1]))
            dve.tensor_copy(twi[:, :], tw[:, :]).then_inc(tw_ready, 1)
            dve.wait_ge(td_in, 16 * WG)
            link(dve.tensor_copy(TDF, TD))
            for g in range(WG):
                last = dve.tensor_scalar(TDF[:, g * P:(g + 1) * P], TDF[:, g * P:(g + 1) * P], w2[:, g:g + 1], None, ALU.is_lt, ALU.add, accum_out=over[:, g:g + 1])
            link(last)
            link(dve.scalar_tensor_tensor(tw[:, :], tw[:, :], float(P), over[:, :], ALU.mult, ALU.add))
            dve.tensor_copy(wstart[:, :], tw[:, :]).then_inc(wstart_ready, 1)
            dve.wait_ge(wrows_in, 16 * 3 * WG)
            link(dve.tensor_scalar(CODEF.bitcast(I32), SR, P - 1, None, ALU.bitwise_and))
            link(dve.tensor_copy(LOF, CODEF.bitcast(I32)))
            link(dve.tensor_scalar(SR, SR, 7, 1, ALU.logical_shift_right, ALU.logical_shift_left))
            DR3 = DR.rearrange("p (g c) -> p g c", c=RUN)
            for g in range(WG):
                dve.tensor_scalar(over[:, g:g + 1], DR3[:, g, P:RUN], w2[:, g:g + 1], float(WN), ALU.subtract, ALU.is_lt)
                last = dve.tensor_scalar(CODEF[:, g * P:(g + 1) * P], DR3[:, g, 0:P], w2[:, g:g + 1], None, ALU.subtract)
            link(last)
            dve.sem_inc(over_ready, 1)
            FARR = DR[:, 0:WG * P].bitcast(FP32)
            link(dve.tensor_scalar(FARR, CODEF, float(WN), 4096.0, ALU.is_ge, ALU.mult))
            link(dve.tensor_tensor(CODEF, CODEF, FARR, ALU.add))
            link(dve.tensor_copy(FARR, SR))
            link(dve.tensor_tensor(CODEF, CODEF, FARR, ALU.add))
            dve.sem_inc(wcode_ready, 3)
            dve.wait_ge(over_ps, 1)
            link(dve.tensor_reduce(tw[0:1, 0:1], PS[7][0:1, 0:WG], op=ALU.add, axis=mybir.AxisListType.X))
            dve.tensor_copy(flag[:, :], tw[0:1, 0:1]).then_inc(flag_ready, 1)
            dve.wait_ge(wcopied, WCOPIES)

            def onehots(b, par, i):
                for q in range(GROUPS):
                    dve.wait_ge(group_ps, b * GROUPS + q + 1)
                    for j in range(QW):
                        k, w = q % RING * QW + j, bass.ds(b * WPB + q * QW + j, 1)
                        dve.tensor_scalar(OA[:, k, :], iota[:, :], LO[:, w], None, ALU.is_equal)
                        last = dve.tensor_scalar(OR[:, k, 0:WCOLS], iota[:, 0:WCOLS], CODE[:, w], None, ALU.is_equal)
                    last.then_inc(hot_ready, 1)
            block_pairs(dve, onehots)
            dve.wait_ge(group_ps, BLOCKS * GROUPS + RING)
            overfull = flag_of(ENG.DVE, dve)

            def weight_sums(base, array):
                def body(b, par, i):
                    dve.wait_ge(wsum_ps, base * BLOCKS + b + 3)
                    dve.tensor_tensor(array[:, b, :], array[:, b, :], PS[par][:, 0:F], ALU.add).then_inc(wsum_used, 1)
                block_pairs(dve, body)
                dve.wait_ge(wsum_used, (base + 1) * BLOCKS + 2)

            def rest_parts(l):
                def rest1(c, nb, par):
                    dve.wait_ge(part1, l * C1 + c + 1)
                    dve.tensor_tensor(ACC[:, bass.ds(c * CHUNK, nb), 0:F], blk(H, c, nb), HP[:, bass.ds(c * CHUNK, nb), 0, :], ALU.subtract).then_inc(part2, 1)

                def rest2(c, nb, par):
                    dve.wait_ge(part3, l * C1 + c + 1)
                    dve.tensor_tensor(HP[:, bass.ds(c * CHUNK, nb), 2, :], ACC[:, bass.ds(c * CHUNK, nb), 0:F], HP[:, bass.ds(c * CHUNK, nb), 1, :],
                                      ALU.subtract).then_inc(parts_ready, 1)
                chunks(dve, rest1)
                chunks(dve, rest2)

            def onehot(i, u, weighted, slots=4, signal=general_hot):
                col = bass.ds(i * U + u, 1)
                return dve.tensor_scalar(D[u % slots], iota[:, :], REL[:, col], WT[:, col] if weighted else None,
                                         ALU.is_equal, ALU.mult if weighted else ALU.bypass).then_inc(signal, 1)

            def accumulate(i, u, at, to, width, sums, slots):
                dve.wait_ge(sums, at * STEPS + (i * U + u + 1))
                dve.wait_ge(slots, at * STEPS + (i * U + u + SLOTS))
                dve.tensor_tensor(to, to, PS[4 + u % 4][:, 0:width], ALU.add).then_inc(slots, 1)

            def pass_sums(at, array, weighted):
                with dve.Fori(0, BODIES) as i:
                    b = registers(ENG.DVE, blk_row, i, BLOCKS - 1)
                    for u in range(U + 2):
                        if u < U:
                            onehot(i, u, weighted)
                        if u >= 2:
                            accumulate(i, u - 2, at, array[:, b[u - 2], :], F, general_sum, general_slots)
                wait_alone(dve, general_slots, (at + 1) * STEPS + SLOTS)

            dve.wait_ge(h_ready, C1)
            two_ways(dve, overfull, lambda: weight_sums(0, X), lambda: pass_sums(0, X, True))
            statistics(X, 2)
            rstds(2)

            def q_out(c, nb, par):
                dve.wait_ge(p_ps, c + 1)
                for j in range(nb):
                    last = dve.tensor_tensor(T1[:, c * CHUNK + j, :], PS[4 + par][:, j * P:(j + 1) * P], bc["mb1"][:, :], ALU.add)
                last.then_inc(q_sb, 1)
            chunks(dve, q_out)
            dve.wait_ge(table_out, 32)
            dve.memset(HE[:, :, ONE:ONE + 1], 1.0)
            link(dve.memset(ACC[:, :, :], 0.0))
            dve.sem_inc(acc_ready, 1)

            def dve_step(i, u, b, on):
                if on(0):
                    onehot(i, u, False, DSLOTS, onehot_ready)
                if on(LAG_PRE):
                    v = (u - LAG_PRE) % U
                    dve.wait_ge(pre_ps, i * U + (u - LAG_PRE + 1))
                    dve.wait_ge(gathered[v % SLOTS], i * 32 + 16 * ((u - LAG_PRE) // SLOTS + 1))
                    dve.tensor_tensor(HE[:, v % SLOTS, 0:F], PS[2 + v % 2][:, 0:F], G[:, v % SLOTS, :], ALU.add).then_inc(hid_ready, 1)
                if on(LAG_SUM):
                    accumulate(i, u - LAG_SUM, 0, ACC[:, b[u], :], 2 * F + 1, sum_ready, slots_free)
            pipeline(dve, LAG_SUM, lambda i, n: registers(ENG.DVE, blk_row, i, BLOCKS - 1, LAG_SUM, n or LAG_SUM), dve_step)
            dve.wait_ge(slots_free, STEPS + SLOTS)
            link(dve.tensor_scalar(rcnt[:, :], ACC[:, :, ONE], 1.0, None, ALU.max))
            link(dve.reciprocal(rcnt[:, :], rcnt[:, :]))
            link(dve.tensor_tensor(cn[:, :], ACC[:, :, ONE], rcnt[:, :], ALU.mult))

            def mean_hidden(c, nb, par):
                for j in range(nb):
                    b = c * CHUNK + j
                    last = dve.tensor_scalar(ACC[:, b, 0:F], ACC[:, b, 0:F], rcnt[:, bass.ds(b, 1)], None, ALU.mult)
                last.then_inc(s_ready, 1)
            chunks(dve, mean_hidden)

            def agg_out(c, nb, par):
                dve.wait_ge(agg_ps, c + 1)
                for j in range(nb):
                    b = c * CHUNK + j
                    last = dve.scalar_tensor_tensor(ACC[:, b, 0:F], bc["mb2"][:, :], cn[:, bass.ds(b, 1)], PS[2 + par][:, j * P:(j + 1) * P], ALU.mult, ALU.add)
                last.then_inc(agg_sb, 1)
            chunks(dve, agg_out)
            wide = lambda n, nb: bc[n][:, :].rearrange("p (a f) -> p a f", a=1).broadcast_to([P, nb, F])

            def residual(c, nb, par):
                dve.tensor_tensor(blk(H, c, nb), blk(H, c, nb), wide("ub2", nb), ALU.add).then_inc(s_ready, 1)
            chunks(dve, residual)
            dve.wait_ge(s_ready, 2 * C1)

            def upd_out(c, nb, par):
                dve.wait_ge(o_ps, c + 1)
                dve.tensor_tensor(blk(T1, c, nb), bank3(0, par, nb), blk(H, c, nb), ALU.add).then_inc(o_sb, 1)
            chunks(dve, upd_out)
            dve.wait_ge(o_sb, C1 + 1)
            statistics(T1, 3)
            rstds(3)

            def normed(n, to, signal, base):
                wait_alone(dve, norm_ready, n)

                def body(c, nb, par):
                    for j in range(nb):
                        b = c * CHUNK + j
                        last = dve.tensor_scalar(to[:, b, :], to[:, b, :], MV[:, b, 0:1], rstd[:, bass.ds(b, 1)], ALU.subtract, ALU.mult)
                    last.then_inc(signal, 1)
                chunks(dve, body)

            def times_plus(array, scale, shift, plus, signal_a, a0, signal_b):
                def one(c, nb, par):
                    dve.tensor_tensor(blk(array, c, nb), blk(array, c, nb), wide(scale, nb), ALU.mult).then_inc(signal_a, 1)

                def two(c, nb, par):
                    dve.wait_ge(signal_a, a0 + c + 1)
                    dve.tensor_tensor(blk(array, c, nb), blk(array, c, nb), wide(shift, nb) if plus is None else blk(plus, c, nb),
                                      ALU.add).then_inc(signal_b, 1)
                chunks(dve, one)
                chunks(dve, two)

            normed(3, T1, s_ready, 0)
            dve.wait_ge(s_ready, 3 * C1)
            times_plus(T1, "gamma", "beta", None, s_ready, 3 * C1, o_sb)

            def add_to_x(c, nb, par):
                dve.wait_ge(o_sb, c + C1 + 2)
                dve.tensor_tensor(blk(X, c, nb), blk(X, c, nb), blk(T1, c, nb), ALU.add).then_inc(s_ready, 1)
            chunks(dve, add_to_x)
            dve.wait_ge(s_ready, 5 * C1)
            statistics(X, 4)
            rstds(4)

            def support_out(c, nb, par):
                dve.wait_ge(sup_ps, c + 1)
                dve.tensor_copy(blk(T1, c, nb), bank3(2, par, nb)).then_inc(sup_sb, 1)
            chunks(dve, support_out)

            def bias_init(c, nb, par):
                dve.tensor_copy(blk(H, c, nb), wide("bias2g", nb)).then_inc(s_ready, 1)
            dve.wait_ge(hT_sb, 2 * C1 + 1)
            chunks(dve, bias_init)
            dve.wait_ge(s_ready, 6 * C1)
            two_ways(dve, overfull, lambda: weight_sums(1, H), lambda: pass_sums(1, H, True))

            def relu_to_x(c, nb, par):
                dve.scalar_tensor_tensor(blk(X, c, nb), blk(H, c, nb), 0.0, blk(X, c, nb), ALU.max, ALU.add).then_inc(s_ready, 1)
            chunks(dve, relu_to_x)
            dve.wait_ge(s_ready, 7 * C1)
            statistics(X, 5)
            rstds(5)
            dve.wait_ge(h_ready, 4 * C1)
            with dve.Fori(0, LAYERS) as l:
                done = lambda v: l * BLOCKS + (v + 1)
                wait_alone(dve, gelu_done, l * BLOCKS)
                wait_alone(dve, layer_in, l * 128 + 128)

                def out_sum(v, par, _):
                    if again(v):
                        dve.wait_ge(oT_ps, done(v - 2))
                    dve.tensor_tensor(NB_O[par], H[:, v, :], ACC[:, v, F:2 * F], ALU.add).then_inc(csum_part, 1)
                    dve.wait_ge(csum_ps, done(v))
                    for n, k in enumerate((2, 1, 0)):
                        dve.wait_ge(csum_part, (l * BLOCKS + v) * 3 + (n + 1))
                        dve.tensor_tensor(NB_O[par], NB_O[par], PS[par][:, k * F:(k + 1) * F], ALU.add).then_inc(osum_ready if k == 0 else csum_part, 1)

                def general_out_sum(v, par, _):
                    if again(v):
                        dve.wait_ge(oT_ps, done(v - 2))
                    dve.tensor_copy(NB_O[par], T1[:, v, :]).then_inc(osum_ready, 1)

                def stats_z(v, par, _):
                    dve.wait_ge(z_ps, done(v))
                    dve.bn_stats(ST[:, par, :], PS[4 + par][:, 0:F]).then_inc(z_stats, 1)
                    wait_alone(dve, z_stats, done(v))
                    dve.bn_aggr(MV[:, par, :], ST[:, par, :]).then_inc(z_aggr, 1)

                def stats_y(v, par, _):
                    dve.wait_ge(y_ps, done(v))
                    dve.bn_stats(ST[:, 2 + par, :], PS[6 + par][:, 0:F]).then_inc(y_stats, 1)
                    wait_alone(dve, y_stats, done(v))
                    dve.bn_aggr(MV[:, 2 + par, :], ST[:, 2 + par, :]).then_inc(y_aggr, 1)

                def shift_h(v, par, _):
                    if again(v):
                        dve.wait_ge(yn_ready, done(v - 2))
                    dve.tensor_tensor(NB_S[par], H[:, v, :], bc["be2"][:, :], ALU.add).then_inc(h_shifted, 1)

                def norm_z(v, par, _):
                    dve.wait_ge(z_std, done(v))
                    dve.reciprocal(rstd[:, par:par + 1], rstd[:, par:par + 1]).then_inc(z_rstd, 1)
                    dve.wait_ge(z_rstd, done(v))
                    if again(v):
                        dve.wait_ge(zT_ps, done(v - 2))
                    dve.tensor_scalar(NB_Z[par], PS[4 + par][:, 0:F], MV[:, par, 0:1], rstd[:, par:par + 1], ALU.subtract, ALU.mult).then_inc(zn_ready, 1)

                def norm_y(v, par, _):
                    dve.wait_ge(y_std, done(v))
                    dve.reciprocal(rstd[:, 2 + par:3 + par], rstd[:, 2 + par:3 + par]).then_inc(y_rstd, 1)
                    dve.wait_ge(y_rstd, done(v))
                    if again(v):
                        dve.wait_ge(gelu_done, done(v - 2))
                    dve.tensor_scalar(NB_Y[par], PS[6 + par][:, 0:F], MV[:, 2 + par, 0:1], rstd[:, 2 + par:3 + par], ALU.subtract, ALU.mult).then_inc(y_normed, 1)
                    dve.wait_ge(y_normed, done(v))
                    dve.tensor_tensor(NB_Y[par], NB_Y[par], bc["g2"][:, :], ALU.mult).then_inc(y_scaled, 1)
                    dve.wait_ge(y_scaled, done(v))
                    dve.wait_ge(h_shifted, done(v))
                    dve.tensor_tensor(NB_Y[par], NB_Y[par], NB_S[par], ALU.add).then_inc(yn_ready, 1)
                nodes = ((2, stats_z), (4, stats_y), (4, shift_h), (2, norm_z), (4, norm_y))

                def dense():
                    rest_parts(l)
                    wait_alone(dve, parts_ready, (l + 1) * C1)
                    staggered(dve, ((0, out_sum),) + nodes)

                def general():
                    def out_init(c, nb, par):
                        dve.tensor_tensor(blk(T1, c, nb), blk(H, c, nb), ACC[:, bass.ds(c * CHUNK, nb), F:2 * F], ALU.add).then_inc(agg_sb, 1)
                    chunks(dve, out_init)
                    wait_alone(dve, agg_sb, (l + 2) * C1 + 1)
                    pass_sums(l + 2, T1, False)
                    staggered(dve, ((0, general_out_sum),) + nodes)
                two_ways(dve, overfull, dense, general)
                dve.sem_inc(layer_used, 1)
            dve.wait_ge(gelu_done, LAYERS * BLOCKS)

            def final(c, nb, par):
                dve.tensor_tensor(blk(X, c, nb), blk(X, c, nb), blk(H, c, nb), ALU.add).then_inc(s_ready, 1)
            chunks(dve, final)
            dve.wait_ge(s_ready, 8 * C1)
            dve.sem_inc(out_ready, 1)


_INS = ["x", "src", "dst", "edge_weight", "edge_attr_128", "edge_attr_2", "L1_gnn_mW1", "L1_gnn_mb1", "L1_gnn_mW2", "L1_gnn_mb2",
        "L1_gnn_uW1", "L1_gnn_ub1", "L1_gnn_uW2", "L1_gnn_ub2", "L1_gnn_gamma", "L1_gnn_beta", "L2_gnn_weight", "L2_gnn_bias",
        "L3_gnn_W1", "L3_gnn_b1", "L3_gnn_g1", "L3_gnn_be1", "L3_gnn_W2", "L3_gnn_b2", "L3_gnn_g2", "L3_gnn_be2"]


def kernel(**inputs):
    import numpy as np
    import concourse.bacc as bacc
    from concourse.bass_utils import run_bass_kernel_spmd

    nc = bacc.Bacc("TRN2", target_bir_lowering=False, num_devices=1)
    layout = {"edge_attr_2": lambda a: a.T,
              "L3_gnn_W1": lambda a: a.transpose(0, 2, 1).reshape(LAYERS * F, F),
              "L3_gnn_W2": lambda a: a.transpose(0, 2, 1).reshape(LAYERS * F, F),
              "L3_gnn_g1": lambda a: a.reshape(LAYERS * F, 1),
              "L3_gnn_be1": lambda a: a.reshape(LAYERS * F, 1)}
    arrays, args = {}, []
    for name in _INS:
        a = np.asarray(inputs[name])
        a = np.ascontiguousarray(layout[name](a) if name in layout else a)
        arrays[f"in_{name}"] = a
        args.append(nc.dram_tensor(f"in_{name}", a.shape, mybir.dt.from_np(a.dtype), kind="ExternalInput").ap())
    out = nc.dram_tensor("out", (NODES, F), FP32, kind="ExternalOutput").ap()
    build_gnn(nc, *args, out)
    r = run_bass_kernel_spmd(nc, [arrays], core_ids=[0])
    return r.results[0]["out"]
```
